# Optimizing a Trainium2 kernel written in Bass

```python
import numpy as np
import os as _os
import jax
import jax.numpy as jnp

def _softmax(x, axis=-1):
    return jax.nn.softmax(x, axis=axis)

def _gelu(x):
    return jax.nn.gelu(x, approximate=True)

def _silu(x):
    return jax.nn.silu(x)

def _sigmoid(x):
    return jax.nn.sigmoid(x)

def _layernorm(x, axis=-1, eps=1e-05):
    m = jnp.mean(x, axis=axis, keepdims=True)
    v = jnp.var(x, axis=axis, keepdims=True)
    return (x - m) / jnp.sqrt(v + eps)

def _scatter_add(tgt, idx, src, axis=0):
    return tgt.at[idx].add(src)

def _segment_sum(src, seg, n):
    return jax.ops.segment_sum(src, seg, n)
kernel_name = 'mk_seq_postln_d2_jaxref_r4_1f0b2b'

def setup_inputs(seed: int=0):
    np.random.seed(seed)
    _w = jnp.asarray

    def _L0_attn_setup():
        import jax, jax.numpy as jnp
        import numpy as np
        D_MODEL = 256
        NUM_HEADS = 16
        HEAD_DIM = D_MODEL // NUM_HEADS
        DILATION = 2
        SEGMENT = 256
        OFFSET = 0
        key = jax.random.key(seed)
        x = jax.random.normal(key, (4, 2048, D_MODEL), dtype=jnp.float32)
        return {'x': x}
    _L0_attn_in = _L0_attn_setup()

    def _L0_ffn_setup():
        import jax, jax.numpy as jnp
        import numpy as np
        B, S, DIM, FFN, E = (4, 512, 256, 1024, 8)
        key = jax.random.key(seed)
        k0, k1, k2, k3 = jax.random.split(key, 4)
        scale = 0.02
        return {'hidden_states': jax.random.normal(k0, (B, S, DIM), jnp.float32), 'router_w': jax.random.normal(k1, (DIM, E), jnp.float32) * scale, 'router_b': jnp.zeros((E,), jnp.float32), 'w1': jax.random.normal(k2, (E, DIM, 2 * FFN), jnp.float32) * scale, 'w2': jax.random.normal(k3, (E, FFN, DIM), jnp.float32) * scale}
    _L0_ffn_in = _L0_ffn_setup()

    def _L1_attn_setup():
        import jax, jax.numpy as jnp
        import numpy as np
        EPS = 1e-06
        key = jax.random.key(seed)
        kx, kw = jax.random.split(key)
        B, L, D = (4, 2048, 256)
        x = jax.random.normal(kx, (B, L, D), dtype=jnp.float32)
        W = jax.random.normal(kw, (D, 3 * D), dtype=jnp.float32) * 0.02
        return {'x': x, 'W': W}
    _L1_attn_in = _L1_attn_setup()

    def _L1_ffn_setup():
        import jax, jax.numpy as jnp
        import numpy as np
        B, M, D = (4, 512, 256)
        N, P = (64, 32)
        key = jax.random.key(seed)
        k1, k2, k3, k4 = jax.random.split(key, 4)
        x = jax.random.normal(k1, (B, M, D), dtype=jnp.float32)
        phi = jax.random.normal(k2, (D, N, P), dtype=jnp.float32) * (1.0 / np.sqrt(D))
        W = jax.random.normal(k3, (N, D, D), dtype=jnp.float32) * (1.0 / np.sqrt(D))
        b = jax.random.normal(k4, (N, D), dtype=jnp.float32) * 0.01
        return {'x': x, 'phi': phi, 'W': W, 'b': b}
    _L1_ffn_in = _L1_ffn_setup()
    _d = {'L0_attn_x': _L0_attn_in['x'], 'L0_ffn_router_w': _L0_ffn_in['router_w'], 'L0_ffn_router_b': _L0_ffn_in['router_b'], 'L0_ffn_w1': _L0_ffn_in['w1'], 'L0_ffn_w2': _L0_ffn_in['w2'], 'L1_attn_W': _L1_attn_in['W'], 'L1_ffn_phi': _L1_ffn_in['phi'], 'L1_ffn_W': _L1_ffn_in['W'], 'L1_ffn_b': _L1_ffn_in['b']}
    _x0 = _d['L0_attn_x']
    _d['L0_attn_x'] = jax.random.normal(jax.random.fold_in(jax.random.key(seed), 1), (4, 1024, 256), dtype=_x0.dtype)
    del _x0
    return _d

def reference(L0_attn_x, L0_ffn_router_w, L0_ffn_router_b, L0_ffn_w1, L0_ffn_w2, L1_attn_W, L1_ffn_phi, L1_ffn_W, L1_ffn_b):

    def _L0_attn_ref(x):
        import jax, jax.numpy as jnp
        import numpy as np
        D_MODEL = 256
        NUM_HEADS = 16
        HEAD_DIM = D_MODEL // NUM_HEADS
        DILATION = 2
        SEGMENT = 256
        OFFSET = 0
        b, n, d = x.shape
        n_seg = n // SEGMENT
        k = SEGMENT // DILATION
        local_idx = OFFSET + DILATION * jnp.arange(k)
        global_idx = SEGMENT * jnp.arange(n_seg)[:, None] + local_idx[None, :]
        xs = x[:, global_idx, :]
        qh = xs.reshape(b, n_seg, k, NUM_HEADS, HEAD_DIM)
        scale = 1.0 / jnp.sqrt(jnp.asarray(HEAD_DIM, dtype=xs.dtype))
        scores = jnp.einsum('bsqhd,bskhd->bshqk', qh, qh) * scale
        attn = jax.nn.softmax(scores, axis=-1)
        seg_out = jnp.einsum('bshqk,bskhd->bsqhd', attn, qh)
        a_os = seg_out.reshape(b, n_seg * k, d)
        idx = jnp.broadcast_to(global_idx.reshape(-1), (b, n_seg * k))
        a_denoms = a_os.sum(axis=-1)

        def mix(o_b, den_b, idx_b):
            sums = jnp.zeros((n,), o_b.dtype).at[idx_b].add(den_b)
            alphas = den_b / sums[idx_b]
            return jnp.zeros((n, d), o_b.dtype).at[idx_b].add(o_b * alphas[:, None])
        return jax.vmap(mix)(a_os, a_denoms, idx)

    def _L0_ffn_ref(hidden_states, router_w, router_b, w1, w2):
        import jax, jax.numpy as jnp
        import numpy as np
        B, S, DIM, FFN, E = (4, 512, 256, 1024, 8)
        b, s, d = hidden_states.shape
        x = hidden_states.reshape(-1, d)
        logits = x @ router_w + router_b
        route = jax.nn.softmax(logits, axis=1)
        max_prob = jnp.max(route, axis=1, keepdims=True)
        max_ind = jnp.argmax(route, axis=1)
        out = jnp.zeros_like(x)
        num_experts = w1.shape[0]
        for e in range(num_experts):
            h = x @ w1[e]
            a, g = jnp.split(h, 2, axis=1)
            y = jax.nn.silu(a) * g @ w2[e]
            out = jnp.where((max_ind == e)[:, None], y, out)
        out = out * max_prob
        return out.reshape(b, s, d)

    def _L1_attn_ref(x, W):
        import jax, jax.numpy as jnp
        import numpy as np
        EPS = 1e-06
        D = x.shape[-1]
        qkv = x @ W
        q, k, v = jnp.split(qkv, 3, axis=-1)
        q = jax.nn.elu(q) + 1.0
        k = jax.nn.elu(k) + 1.0
        KV = jnp.einsum('bld,blh->bhd', k, v)
        k_sum = k.sum(axis=1)
        Z = 1.0 / (jnp.einsum('bld,bd->bl', q, k_sum) + EPS)
        V = jnp.einsum('bld,bhd,bl->blh', q, KV, Z)
        return V

    def _L1_ffn_ref(x, phi, W, b):
        import jax, jax.numpy as jnp
        import numpy as np
        B, M, D = (4, 512, 256)
        N, P = (64, 32)
        logits = jnp.einsum('bmd,dnp->bmnp', x, phi)
        dispatch = jax.nn.softmax(logits, axis=0)
        bsz, m, n, p = logits.shape
        combine = jax.nn.softmax(logits.reshape(bsz, m, n * p), axis=-1).reshape(bsz, m, n, p)
        slots = jnp.einsum('bmd,bmnp->bnpd', x, dispatch)
        y = jnp.einsum('bnpd,nde->bnpe', slots, W) + b[None, :, None, :]
        out = jnp.einsum('bnpd,bmnp->bmd', y, combine)
        return out
    x = L0_attn_x
    x = _layernorm(x + _L0_attn_ref(x), axis=-1)
    x = _layernorm(x + _L0_ffn_ref(x, L0_ffn_router_w, L0_ffn_router_b, L0_ffn_w1, L0_ffn_w2), axis=-1)
    x = _layernorm(x + _L1_attn_ref(x, L1_attn_W), axis=-1)
    x = _layernorm(x + _L1_ffn_ref(x, L1_ffn_phi, L1_ffn_W, L1_ffn_b), axis=-1)
    return x

_drawn_inputs = setup_inputs


def setup_inputs(seed=0):
    import zlib

    import numpy as np

    out = dict(_drawn_inputs(seed))
    spreads = {'L0_ffn_router_b': (0.0, 0.8)}
    factors = {'L0_ffn_router_w': 8.0, 'L0_ffn_w1': 7.904, 'L0_ffn_w2': 8.0, 'L1_ffn_b': 64.0}
    for name, (base, spread) in spreads.items():
        noise = np.random.default_rng([zlib.crc32(name.encode()), seed]).standard_normal(out[name].shape)
        drawn = base * np.exp(spread * noise) if base else spread * noise
        out[name] = jnp.asarray(drawn.astype(out[name].dtype))
    for name, factor in factors.items():
        out[name] = (out[name] * factor).astype(out[name].dtype)
    return out
```

```python
from contextlib import ExitStack

import concourse.bass as bass
from concourse import mybir

ALU = mybir.AluOpType
ACT = mybir.ActivationFunctionType
X = mybir.AxisListType.X
F32 = mybir.dt.float32
F32R = mybir.dt.float32r
BF16 = mybir.dt.bfloat16
I32 = mybir.dt.int32

P = 128
B, S, D = 4, 1024, 256
KD = D // P
SEG = 256
NSEG = B * S // SEG
NT = B * S // P
TB = NT // B
NH, HD = 16, 16
UH = 4
UPS = NH // UH
HG = P // HD // UH
NE, FF = 8, 1024
SLOTS = NT + NE - 1
LN_EPS = 1e-5


def wait(eng, sem, count):
    if not isinstance(count, int) or count > 0:
        eng.wait_ge(sem, count)


def stages(step, lag, period, fresh, draining):
    k = step - lag
    if k < 0:
        return None if fresh else k
    return None if draining else k


def norm_steps(v, link, stats, mean, rstd, var, tmp, magic):
    link(v.tensor_tensor(mean, stats[:, :, 1], stats[:, :, 4], ALU.add))
    link(v.tensor_scalar(mean, mean, 0.5, None, ALU.mult))
    link(v.tensor_tensor(var, stats[:, :, 1], stats[:, :, 4], ALU.subtract))
    link(v.tensor_tensor(var, var, var, ALU.mult))
    link(v.tensor_tensor(tmp, stats[:, :, 2], stats[:, :, 5], ALU.add))
    link(v.tensor_scalar(tmp, tmp, 1.0 / D, LN_EPS, ALU.mult, ALU.add))
    link(v.scalar_tensor_tensor(var, var, 0.25, tmp, ALU.mult, ALU.add))
    link(v.tensor_scalar(magic, var.bitcast(I32), 1, None, ALU.logical_shift_right))
    link(v.tensor_scalar(rstd.bitcast(I32), magic, -1.0, 1597463007.0, ALU.mult, ALU.add))
    for _ in range(3):
        link(v.tensor_tensor(tmp, rstd, rstd, ALU.mult))
        link(v.tensor_tensor(tmp, tmp, var, ALU.mult))
        link(v.tensor_scalar(tmp, tmp, -0.5, 1.5, ALU.mult, ALU.add))
        link(v.tensor_tensor(rstd, rstd, tmp, ALU.mult))


NORM_LINKS = 21


class Scope:

    def __init__(self, nc, ctx, tag):
        self.nc, self.ctx, self.tag = nc, ctx, tag

    def sb(self, name, shape, dt=F32):
        return self.ctx.enter_context(self.nc.sbuf_tensor(f"{self.tag}_{name}", shape, dt))

    def ps(self, name, shape, dt=F32):
        return self.ctx.enter_context(self.nc.psum_tensor(f"{self.tag}_{name}", shape, dt))

    def sem(self, name):
        return self.ctx.enter_context(self.nc.semaphore(f"{self.tag}_{name}"))


def constants(nc, ctx, held, c):
    c["ident"] = Scope(nc, ctx, "const").sb("ident", [P, P])
    m = Scope(nc, held, "const")
    c["headmask"] = m.sb("headmask", [P, HG * UH])
    c["rowmask"] = m.sb("rowmask", [2 * UH, UH])
    c["ones8"] = m.sb("ones8", [2 * UH, P], F32R)
    c["eidx"] = m.sb("eidx", [P, NE])
    c["tri"] = m.sb("tri", [P, P])
    c["ones"] = m.sb("ones", [P, P])
    c["iota_r"] = m.sb("iota_r", [P, P])
    c["iota_s"] = m.sb("iota_s", [P, SLOTS + 1])
    c["iota_t"] = m.sb("iota_t", [P, NT])
    c["iota_p"] = m.sb("iota_p", [P, 1])
    filled = m.sem("filled")
    with nc.Block() as block:
        @block.gpsimd
        def _(pool):
            g = nc.gpsimd
            n = 0
            for key, value in (("ident", 0.0), ("headmask", 1.0), ("rowmask", 0.0), ("ones8", 1.0),
                               ("ones", 1.0), ("tri", 1.0)):
                g.memset(c[key][:].bitcast(F32), value).then_inc(filled, 1)
                n += 1
            g.iota(c["iota_r"][:], [[1, P]], base=0, channel_multiplier=0, allow_small_or_imprecise_dtypes=True).then_inc(filled, 1)
            g.iota(c["iota_s"][:], [[1, SLOTS + 1]], base=0, channel_multiplier=0, allow_small_or_imprecise_dtypes=True).then_inc(filled, 1)
            g.iota(c["iota_t"][:], [[1, NT]], base=0, channel_multiplier=0, allow_small_or_imprecise_dtypes=True).then_inc(filled, 1)
            g.iota(c["iota_p"][:], [[1, 1]], base=0, channel_multiplier=1, allow_small_or_imprecise_dtypes=True).then_inc(filled, 1)
            g.iota(c["eidx"][:], [[1, NE]], base=-NE, channel_multiplier=0, allow_small_or_imprecise_dtypes=True).then_inc(filled, 1)
            n += 5
            pool.wait_ge(filled, n)
            g.affine_select(out=c["ident"][:], in_=c["ident"][:], compare_op=ALU.not_equal, fill=1.0,
                            base=0, pattern=[[-1, P]], channel_multiplier=1).then_inc(filled, 1)
            g.affine_select(out=c["tri"][:], in_=c["tri"][:], compare_op=ALU.is_gt, fill=0.0,
                            base=0, pattern=[[1, P]], channel_multiplier=-1).then_inc(filled, 1)
            g.affine_select(out=c["headmask"][:], in_=c["headmask"][:], compare_op=ALU.is_ge, fill=0.0,
                            base=0, pattern=[[-HD, HG * UH]], channel_multiplier=1).then_inc(filled, 1)
            g.affine_select(out=c["rowmask"][:], in_=c["rowmask"][:], compare_op=ALU.not_equal, fill=1.0,
                            base=0, pattern=[[-1, UH]], channel_multiplier=1).then_inc(filled, 1)
            pool.wait_ge(filled, n + 4)
            g.affine_select(out=c["headmask"][:], in_=c["headmask"][:], compare_op=ALU.is_ge, fill=0.0,
                            base=HD - 1, pattern=[[HD, HG * UH]], channel_multiplier=-1).then_inc(filled, 1)
            g.affine_select(out=c["rowmask"][:], in_=c["rowmask"][:], compare_op=ALU.not_equal, fill=1.0,
                            base=-UH, pattern=[[-1, UH]], channel_multiplier=1).then_inc(filled, 1)
            pool.wait_ge(filled, n + 6)


def dilated_attention(nc, c, x_dram, x1, stats):
    LS, LM, LA, LO = 2, 3, 4, 5
    OW = UH * (HD + 1)
    ctx = ExitStack()
    m = Scope(nc, ctx, "att")
    with ctx:
        xe = [m.sb(f"xe{i}", [P, D]) for i in range(2)]
        xaug = [m.sb(f"xaug{i}", [P, NH, HD + 1]) for i in range(2)]
        xT = [m.sb(f"xT{i}", [P, KD, P]) for i in range(2)]
        xm = [m.sb(f"xm{i}", [P, UH, P]) for i in range(UPS)]
        prob = [m.sb(f"prob{i}", [P, UH, P]) for i in range(UPS)]
        mx = [m.sb(f"mx{i}", [P, UH]) for i in range(UPS)]
        negmax = [m.sb(f"negmax{i}", [P, 2 * UH], F32R) for i in range(UPS)]
        shift = [m.sb(f"shift{i}", [2 * UH, UH, P], F32R) for i in range(UPS)]
        rden = [m.sb(f"rden{i}", [P, UH]) for i in range(UPS)]
        heads = [m.sb(f"heads{i}", [P, D]) for i in range(2)]
        small = [m.sb(f"small{i}", [P, 4]) for i in range(2)]
        psS = [m.ps(f"psS{i}", [P, UH, P]) for i in range(UPS)]
        psT = m.ps("psT", [P, KD, P])
        psM = m.ps("psM", [2 * UH, P])
        psO = [m.ps(f"psO{i}", [P, 512]) for i in range(2)]
        loaded, aug_ready, xT_raw, xT_ready, xm_ready = (m.sem(s) for s in ("loaded", "aug_ready", "xT_raw", "xT_ready", "xm_ready"))
        scored, max_ready, hi_ready, negmax_ready, max_turned, shift_ready, shifted, prob_ready, out_raw, rden_ready, heads_ready, fin = (
            m.sem(s) for s in ("scored", "max_ready", "hi_ready", "negmax_ready", "max_turned", "shift_ready", "shifted",
                               "prob_ready", "out_raw", "rden_ready", "heads_ready", "fin"))
        ones_set = m.sem("ones_set")
        even_loaded = [m.sem(f"even_loaded{i}") for i in range(2)]
        block = ctx.enter_context(nc.Block())

        @block.sync
        def _(sp):
            src = x_dram.rearrange("b (g p w) d -> p (b g) (w d)", p=P, w=2)
            dst = x1[:].rearrange("p (g w) d -> p g (w d)", w=2)

            def load(i, segs):
                wait(sp, loaded, i * 16)
                sp.dma_start(dst[:, bass.ds(segs[0], 2), :], src[:, bass.ds(segs[0], 2), :]).then_inc(loaded, 16)
                for q in range(2):
                    if not isinstance(i, int):
                        sp.wait_ge(xT_raw, i * 2 + (q - 1))
                    sp.dma_start(xe[q][:], src[:, bass.ds(segs[q], 1), 0:D].rearrange("p a d -> p (a d)")).then_inc(even_loaded[q], 16)

            load(0, (0, 1))
            with sp.Fori(1, NSEG // 2) as i:
                load(i, (sp.snap(i * 2), sp.snap(i * 2 + 1)))

        @block.gpsimd
        def _(pool):
            def masks(i):
                for k in range(2 * UPS):
                    q, g = divmod(k, UPS)
                    half, part = divmod(g, HG)
                    if g == 0:
                        wait(pool, xT_ready, i * 2 + (q + 1))
                    wait(pool, scored, i * 8 + (k - UPS + 1))
                    nc.gpsimd.tensor_tensor(
                        xm[g][:], xT[q][:, half, :].unsqueeze(1).to_broadcast([P, UH, P]),
                        c["headmask"][:, part * UH:(part + 1) * UH].unsqueeze(2).to_broadcast([P, UH, P]),
                        ALU.mult).then_inc(xm_ready, 1)

            masks(0)
            with pool.Fori(1, NSEG // 2) as i:
                masks(i)

        @block.tensor
        def _(pe):
            def step(i, k, fresh=False, draining=False):
                def unit(lag):
                    j = stages(k, lag, 8, fresh, draining)
                    return (None, 0, 0) if j is None else (i * 8 + j, (j % 8) // UPS, j % UPS)

                u, q, g = unit(LS)
                if u is not None:
                    wait(pe, xm_ready, u + 1)
                    wait(pe, prob_ready, u - (UPS - 1))
                    nc.tensor.matmul(psS[g][:].rearrange("p a b -> p (a b)"), xT[q][:, g // HG, :],
                                     xm[g][:].rearrange("p a b -> p (a b)"), start=True, stop=True).then_inc(scored, 1)
                u, q, g = unit(LM)
                if u is not None:
                    wait(pe, negmax_ready, u + 1)
                    wait(pe, shift_ready, u)
                    nc.tensor.transpose(psM[:], negmax[g][:].bitcast(F32), c["ident"][:]).then_inc(max_turned, 1)
                u, q, g = unit(LA)
                if u is not None:
                    wait(pe, shift_ready, u + 1)
                    nc.tensor.matmul(psS[g][:].rearrange("p a b -> p (a b)"), c["ones8"][:],
                                     shift[g][:].rearrange("p a b -> p (a b)"), start=False, stop=True,
                                     skip_group_check=True).then_inc(shifted, 1)
                u, q, g = unit(LO)
                if u is not None:
                    wait(pe, prob_ready, u + 1)
                    if g == 0:
                        wait(pe, aug_ready, i * 2 + (k - LO) // UPS + 1)
                    wait(pe, heads_ready, u - 1)
                    for j in range(UH):
                        last = nc.tensor.matmul(psO[g % 2][:, j * OW:(j + 1) * OW], prob[g][:, j, :],
                                                xaug[q][:, g * UH:(g + 1) * UH, :].rearrange("p h d -> p (h d)"),
                                                start=True, stop=True)
                    last.then_inc(out_raw, 1)
                if k % UPS == 0 and not draining:
                    q = k // UPS
                    seg = i * 2 + q
                    wait(pe, even_loaded[q], i * 16 + 16)
                    wait(pe, xT_ready, seg)
                    for half in range(KD):
                        last = nc.tensor.transpose(psT[:, half, :], xe[q][:, half * P:(half + 1) * P], c["ident"][:])
                    last.then_inc(xT_raw, 1)

            for k in range(8):
                step(0, k, fresh=True)
            with pe.Fori(1, NSEG // 2) as i:
                for k in range(8):
                    step(i, k)
            for k in range(LO):
                step(NSEG // 2, k, draining=True)

        @block.scalar
        def _(act):
            act.wait_ge(ones_set, 2)

            def step(i, k, fresh=False, draining=False):
                j = stages(k, LA, 8, fresh, draining)
                if j is not None:
                    u, g = i * 8 + j, j % UPS
                    wait(act, shifted, u + 1)
                    wait(act, out_raw, u - (UPS - 1))
                    nc.scalar.activation(prob[g][:], psS[g][:], ACT.Exp, scale=HD ** -0.5).then_inc(prob_ready, 1)
                if k % UPS == 0 and not draining:
                    q = k // UPS
                    seg = i * 2 + q
                    act.wait_ge(loaded, i * 16 + 16)
                    wait(act, out_raw, (seg - 1) * UPS)
                    nc.scalar.activation(xaug[q][:, :, 0:HD],
                                         x1[:, bass.ds(seg * 2, 1), :].rearrange("p a (h d) -> p (a h) d", d=HD),
                                         ACT.Copy).then_inc(aug_ready, 1)
                    wait(act, xT_raw, seg + 1)
                    wait(act, scored, (seg - 1) * UPS + 1)
                    nc.scalar.activation(xT[q][:], psT[:], ACT.Copy).then_inc(xT_ready, 1)

            for k in range(8):
                step(0, k, fresh=True)
            with act.Fori(1, NSEG // 2) as i:
                for k in range(8):
                    step(i, k)
            for k in range(LA):
                step(NSEG // 2, k, draining=True)

        @block.vector
        def _(dve):
            for q in range(2):
                nc.vector.memset(xaug[q][:, :, HD:HD + 1], 1.0).then_inc(ones_set, 1)

            def finish(seg, q):
                row = x1[:, bass.ds(seg * 2, 1), :].rearrange("p a d -> p (a d)")
                den, rec, alpha = (small[q][:, n:n + 1] for n in range(3))
                wait(dve, heads_ready, seg * UPS + UPS)
                nc.vector.tensor_reduce(den, heads[q][:], X, ALU.add).then_inc(fin, 1)
                wait(dve, fin, seg * 4 + 1)
                nc.vector.reciprocal(rec, den).then_inc(fin, 1)
                wait(dve, fin, seg * 4 + 2)
                nc.vector.tensor_tensor(alpha, den, rec, ALU.mult).then_inc(fin, 1)
                wait(dve, fin, seg * 4 + 3)
                nc.vector.scalar_tensor_tensor(row, heads[q][:], alpha, row, ALU.mult, ALU.add).then_inc(fin, 1)

            def row_stats(seg, w):
                nc.vector.bn_stats(stats[:, bass.ds(seg * 2 + w, 1), :].rearrange("p a d -> p (a d)"),
                                   x1[:, bass.ds(seg * 2 + w, 1), :].rearrange("p a d -> p (a d)"))

            def step(i, k, fresh=False, draining=False):
                def unit(lag):
                    j = stages(k, lag, 8, fresh, draining)
                    return (None, 0, 0) if j is None else (i * 8 + j, (j % 8) // UPS, j % UPS)

                u, q, g = unit(LS)
                done = (k - 1 - LO) // UPS if (k - 1 - LO) % UPS == UPS - 1 and (k > LO or not fresh) else None
                if u is not None:
                    if done is not None:
                        wait(dve, fin, (i * 2 + done) * 4 + 4)
                    wait(dve, scored, u + 1)
                    wait(dve, max_turned, u - (UPS - 1))
                    nc.vector.tensor_reduce(mx[g][:], psS[g][:], X, ALU.max).then_inc(max_ready, 1)
                    if done is not None:
                        row_stats(i * 2 + done, 0)
                        row_stats(i * 2 + done, 1)
                    wait(dve, max_ready, u + 1)
                    nc.vector.tensor_scalar(negmax[g][:, 0:UH], mx[g][:], -1.0, None, ALU.mult).then_inc(hi_ready, 1)
                    wait(dve, hi_ready, u + 1)
                    nc.vector.scalar_tensor_tensor(negmax[g][:, UH:2 * UH], mx[g][:], -1.0, negmax[g][:, 0:UH].bitcast(F32),
                                                   ALU.mult, ALU.subtract).then_inc(negmax_ready, 1)
                u, q, g = unit(LM)
                if u is not None:
                    wait(dve, max_turned, u + 1)
                    wait(dve, shifted, u - (UPS - 1))
                    nc.vector.tensor_tensor(shift[g][:], psM[:].unsqueeze(1).to_broadcast([2 * UH, UH, P]),
                                            c["rowmask"][:].unsqueeze(2).to_broadcast([2 * UH, UH, P]),
                                            ALU.mult).then_inc(shift_ready, 1)
                u, q, g = unit(LO)
                if u is not None:
                    wait(dve, out_raw, u + 1)
                    o = psO[g % 2][:, 0:UH * (OW + HD + 1)].rearrange("p (h d) -> p h d", h=UH)
                    nc.vector.reciprocal(rden[g][:].unsqueeze(2), o[:, :, HD:HD + 1]).then_inc(rden_ready, 1)
                    wait(dve, rden_ready, u + 1)
                    nc.vector.tensor_tensor(heads[q][:, g * UH * HD:(g + 1) * UH * HD].rearrange("p (h d) -> p h d", h=UH),
                                            o[:, :, 0:HD], rden[g][:].unsqueeze(2).to_broadcast([P, UH, HD]),
                                            ALU.mult).then_inc(heads_ready, 1)
                    if g == UPS - 1:
                        finish(i * 2 + (k - LO) // UPS, q)

            for k in range(8):
                step(0, k, fresh=True)
            with dve.Fori(1, NSEG // 2) as i:
                for k in range(8):
                    step(i, k)
            for k in range(LO):
                step(NSEG // 2, k, draining=True)
            dve.wait_ge(fin, NSEG * 4)
            for w in range(2):
                row_stats(NSEG - 1, w)


NCOL = SLOTS + 1


def normalise_and_route(nc, c, x1, stats, router_w, router_b, x1_dram, route, weights):
    ctx = ExitStack()
    m = Scope(nc, ctx, "route")
    with ctx:
        mean = m.sb("mean", [P, NT])
        rstd = m.sb("rstd", [P, NT])
        var = m.sb("var", [P, NT])
        tmp = m.sb("tmp", [P, NT])
        magic = m.sb("magic", [P, NT], I32)
        xn = [m.sb(f"xn{i}", [P, D]) for i in range(2)]
        xT = [m.sb(f"xT{i}", [P, KD, P]) for i in range(2)]
        rw = m.sb("rw", [P, KD, NE])
        rb = m.sb("rb", [P, NE])
        logit = m.sb("logit", [P, NT, NE])
        best = m.sb("best", [P, NT])
        expd = m.sb("expd", [P, NT, NE])
        cand = m.sb("cand", [P, NT, NE])
        bidx = m.sb("bidx", [P, NT])
        onehot = m.sb("onehot", [P, NT, NE])
        PADT = NT // 2
        count = [m.sb(f"count{i}", [P, PADT + NT, NE]) for i in range(2)]
        tiles = [m.sb(f"tiles{i}", [P, NE // 2 + NE]) for i in range(2)]
        nt_f = m.sb("nt_f", [P, NE])
        nt_i = m.sb("nt_i", [P, NE], I32)
        base = m.sb("base", [P, NE])
        place = m.sb("place", [P, NT])
        ptile_i = m.sb("ptile_i", [P, NT], I32)
        ptile = m.sb("ptile", [P, NT])
        prow = m.sb("prow", [P, NT])
        past = m.sb("past", [P, NCOL, NE - 1])
        sexp = m.sb("sexp", [P, NCOL])
        rows1 = m.sb("rows1", [P, NT, P], BF16)
        slots1 = m.sb("slots1", [P, NT, NCOL])
        ids = m.sb("ids", [P, NT, 2 * NCOL], BF16)
        psX = [m.ps(f"psX{i}", [P, KD, P]) for i in range(2)]
        psR = [m.ps(f"psR{i}", [P, 512]) for i in range(2)]
        psA = m.ps("psA", [P, NT, NE])
        psB = m.ps("psB", [P, NT, NE])
        psI = m.ps("psI", [P, 2 * NCOL])
        (w_loaded, chain, xn_ready, kept, turned, xT_ready, routed, logit_ready, diff_ready, exp_ready,
         onehot_ready, counted, tables_ready, gathered, stored) = (m.sem(s) for s in (
             "w_loaded", "chain", "xn_ready", "kept", "turned", "xT_ready", "routed", "logit_ready", "diff_ready",
             "exp_ready", "onehot_ready", "counted", "tables_ready", "gathered", "stored"))
        block = ctx.enter_context(nc.Block())

        @block.sync
        def _(sp):
            sp.dma_start(rw[:], router_w.rearrange("(k p) e -> p k e", p=P)).then_inc(w_loaded, 16)
            sp.dma_start(rb[:], router_b.partition_broadcast(P)).then_inc(w_loaded, 16)
            weights.load(sp, 0)
            for b in range(B):
                sp.wait_ge(kept, (b + 1) * TB)
                sp.dma_start(x1_dram.rearrange("(t p) d -> p t d", p=P)[:, b * TB:(b + 1) * TB, :],
                             x1[:, b * TB:(b + 1) * TB, :]).then_inc(stored, 16)
            sp.wait_ge(stored, 16 * B)

        @block.gpsimd
        def _(pool):
            weights.divide(pool, 0)

        @block.tensor
        def _(pe):
            def turn(t, q):
                wait(pe, xn_ready, t + 1)
                wait(pe, xT_ready, t - 1)
                for k in range(KD):
                    last = nc.tensor.transpose(psX[q][:, k, :], xn[q][:, k * P:(k + 1) * P], c["ident"][:])
                last.then_inc(turned, 1)

            def score(t, q):
                wait(pe, xT_ready, t + 1)
                wait(pe, logit_ready, t - 1)
                for k in range(KD):
                    last = nc.tensor.matmul(psR[q][:, 0:NE], xT[q][:, k, :], rw[:, k, :], start=k == 0, stop=k == KD - 1)
                last.then_inc(routed, 1)

            pe.wait_ge(w_loaded, 32)
            turn(0, 0)
            turn(1, 1)
            score(0, 0)
            with pe.Fori(1, NT // 2) as i:
                for q in range(2):
                    turn(i * 2 + q, q)
                    score(i * 2 + (q - 1), 1 - q)
            score(NT - 1, 1)
            pe.wait_ge(onehot_ready, 1)
            nc.tensor.matmul(psA[:].rearrange("p t e -> p (t e)"), c["tri"][:], onehot[:].rearrange("p t e -> p (t e)"),
                             start=True, stop=True).then_inc(counted, 1)
            nc.tensor.matmul(psB[:].rearrange("p t e -> p (t e)"), c["ones"][:], onehot[:].rearrange("p t e -> p (t e)"),
                             start=True, stop=True).then_inc(counted, 1)
            pe.wait_ge(tables_ready, 3)
            nc.tensor.matmul(psI[:], rows1[:, 0, :], ids[:, 0, :], start=True, stop=False)
            with pe.Fori(1, NT - 1) as t:
                nc.tensor.matmul(psI[:], rows1[:, bass.ds(t, 1), :].rearrange("p a r -> p (a r)"),
                                 ids[:, bass.ds(t, 1), :].rearrange("p a r -> p (a r)"), start=False, stop=False)
            nc.tensor.matmul(psI[:], rows1[:, NT - 1, :], ids[:, NT - 1, :], start=False, stop=True).then_inc(gathered, 1)

        @block.scalar
        def _(act):
            def move(t, q):
                wait(act, turned, t + 1)
                wait(act, routed, t - 1)
                nc.scalar.activation(xT[q][:], psX[q][:], ACT.Copy).then_inc(xT_ready, 1)

            move(0, 0)
            move(1, 1)
            with act.Fori(1, NT // 2) as i:
                for q in range(2):
                    move(i * 2 + q, q)
            act.wait_ge(diff_ready, 1)
            nc.scalar.activation(expd[:], expd[:], ACT.Exp).then_inc(exp_ready, 1)

        @block.vector
        def _(dve):
            v = nc.vector
            n = [0]

            def link(ins):
                n[0] += 1
                ins.then_inc(chain, 1)
                dve.wait_ge(chain, n[0])

            norm_steps(v, link, stats[:], mean[:], rstd[:], var[:], tmp[:], magic[:])

            def norm(t, q):
                mu, r = mean[:, bass.ds(t, 1)], rstd[:, bass.ds(t, 1)]
                row = x1[:, bass.ds(t, 1), :].rearrange("p a d -> p (a d)")
                wait(dve, turned, t - 1)
                v.tensor_scalar(xn[q][:], row, mu, r, ALU.subtract, ALU.mult).then_inc(xn_ready, 1)
                v.tensor_scalar(row, row, mu, r, ALU.subtract, ALU.mult).then_inc(kept, 1)

            def take(t, q):
                wait(dve, routed, t + 1)
                v.tensor_tensor(logit[:, bass.ds(t, 1), :].rearrange("p a e -> p (a e)"), psR[q][:, 0:NE], rb[:],
                                ALU.add).then_inc(logit_ready, 1)

            dve.wait_ge(w_loaded, 32)
            norm(0, 0)
            norm(1, 1)
            take(0, 0)
            with dve.Fori(1, NT // 2) as i:
                for q in range(2):
                    norm(i * 2 + q, q)
                    take(i * 2 + (q - 1), 1 - q)
            take(NT - 1, 1)
            dve.wait_ge(logit_ready, NT)
            link(v.tensor_reduce(best[:], logit[:], X, ALU.max))
            bc = lambda ap: ap.unsqueeze(2).to_broadcast([P, NT, NE])
            over_t = lambda ap: ap.unsqueeze(1).to_broadcast([P, NT, NE])
            v.tensor_tensor(expd[:], logit[:], bc(best[:]), ALU.subtract).then_inc(diff_ready, 1)
            dve.wait_ge(diff_ready, 1)
            link(v.tensor_tensor(cand[:], logit[:], bc(best[:]), ALU.is_ge))
            link(v.tensor_tensor(cand[:], cand[:], over_t(c["eidx"][:]), ALU.mult))
            link(v.tensor_reduce(bidx[:], cand[:], X, ALU.min))
            v.tensor_tensor(onehot[:], bc(bidx[:]), over_t(c["eidx"][:]), ALU.is_equal).then_inc(onehot_ready, 1)
            dve.wait_ge(exp_ready, 1)
            link(v.tensor_reduce(tmp[:], expd[:], X, ALU.add))
            v.reciprocal(route["prob"][:], tmp[:])
            for i in range(2):
                link(v.memset(count[i][:, 0:PADT, :], 0.0))
                link(v.memset(tiles[i][:, 0:NE // 2], 0.0))
            dve.wait_ge(counted, 2)
            link(v.tensor_copy(count[0][:, PADT:, :], psB[:]))
            a, shift = 0, 1
            while shift < NT:
                link(v.tensor_tensor(count[1 - a][:, PADT:, :], count[a][:, PADT:, :],
                                     count[a][:, PADT - shift:PADT + NT - shift, :], ALU.add))
                a, shift = 1 - a, 2 * shift
            total = count[a][:, PADT + NT - 1, :]
            link(v.tensor_scalar(nt_i[:], total, float(P - 1), None, ALU.add))
            link(v.tensor_scalar(nt_i[:], nt_i[:], 7, None, ALU.logical_shift_right))
            link(v.tensor_scalar(nt_f[:], nt_i[:], 1.0, None, ALU.max))
            half = NE // 2
            link(v.tensor_copy(tiles[0][:, half:], nt_f[:]))
            e, shift = 0, 1
            while shift < NE:
                link(v.tensor_tensor(tiles[1 - e][:, half:], tiles[e][:, half:], tiles[e][:, half - shift:half + NE - shift], ALU.add))
                e, shift = 1 - e, 2 * shift
            ends = tiles[e][:, half:]
            link(v.tensor_copy(route["ends"][:], ends))
            link(v.tensor_tensor(base[:], ends, nt_f[:], ALU.subtract))
            link(v.tensor_scalar(base[:], base[:], float(P), None, ALU.mult))
            run = count[1 - a][:, PADT:, :]
            link(v.tensor_tensor(run, count[a][:, PADT:, :], psB[:], ALU.subtract))
            link(v.tensor_tensor(run, run, psA[:], ALU.add))
            link(v.tensor_tensor(run, run, over_t(base[:]), ALU.add))
            link(v.tensor_tensor(run, run, onehot[:], ALU.mult))
            link(v.tensor_reduce(place[:], run, X, ALU.add))
            link(v.tensor_copy(route["place"][:], place[:]))
            link(v.tensor_scalar(ptile_i[:], route["place"][:], 7, None, ALU.logical_shift_right))
            link(v.tensor_copy(ptile[:], ptile_i[:]))
            link(v.scalar_tensor_tensor(prow[:], ptile[:], -float(P), place[:], ALU.mult, ALU.add))
            v.tensor_tensor(rows1[:], prow[:].unsqueeze(2).to_broadcast([P, NT, P]),
                            c["iota_r"][:].unsqueeze(1).to_broadcast([P, NT, P]), ALU.is_equal).then_inc(tables_ready, 1)
            link(v.tensor_tensor(slots1[:], ptile[:].unsqueeze(2).to_broadcast([P, NT, NCOL]),
                                 c["iota_s"][:].unsqueeze(1).to_broadcast([P, NT, NCOL]), ALU.is_equal))
            v.tensor_scalar(ids[:, :, 0:NCOL], slots1[:], c["iota_p"][:], None, ALU.mult).then_inc(tables_ready, 1)
            v.tensor_tensor(ids[:, :, NCOL:], slots1[:], c["iota_t"][:].unsqueeze(2).to_broadcast([P, NT, NCOL]),
                            ALU.mult).then_inc(tables_ready, 1)
            link(v.tensor_tensor(past[:], c["iota_s"][:].unsqueeze(2).to_broadcast([P, NCOL, NE - 1]),
                                 ends[:, 0:NE - 1].unsqueeze(1).to_broadcast([P, NCOL, NE - 1]), ALU.is_ge))
            link(v.tensor_reduce(sexp[:], past[:], X, ALU.add))
            link(v.tensor_copy(route["expert"][:], sexp[:]))
            link(v.tensor_scalar(route["buffer"][:], route["expert"][:], 1, None, ALU.bitwise_and))
            dve.wait_ge(gathered, 1)
            link(v.tensor_copy(slots1[:, 0, :], psI[:, 0:NCOL]))
            link(v.scalar_tensor_tensor(route["token"][:], psI[:, NCOL:], float(P), slots1[:, 0, :], ALU.mult, ALU.add))


def routing_tables(nc, ctx):
    m = Scope(nc, ctx, "table")
    return {"prob": m.sb("prob", [P, NT]), "place": m.sb("place", [P, NT], I32), "ends": m.sb("ends", [P, NE], I32),
            "expert": m.sb("expert", [P, NCOL], I32), "buffer": m.sb("buffer", [P, NCOL], I32),
            "token": m.sb("token", [P, NCOL], I32)}


NB = 512
FK = FF // P


class Weights:

    def __init__(self, nc, ctx, w1_dram, w2_dram):
        m = Scope(nc, ctx, "w")
        self.nc, self.w1_dram, self.w2_dram = nc, w1_dram, w2_dram
        self.raw1 = m.sb("raw1", [P, KD, 2 * FF])
        self.raw2 = m.sb("raw2", [P, FK, D])
        self.hi1 = m.sb("hi1", [P, 2, KD * 2 * FF], F32R)
        self.lo1 = m.sb("lo1", [P, 2, KD * 2 * FF], F32R)
        self.hi2 = m.sb("hi2", [P, 2, FK * D], F32R)
        self.lo2 = m.sb("lo2", [P, 2, FK * D], F32R)
        self.zero = m.sb("zero", [P, 1])
        self.loaded1, self.loaded2, self.zeroed = m.sem("loaded1"), m.sem("loaded2"), m.sem("zeroed")
        self.split = m.sem("split")

    def load(self, sp, e):
        wait(sp, self.split, 4 * e)
        sp.dma_start(self.raw1[:], self.w1_dram[e].rearrange("(k p) f -> p k f", p=P)).then_inc(self.loaded1, 16)
        sp.dma_start(self.raw2[:], self.w2_dram[e].rearrange("(k p) d -> p k d", p=P)).then_inc(self.loaded2, 16)

    def divide(self, pool, e):
        g, n = self.nc.gpsimd, 4 * e
        if e == 0:
            g.memset(self.zero[:], 0.0).then_inc(self.zeroed, 1)
            pool.wait_ge(self.zeroed, 1)
        for loaded, raw, hi, lo in ((self.loaded1, self.raw1, self.hi1, self.lo1), (self.loaded2, self.raw2, self.hi2, self.lo2)):
            flat = raw[:].rearrange("p k f -> p (k f)")
            pool.wait_ge(loaded, 16 * (e + 1))
            g.tensor_tensor(hi[:, e % 2, :], flat, self.zero[:].to_broadcast([P, flat.shape[1]]), ALU.add).then_inc(self.split, 1)
            pool.wait_ge(self.split, n + 1)
            g.tensor_tensor(lo[:, e % 2, :], flat, hi[:, e % 2, :].bitcast(F32), ALU.subtract).then_inc(self.split, 1)
            n += 2


def experts(nc, c, w, route, x1_dram, ys_dram):
    ctx = ExitStack()
    m = Scope(nc, ctx, "moe")
    FIRST = 8
    with ctx:
        xg = m.sb("xg", [P, NCOL, D])
        xs = m.sb("xs", [P, D])
        xh = m.sb("xh", [P, KD, P], F32R)
        xl = m.sb("xl", [P, KD, P], F32R)
        act_a = m.sb("act_a", [P, FF])
        hs = m.sb("hs", [P, FF])
        hh = m.sb("hh", [P, FK, P], F32R)
        hl = m.sb("hl", [P, FK, P], F32R)
        yo = [m.sb(f"yo{i}", [P, D]) for i in range(2)]
        psH = m.ps("psH", [P, 4, NB])
        psHT = m.ps("psHT", [P, FK, P])
        psX = m.ps("psX", [P, NB])
        psY = m.ps("psY", [P, NB])
        psXv = psX[:, 0:KD * P].rearrange("p (k t) -> p k t", k=KD)
        (xs_ready, x_turned, xh_ready, xl_ready, a_ready, g_ready, silu_ready, hs_ready, h_turned, hh_ready,
         hl_ready, y_raw, yo_ready) = (m.sem(s) for s in (
             "xs_ready", "x_turned", "xh_ready", "xl_ready", "a_ready", "g_ready", "silu_ready", "hs_ready",
             "h_turned", "hh_ready", "hl_ready", "y_raw", "yo_ready"))
        gathered = [m.sem(f"gathered{i}") for i in range(4)]
        stored = [m.sem(f"stored{i}") for i in range(2)]
        block = ctx.enter_context(nc.Block())

        def tiles(eng, step):
            for t in range(4):
                step(t, t % 4)
            with eng.Fori(1, SLOTS // 4) as i:
                for q in range(4):
                    step(i * 4 + q, q)
            for t in range(SLOTS // 4 * 4, SLOTS + 2):
                step(t, t % 4)

        def before(t, q, n):
            return (t - q) * (16 // n)

        ys_tiles = ys_dram.rearrange("(t p) d -> t p d", p=P)

        def live(t):
            return not isinstance(t, int) or 0 <= t < SLOTS

        @block.sync
        def _(sp):
            for e in range(1, NE):
                w.load(sp, e)

        @block.gpsimd
        def _(pool):
            def gather(slot):
                q = slot % 4
                wait(pool, gathered[q], 16 * (slot // 4))
                nc.gpsimd.indirect_dma_start(xg[:, slot, :], None, x1_dram,
                                             bass.IndirectOffsetOnAxis(route["token"][:, slot:slot + 1], 0)).then_inc(gathered[q], 16)

            for slot in range(FIRST):
                gather(slot)
            w.divide(pool, 1)
            for slot in range(FIRST, SLOTS):
                gather(slot)
            for e in range(2, NE):
                w_free = pool.value_load(route["ends"][0:1, e - 2:e - 1], min_val=1, max_val=SLOTS)
                pool.wait_ge(yo_ready, w_free)
                w.divide(pool, e)

        @block.tensor
        def _(pe):
            def buffer_of(t):
                return pe.value_load(route["buffer"][0:1, bass.ds(t, 1)], min_val=0, max_val=1)

            def step(s, q):
                t = s - 1
                if live(t):
                    e = pe.value_load(route["expert"][0:1, bass.ds(t, 1)], min_val=0, max_val=NE - 1)
                    b = buffer_of(t)
                    pe.wait_ge(xl_ready, t + 1)
                    pe.wait_ge(w.split, e * 4 + 4)
                    wait(pe, silu_ready, t)
                    for n in range(4):
                        if n == 2:
                            wait(pe, hs_ready, t)
                        first = True
                        for k in range(KD):
                            cols = slice(k * 2 * FF + n * NB, k * 2 * FF + (n + 1) * NB)
                            for xpart, wpart in ((xh, w.hi1), (xh, w.lo1), (xl, w.hi1)):
                                last = nc.tensor.matmul(psH[:, n, :], xpart[:, k, :],
                                                        wpart[:, bass.ds(b, 1), cols].rearrange("p a f -> p (a f)"),
                                                        start=first, stop=k == KD - 1 and xpart is xl)
                                first = False
                        if n == 1:
                            last.then_inc(a_ready, 1)
                    last.then_inc(g_ready, 1)
                t = s
                if live(t):
                    pe.wait_ge(xs_ready, t + 1)
                    wait(pe, xl_ready, t)
                    for k in range(KD):
                        last = nc.tensor.transpose(psXv[:, k, :], xs[:, k * P:(k + 1) * P], c["ident"][:])
                    last.then_inc(x_turned, 1)
                t = s - 2
                if live(t):
                    b = buffer_of(t)
                    pe.wait_ge(hl_ready, t + 1)
                    wait(pe, yo_ready, t)
                    first = True
                    for k in range(FK):
                        for hpart, wpart in ((hh, w.hi2), (hh, w.lo2), (hl, w.hi2)):
                            last = nc.tensor.matmul(psY[:, 0:D], hpart[:, k, :],
                                                    wpart[:, bass.ds(b, 1), k * D:(k + 1) * D].rearrange("p a f -> p (a f)"),
                                                    start=first, stop=k == FK - 1 and hpart is hl)
                            first = False
                    last.then_inc(y_raw, 1)
                t = s - 1
                if live(t):
                    pe.wait_ge(hs_ready, t + 1)
                    wait(pe, hl_ready, t)
                    for k in range(FK):
                        last = nc.tensor.transpose(psHT[:, k, :], hs[:, k * P:(k + 1) * P], c["ident"][:])
                    last.then_inc(h_turned, 1)

            tiles(pe, step)

        @block.scalar
        def _(act):
            def step(s, q):
                t = s - 3
                if live(t):
                    act.wait_ge(yo_ready, t + 1)
                    act.dma_start(ys_tiles[bass.ds(t, 1), :, :].rearrange("a p d -> (a p) d"), yo[1 - q % 2][:]).then_inc(stored[1 - q % 2], 16)
                t = s - 1
                if live(t):
                    act.wait_ge(a_ready, t + 1)
                    wait(act, hs_ready, t)
                    nc.scalar.activation(act_a[:], psH[:, 0:2, :].rearrange("p a b -> p (a b)"), ACT.Silu).then_inc(silu_ready, 1)
                t = s
                if live(t):
                    act.wait_ge(x_turned, t + 1)
                    wait(act, g_ready, t)
                    nc.scalar.activation(xh[:], psXv, ACT.Copy).then_inc(xh_ready, 1)
                t = s - 2
                if live(t):
                    act.wait_ge(y_raw, t + 1)
                    wait(act, stored[q % 2], before(t, q % 2, 2))
                    nc.scalar.activation(yo[q % 2][:], psY[:, 0:D], ACT.Copy).then_inc(yo_ready, 1)
                t = s - 1
                if live(t):
                    act.wait_ge(h_turned, t + 1)
                    wait(act, y_raw, t)
                    nc.scalar.activation(hh[:], psHT[:], ACT.Copy).then_inc(hh_ready, 1)

            tiles(act, step)
            act.wait_ge(yo_ready, SLOTS)
            act.dma_start(ys_tiles[SLOTS - 1], yo[(SLOTS - 1) % 2][:]).then_inc(stored[(SLOTS - 1) % 2], 16)
            act.wait_ge(stored[0], before(SLOTS + 1, 0, 2))
            act.wait_ge(stored[1], before(SLOTS, 1, 2))

        @block.vector
        def _(dve):
            v = nc.vector

            def step(s, q):
                t = s
                if live(t):
                    dve.wait_ge(gathered[q], before(t, q, 4) + 16)
                    wait(dve, x_turned, t)
                    v.tensor_copy(xs[:], xg[:, bass.ds(t, 1), :].rearrange("p a d -> p (a d)")).then_inc(xs_ready, 1)
                t = s - 1
                if live(t):
                    dve.wait_ge(silu_ready, t + 1)
                    dve.wait_ge(g_ready, t + 1)
                    wait(dve, h_turned, t)
                    v.tensor_tensor(hs[:], psH[:, 2:4, :].rearrange("p a b -> p (a b)"), act_a[:], ALU.mult).then_inc(hs_ready, 1)
                t = s
                if live(t):
                    dve.wait_ge(xh_ready, t + 1)
                    v.tensor_tensor(xl[:], psXv, xh[:].bitcast(F32), ALU.subtract).then_inc(xl_ready, 1)
                t = s - 1
                if live(t):
                    dve.wait_ge(hh_ready, t + 1)
                    v.tensor_tensor(hl[:], psHT[:], hh[:].bitcast(F32), ALU.subtract).then_inc(hl_ready, 1)

            tiles(dve, step)


EPS = 1e-6


def linear_attention(nc, c, route, x1_dram, ys_dram, w_dram, x):
    ctx = ExitStack()
    m = Scope(nc, ctx, "lin")
    with ctx:
        yg = [m.sb(f"yg{i}", [P, D]) for i in range(4)]
        xb = m.sb("xb", [P, TB, D])
        xh = m.sb("xh", [P, KD, TB, P], F32R)
        xl = m.sb("xl", [P, KD, TB, P], F32R)
        w_raw = m.sb("w_raw", [P, KD, 3 * D])
        wh = m.sb("wh", [P, KD, 3 * D], F32R)
        wl = m.sb("wl", [P, KD, 3 * D], F32R)
        qT = m.sb("qT", [P, KD, TB * P])
        qe = [m.sb(f"qe{i}", [P, NB]) for i in range(2)]
        ke = [m.sb(f"ke{i}", [P, D]) for i in range(2)]
        kk = [m.sb(f"kk{i}", [P, D]) for i in range(2)]
        v1 = [m.sb(f"v1{i}", [P, D + 1]) for i in range(2)]
        kv = m.sb("kv", [P, KD, D + 1])
        z = [m.sb(f"z{i}", [P, 2]) for i in range(2)]
        xo = m.sb("xo", [P, TB, D])
        stats = [m.sb(f"stats{i}", [P, TB, 6]) for i in range(2)]
        mean, var, rstd, tmp = (m.sb(s, [P, TB]) for s in ("mean", "var", "rstd", "tmp"))
        magic = m.sb("magic", [P, TB], I32)
        psX = m.ps("psX", [P, KD, P])
        psQ = [m.ps(f"psQ{i}", [P, NB]) for i in range(2)]
        psK = [m.ps(f"psK{i}", [P, 2 * D]) for i in range(2)]
        psC = [m.ps(f"psC{i}", [P, NB]) for i in range(KD)]
        psO = m.ps("psO", [P, NB])
        names = ("x_loaded", "w_loaded", "w_split", "summed", "xb_ready", "turned", "xh_ready", "xl_ready", "q_raw",
                 "q_exp", "q_min", "q_ready", "k_raw", "k_exp", "k_min", "k_ready", "v_ready", "added", "kv_ready", "o_raw", "z_ready",
                 "o_ready", "ones_set", "stat_in", "stat_out", "normed")
        (x_loaded, w_loaded, w_split, summed, xb_ready, turned, xh_ready, xl_ready, q_raw,
         q_exp, q_min, q_ready, k_raw, k_exp, k_min, k_ready, v_ready, added, kv_ready, o_raw, z_ready,
         o_ready, ones_set, stat_in, stat_out, normed) = (m.sem(s) for s in names)
        chain = [m.sem(f"chain{i}") for i in range(2)]
        gathered = [m.sem(f"gathered{i}") for i in range(4)]
        block = ctx.enter_context(nc.Block())
        NQ = KD * 2

        @block.sync
        def _(sp):
            sp.dma_start(w_raw[:], w_dram.rearrange("(k p) f -> p k f", p=P)).then_inc(w_loaded, 16)
            for b in range(B):
                sp.dma_start(x[:, b * TB:(b + 1) * TB, :],
                             x1_dram.rearrange("(t p) d -> p t d", p=P)[:, b * TB:(b + 1) * TB, :]).then_inc(x_loaded, 16)
                sp.wait_ge(x_loaded, 16 * (b + 1))

        @block.gpsimd
        def _(pool):
            for t in range(NT):
                wait(pool, gathered[t % 4], 16 * (t // 4))
                wait(pool, summed, t - 3)
                nc.gpsimd.indirect_dma_start(yg[t % 4][:], None, ys_dram,
                                             bass.IndirectOffsetOnAxis(route["place"][:, t:t + 1], 0)).then_inc(gathered[t % 4], 16)

        @block.tensor
        def _(pe):
            def turn(s):
                for j in range(TB):
                    t = s * TB + j
                    wait(pe, xb_ready, t + 1)
                    wait(pe, xl_ready, t)
                    for k in range(KD):
                        last = nc.tensor.transpose(psX[:, k, :], xb[:, j, k * P:(k + 1) * P], c["ident"][:])
                    last.then_inc(turned, 1)

            def project(s):
                wait(pe, xl_ready, s * TB + TB)
                for n in range(NQ):
                    chunk, half = divmod(n, 2)
                    wait(pe, q_ready, s * NQ + (n - 1))
                    cols = slice(chunk * P, (chunk + 1) * P)
                    for k in range(KD):
                        for a, (wpart, xpart) in enumerate(((wh, xh), (wh, xl), (wl, xh))):
                            last = nc.tensor.matmul(psQ[n % 2][:], wpart[:, k, cols],
                                                    xpart[:, k, half * 4:half * 4 + 4, :].rearrange("p a b -> p (a b)"),
                                                    start=k == 0 and a == 0, stop=k == KD - 1 and a == 2)
                    last.then_inc(q_raw, 1)

                def add_up(j):
                    t = s * TB + j
                    wait(pe, k_ready, t + 1)
                    wait(pe, v_ready, t + 1)
                    if j == 0:
                        wait(pe, kv_ready, s)
                    for chunk in range(KD):
                        last = nc.tensor.matmul(psC[chunk][:, 0:D + 1], kk[j % 2][:, chunk * P:(chunk + 1) * P], v1[j % 2][:],
                                                start=j == 0, stop=j == TB - 1)
                    last.then_inc(added, 1)

                for j in range(TB):
                    t = s * TB + j
                    wait(pe, k_ready, t - 1)
                    wait(pe, v_ready, t - 1)
                    for k in range(KD):
                        for a, (xpart, wpart) in enumerate(((xh, wh), (xh, wl), (xl, wh))):
                            last = nc.tensor.matmul(psK[j % 2][:], xpart[:, k, j, :], wpart[:, k, D:3 * D],
                                                    start=k == 0 and a == 0, stop=k == KD - 1 and a == 2)
                    last.then_inc(k_raw, 1)
                    if j > 0:
                        add_up(j - 1)
                add_up(TB - 1)

            def attend(s):
                wait(pe, kv_ready, s + 1)
                wait(pe, q_ready, s * NQ + NQ)
                for j in range(TB):
                    wait(pe, o_ready, s * TB + j)
                    for chunk in range(KD):
                        last = nc.tensor.matmul(psO[:, 0:D + 1], qT[:, chunk, j * P:(j + 1) * P], kv[:, chunk, :],
                                                start=chunk == 0, stop=chunk == KD - 1)
                    last.then_inc(o_raw, 1)

            pe.wait_ge(w_split, 2)
            def step(s):
                project(s - 1)
                turn(s)
                attend(s - 1)

            turn(0)
            step(1)
            with pe.Fori(2, B) as s:
                step(s)
            project(B - 1)
            attend(B - 1)

        @block.scalar
        def _(act):
            a_ = nc.scalar
            act.wait_ge(ones_set, 2)

            def turn(s):
                for j in range(TB):
                    t = s * TB + j
                    wait(act, turned, t + 1)
                    wait(act, k_raw, s * TB)
                    a_.activation(xh[:, :, j, :], psX[:], ACT.Copy).then_inc(xh_ready, 1)

            def project(s):
                for n in range(NQ):
                    wait(act, q_raw, s * NQ + (n + 1))
                    wait(act, q_ready, s * NQ + (n - 1))
                    a_.activation(qe[n % 2][:], psQ[n % 2][:], ACT.Exp).then_inc(q_exp, 1)
                for j in range(TB):
                    t = s * TB + j
                    wait(act, k_raw, t + 1)
                    wait(act, k_ready, t - 1)
                    a_.activation(ke[j % 2][:], psK[j % 2][:, 0:D], ACT.Exp).then_inc(k_exp, 1)
                    wait(act, added, t - 1)
                    a_.activation(v1[j % 2][:, 0:D], psK[j % 2][:, D:2 * D], ACT.Copy).then_inc(v_ready, 1)
                wait(act, added, s * TB + TB)
                wait(act, o_raw, s * TB)
                for chunk in range(KD):
                    last = a_.activation(kv[:, chunk, :], psC[chunk][:, 0:D + 1], ACT.Copy)
                last.then_inc(kv_ready, 1)

            turn(0)
            project(0)
            turn(1)
            with act.Fori(2, B) as s:
                project(s - 1)
                turn(s)
            project(B - 1)

        @block.vector
        def _(dve):
            v = nc.vector
            for i in range(2):
                v.memset(v1[i][:, D:D + 1], 1.0).then_inc(ones_set, 1)
            dve.wait_ge(w_loaded, 16)
            v.tensor_copy(wh[:], w_raw[:]).then_inc(w_split, 1)
            dve.wait_ge(w_split, 1)
            v.tensor_tensor(wl[:], w_raw[:], wh[:].bitcast(F32), ALU.subtract).then_inc(w_split, 1)

            def row(t):
                return x[:, bass.ds(t, 1), :].rearrange("p a d -> p (a d)")

            def root(s, which):
                n = [0]
                wait(dve, (stat_in, stat_out)[which], s * TB + TB)

                def link(ins):
                    n[0] += 1
                    ins.then_inc(chain[which], 1)
                    dve.wait_ge(chain[which], s * NORM_LINKS + n[0])

                norm_steps(v, link, stats[which][:], mean[:], rstd[:], var[:], tmp[:], magic[:])

            def residual(s, j):
                t = s * TB + j
                wait(dve, gathered[j % 4], s * 32 + (j // 4 + 1) * 16)
                wait(dve, x_loaded, s * 16 + 16)
                v.scalar_tensor_tensor(xb[:, j, :], yg[j % 4][:], route["prob"][:, bass.ds(t, 1)], row(t), ALU.mult, ALU.add).then_inc(summed, 1)
                wait(dve, summed, t + 1)
                v.bn_stats(stats[0][:, j, :], xb[:, j, :]).then_inc(stat_in, 1)

            def norm_in(s):
                root(s, 0)
                for j in range(TB):
                    t = s * TB + j
                    v.tensor_scalar(row(t), xb[:, j, :], mean[:, j:j + 1], rstd[:, j:j + 1], ALU.subtract, ALU.mult).then_inc(normed, 1)
                    v.tensor_scalar(xb[:, j, :], xb[:, j, :], mean[:, j:j + 1], rstd[:, j:j + 1], ALU.subtract, ALU.mult).then_inc(xb_ready, 1)
                for j in range(TB):
                    t = s * TB + j
                    wait(dve, xh_ready, t + 1)
                    v.tensor_tensor(xl[:, :, j, :], psX[:], xh[:, :, j, :].bitcast(F32), ALU.subtract).then_inc(xl_ready, 1)

            def elu(dst, raw, e, exp_sem, min_sem, out_sem, n):
                wait(dve, exp_sem, n + 1)
                v.tensor_scalar(e, e, 1.0, None, ALU.min).then_inc(min_sem, 1)
                wait(dve, min_sem, n + 1)
                v.scalar_tensor_tensor(dst, raw, 0.0, e, ALU.max, ALU.add).then_inc(out_sem, 1)

            def queries(s):
                wait(dve, o_raw, s * TB)
                for n in range(NQ):
                    chunk, half = divmod(n, 2)
                    elu(qT[:, chunk, half * NB:(half + 1) * NB], psQ[n % 2][:], qe[n % 2][:], q_exp, q_min, q_ready, s * NQ + n)

            def keys(s, j):
                t = s * TB + j
                wait(dve, added, t - 1)
                wait(dve, v_ready, t + 1)
                elu(kk[j % 2][:], psK[j % 2][:, 0:D], ke[j % 2][:], k_exp, k_min, k_ready, t)

            def outputs(s):
                wait(dve, normed, s * TB + TB)
                for j in range(TB):
                    t = s * TB + j
                    wait(dve, o_raw, t + 1)
                    v.tensor_scalar(z[j % 2][:, 0:1], psO[:, D:D + 1], EPS, None, ALU.add).then_inc(z_ready, 1)
                    wait(dve, z_ready, s * (2 * TB) + (2 * j + 1))
                    v.reciprocal(z[j % 2][:, 1:2], z[j % 2][:, 0:1]).then_inc(z_ready, 1)
                    wait(dve, z_ready, s * (2 * TB) + (2 * j + 2))
                    v.scalar_tensor_tensor(xo[:, j, :], psO[:, 0:D], z[j % 2][:, 1:2], row(t), ALU.mult, ALU.add).then_inc(o_ready, 1)
                    wait(dve, o_ready, t + 1)
                    v.bn_stats(stats[1][:, j, :], xo[:, j, :]).then_inc(stat_out, 1)
                root(s, 1)
                for j in range(TB):
                    t = s * TB + j
                    v.tensor_scalar(row(t), xo[:, j, :], mean[:, j:j + 1], rstd[:, j:j + 1], ALU.subtract, ALU.mult)

            def step(s):
                queries(s - 1)
                for j in range(TB):
                    keys(s - 1, j)
                    residual(s, j)
                norm_in(s)
                outputs(s - 1)

            for j in range(TB):
                residual(0, j)
            norm_in(0)
            step(1)
            with dve.Fori(2, B) as s:
                step(s)
            queries(B - 1)
            for j in range(TB):
                keys(B - 1, j)
            outputs(B - 1)


N, PS = 64, 32
NP = N * PS
BLK = 256
NBLK = NP // BLK
NPB = BLK // PS
MC = TB
CH = NP // P
MB = 4


def soft_state(nc, ctx):
    m = Scope(nc, ctx, "soft")
    return {"xh": m.sb("xh", [P, KD, NT * P], F32R), "xl": m.sb("xl", [P, KD, NT * P], F32R),
            "ph": m.sb("ph", [P, KD, NP], F32R), "pl": m.sb("pl", [P, KD, NP], F32R),
            "rowmax": m.sb("rowmax", [P, NT, NBLK])}


def turn_tokens(nc, c, st, x, phi_dram):
    ctx = ExitStack()
    m = Scope(nc, ctx, "turn")
    with ctx:
        phi = m.sb("phi", [P, KD, NP])
        psX = [m.ps(f"psX{i}", [P, 2, KD, P]) for i in range(4)]
        loaded, split, turned, hi, lo = (m.sem(s) for s in ("loaded", "split", "turned", "hi", "lo"))
        block = ctx.enter_context(nc.Block())

        @block.sync
        def _(sp):
            sp.dma_start(phi[:], phi_dram.rearrange("(k p) n s -> p k (n s)", p=P)).then_inc(loaded, 16)

        @block.gpsimd
        def _(pool):
            pool.wait_ge(split, 1)
            nc.gpsimd.tensor_tensor(st["pl"][:], phi[:], st["ph"][:].bitcast(F32), ALU.subtract)

        @block.tensor
        def _(pe):
            for g in range(NT // 2):
                wait(pe, lo, g - 3)
                for a in range(2):
                    for k in range(KD):
                        last = nc.tensor.transpose(psX[g % 4][:, a, k, :], x[:, 2 * g + a, k * P:(k + 1) * P], c["ident"][:])
                last.then_inc(turned, 1)

        def view(part, g):
            return st[part][:, :, bass.ds(g * 2 * P, 2 * P)].rearrange("p k (a t) -> p a k t", a=2)

        @block.scalar
        def _(act):
            with act.Fori(0, NT // 8) as i:
                for q in range(4):
                    act.wait_ge(turned, i * 4 + (q + 1))
                    nc.scalar.activation(view("xh", i * 4 + q), psX[q][:], ACT.Copy).then_inc(hi, 1)

        @block.vector
        def _(dve):
            dve.wait_ge(loaded, 16)
            nc.vector.tensor_copy(st["ph"][:], phi[:]).then_inc(split, 1)
            with dve.Fori(0, NT // 8) as i:
                for q in range(4):
                    dve.wait_ge(hi, i * 4 + (q + 1))
                    nc.vector.tensor_tensor(view("xl", i * 4 + q), psX[q][:], view("xh", i * 4 + q).bitcast(F32),
                                            ALU.subtract).then_inc(lo, 1)


def dispatch(nc, c, st, x, w_dram, b_dram, y_dram):
    LAG = 3
    ctx = ExitStack()
    m = Scope(nc, ctx, "disp")
    with ctx:
        e = [m.sb(f"e{i}", [P, B, BLK]) for i in range(4)]
        t2 = [m.sb(f"t2{i}", [P, 2, BLK]) for i in range(2)]
        top = [m.sb(f"top{i}", [P, BLK]) for i in range(2)]
        s2 = [m.sb(f"s2{i}", [P, 2, BLK]) for i in range(2)]
        rs = [m.sb(f"rs{i}", [P, BLK]) for i in range(2)]
        slots = m.sb("slots", [P, KD, NPB, B, PS])
        wt = m.sb("wt", [P, KD, NPB, D])
        bt = m.sb("bt", [P, NPB, D])
        yb = m.sb("yb", [P, NPB, D])
        psL = [m.ps(f"psL{i}", [P, B, BLK]) for i in range(2)]
        psS = [m.ps(f"psS{i}", [P, B, BLK]) for i in range(KD)]
        names = ("w_loaded", "b_loaded", "logits", "copied", "pair_max", "top_ready", "less", "exp_ready", "pair_sum", "sum_ready",
                 "rsum_ready", "share_ready", "gone", "slots_ready", "y_raw", "y_ready", "stored")
        (w_loaded, b_loaded, logits, copied, pair_max, top_ready, less, exp_ready, pair_sum, sum_ready,
         rsum_ready, share_ready, gone, slots_ready, y_raw, y_ready, stored) = (m.sem(s) for s in names)
        block = ctx.enter_context(nc.Block())
        HALF = NPB // 2
        EVAC = LAG - 1
        y_step = {4: 0, 5: 1}
        l_bank = (0, 1, 0, 1, 0, 0, 0, 1)
        Y_BANK = 1

        @block.sync
        def _(sp):
            def load(first):
                for kd in range(KD):
                    sp.dma_start(wt[:, kd], w_dram[bass.ds(first, NPB), kd * P:(kd + 1) * P, :].rearrange("n p e -> p n e")).then_inc(w_loaded, 16)
                sp.dma_start(bt[:], b_dram[bass.ds(first, NPB), :].partition_broadcast(P)).then_inc(b_loaded, 16)

            def store(k, first):
                sp.wait_ge(y_ready, k * 2 + 2)
                for b in range(B):
                    sp.dma_start(y_dram[b, bass.ds(first, NPB), :, :].rearrange("n s e -> s n e"),
                                 yb[b * PS:(b + 1) * PS, :, :]).then_inc(stored, 16)

            load(0)
            with sp.Fori(1, NBLK) as k:
                here, last = sp.snap(k * NPB), sp.snap((k - 1) * NPB)
                store(k - 1, last)
                sp.wait_ge(stored, k * (16 * B))
                load(here)
            store(NBLK - 1, (NBLK - 1) * NPB)
            sp.wait_ge(stored, NBLK * 16 * B)

        @block.tensor
        def _(pe):
            def score(k, mc):
                g = k * MC + mc
                wait(pe, copied, g - 1 if mc < 5 else g if mc < 7 else g - 3)
                if mc == 7:
                    wait(pe, y_ready, k * 2)
                p = l_bank[mc]
                for b in range(B):
                    t = b * TB + mc
                    for kd in range(KD):
                        for a, (xp, pp) in enumerate((("xh", "ph"), ("xh", "pl"), ("xl", "ph"))):
                            last = nc.tensor.matmul(psL[p][:, b, :], st[xp][:, kd, t * P:(t + 1) * P],
                                                    st[pp][:, kd, bass.ds(k * BLK, BLK)],
                                                    start=b % 2 == 0 and kd == 0 and a == 0, stop=kd == KD - 1 and a == 2,
                                                    skip_group_check=True)
                last.then_inc(logits, 1)

            def contract(k, mc):
                g = k * MC + mc
                wait(pe, share_ready, g + 1)
                if mc == 0:
                    wait(pe, slots_ready, k * KD)
                for kd in range(KD):
                    for b in range(B):
                        last = nc.tensor.matmul(psS[kd][:, b, :], x[:, b * TB + mc, kd * P:(kd + 1) * P], e[mc % 4][:, b, :],
                                                start=mc == 0 and b % 2 == 0, stop=mc == MC - 1, skip_group_check=True)
                last.then_inc(gone, 1)

            def expert(k, h, copies):
                wait(pe, w_loaded, k * (16 * KD) + 16 * KD)
                wait(pe, slots_ready, k * KD + KD)
                wait(pe, copied, copies)
                if h == 1:
                    wait(pe, y_ready, k * 2 + 1)
                for i in range(HALF):
                    for kd in range(KD):
                        last = nc.tensor.matmul(psL[Y_BANK][:, i, :], slots[:, kd, h * HALF + i, :, :].rearrange("p b s -> p (b s)"),
                                                wt[:, kd, h * HALF + i, :], start=kd == 0 and i % 2 == 0, stop=kd == KD - 1,
                                                skip_group_check=True)
                last.then_inc(y_raw, 1)

            def step(k, mc, fresh=False, draining=False):
                if not draining:
                    score(k, mc)
                if mc >= LAG and not draining:
                    contract(k, mc - LAG)
                if mc < LAG and not fresh:
                    contract(k - 1, mc - LAG + MC)
                if mc in y_step and not fresh:
                    expert(k - 1, y_step[mc], NBLK * MC if draining else k * MC + 4)

            for mc in range(MC):
                step(0, mc, fresh=True)
            with pe.Fori(1, NBLK) as k:
                for mc in range(MC):
                    step(k, mc)
            for mc in range(MC):
                step(NBLK, mc, draining=True)

        @block.scalar
        def _(act):
            def step(k, mc, fresh=False, draining=False):
                g = k * MC + mc
                if not draining:
                    wait(act, less, g + 1)
                    nc.scalar.activation(e[mc % 4][:], e[mc % 4][:], ACT.Exp).then_inc(exp_ready, 1)
                if mc == EVAC and not fresh:
                    wait(act, gone, k * MC)
                    for kd in range(KD):
                        nc.scalar.activation(slots[:, kd].rearrange("p n b s -> p b n s"),
                                             psS[kd][:].rearrange("p b (n s) -> p b n s", s=PS), ACT.Copy).then_inc(slots_ready, 1)

            for mc in range(MC):
                step(0, mc, fresh=True)
            with act.Fori(1, NBLK) as k:
                for mc in range(MC):
                    step(k, mc)
            step(NBLK, EVAC, draining=True)

        @block.gpsimd
        def _(pool):
            def share(g, q):
                wait(pool, rsum_ready, g + 1)
                nc.gpsimd.tensor_tensor(e[q % 4][:], e[q % 4][:], rs[q % 2][:].unsqueeze(1).to_broadcast([P, B, BLK]),
                                        ALU.mult).then_inc(share_ready, 1)

            def step(k, mc, fresh=False):
                g = k * MC + mc
                wait(pool, top_ready, g + 1)
                nc.gpsimd.tensor_tensor(e[mc % 4][:], e[mc % 4][:], top[mc % 2][:].unsqueeze(1).to_broadcast([P, B, BLK]),
                                        ALU.subtract).then_inc(less, 1)
                if mc > 0 or not fresh:
                    share(g - 1, mc + 7)

            for mc in range(MC):
                step(0, mc, fresh=True)
            with pool.Fori(1, NBLK) as k:
                for mc in range(MC):
                    step(k, mc)
            share(NBLK * MC - 1, MC - 1)

        @block.vector
        def _(dve):
            v = nc.vector

            def sums(g, q):
                wait(dve, exp_ready, g + 1)
                v.tensor_tensor(s2[q % 2][:], e[q % 4][:, 0:2, :], e[q % 4][:, 2:4, :], ALU.add).then_inc(pair_sum, 1)
                wait(dve, pair_sum, g + 1)
                wait(dve, share_ready, g - 1)
                v.tensor_tensor(rs[q % 2][:], s2[q % 2][:, 0, :], s2[q % 2][:, 1, :], ALU.add).then_inc(sum_ready, 1)
                wait(dve, sum_ready, g + 1)
                v.reciprocal(rs[q % 2][:], rs[q % 2][:]).then_inc(rsum_ready, 1)

            def copy_y(k, h):
                wait(dve, y_raw, k * 2 + (h + 1))
                wait(dve, b_loaded, k * 16 + 16)
                v.tensor_tensor(yb[:, h * HALF:(h + 1) * HALF, :], psL[Y_BANK][:], bt[:, h * HALF:(h + 1) * HALF, :],
                                ALU.add).then_inc(y_ready, 1)

            def step(k, mc, fresh=False, draining=False):
                g = k * MC + mc
                if mc - 1 in y_step and not fresh:
                    copy_y(k - 1, y_step[mc - 1])
                if draining:
                    return
                wait(dve, logits, g + 1)
                wait(dve, gone, g - 3)
                for b in range(B):
                    last = v.tensor_scalar(e[mc % 4][:, b, :], psL[l_bank[mc]][:, b, :], 1.0, None, ALU.mult, ALU.max,
                                           accum_out=st["rowmax"][:, b * TB + mc, bass.ds(k, 1)])
                last.then_inc(copied, 1)
                wait(dve, copied, g + 1)
                v.tensor_tensor(t2[mc % 2][:], e[mc % 4][:, 0:2, :], e[mc % 4][:, 2:4, :], ALU.max).then_inc(pair_max, 1)
                wait(dve, pair_max, g + 1)
                wait(dve, less, g - 1)
                v.tensor_tensor(top[mc % 2][:], t2[mc % 2][:, 0, :], t2[mc % 2][:, 1, :], ALU.max).then_inc(top_ready, 1)
                if mc > 0 or not fresh:
                    sums(g - 1, mc + 7)

            for mc in range(MC):
                step(0, mc, fresh=True)
            with dve.Fori(1, NBLK) as k:
                for mc in range(MC):
                    step(k, mc)
            sums(NBLK * MC - 1, MC - 1)
            for mc in range(MC):
                step(NBLK, mc, draining=True)


def combine(nc, c, st, x, y_dram, out_dram):
    LAG = 2
    W = D + 2
    HALVES = TB // MB
    STEPS = HALVES * CH
    ctx = ExitStack()
    m = Scope(nc, ctx, "comb")
    with ctx:
        top = m.sb("top", [P, NT])
        negtop = m.sb("negtop", [P, 2 * NT], F32R)
        tops = m.sb("tops", [2 * NT, P])
        mask = m.sb("mask", [2 * NT, NT + TB])
        ones = m.sb("ones", [2 * NT, P], F32R)
        shift = [m.sb(f"shift{i}", [2 * NT, MB, P], F32R) for i in range(2)]
        zero = m.sb("zero", [P, 1])
        y_in = m.sb("y_in", [P, CH // 2, D])
        yh = m.sb("yh", [P, CH, W], F32R)
        yl = m.sb("yl", [P, CH, W], F32R)
        e = [m.sb(f"e{i}", [P, MB * P]) for i in range(2)]
        eh = [m.sb(f"eh{i}", [P, MB * P], F32R) for i in range(4)]
        el = [m.sb(f"el{i}", [P, MB * P], F32R) for i in range(4)]
        rden = m.sb("rden", [P, MB])
        xo = m.sb("xo", [P, MB, D])
        stats = m.sb("stats", [P, MB, 6])
        mean, var, rstd, tmp = (m.sb(s, [P, MB]) for s in ("mean", "var", "rstd", "tmp"))
        magic = m.sb("magic", [P, MB], I32)
        psL = [m.ps(f"psL{i}", [P, MB * P]) for i in range(4)]
        psO = [m.ps(f"psO{i}", [P, 512]) for i in range(MB)]
        names = ("made", "chain", "top_ready", "neg_ready", "top_turned", "tops_ready", "shift_ready", "y_loaded", "y_split",
                 "logits", "exp_ready", "hi_ready", "lo_ready", "gone", "rden_ready", "summed", "stat", "normed", "stored")
        (made, chain, top_ready, neg_ready, top_turned, tops_ready, shift_ready, y_loaded, y_split,
         logits, exp_ready, hi_ready, lo_ready, gone, rden_ready, summed, stat, normed, stored) = (m.sem(s) for s in names)
        block = ctx.enter_context(nc.Block())

        @block.sync
        def _(sp):
            dst = out_dram.rearrange("b (g p w) d -> p (b g) w d", p=P, w=2)

            def load(b):
                y = y_dram[b].rearrange("n s e -> (n s) e").rearrange("(c p) e -> p c e", p=P)
                for h in range(2):
                    wait(sp, y_split, b * (2 * CH) + h * CH)
                    sp.dma_start(y_in[:], y[:, h * CH // 2:(h + 1) * CH // 2, :]).then_inc(y_loaded, 16)

            def store(mb):
                sp.wait_ge(normed, mb * MB + MB)
                sp.dma_start(dst[:, mb * MB // 2:(mb + 1) * MB // 2, :, :],
                             x[:, mb * MB:(mb + 1) * MB, :].rearrange("p (g w) d -> p g w d", w=2)).then_inc(stored, 16)

            load(0)
            for b in range(B):
                if b + 1 < B:
                    load(b + 1)
                if b > 0:
                    store(2 * b - 2)
                    store(2 * b - 1)
            store(B * HALVES - 2)
            store(B * HALVES - 1)
            sp.wait_ge(stored, B * HALVES * 16)

        @block.gpsimd
        def _(pool):
            g_ = nc.gpsimd
            g_.memset(mask[:], 0.0).then_inc(made, 1)
            g_.memset(ones[:].bitcast(F32), 1.0).then_inc(made, 1)
            g_.memset(zero[:], 0.0).then_inc(made, 1)
            g_.memset(yh[:, :, D:D + 1].bitcast(F32), 1.0).then_inc(made, 1)
            g_.memset(yh[:, :, D + 1:W].bitcast(F32), 0.0).then_inc(made, 1)
            g_.memset(yl[:, :, D:W].bitcast(F32), 0.0).then_inc(made, 1)
            pool.wait_ge(made, 6)
            for n in range(2):
                g_.affine_select(out=mask[:], in_=mask[:], compare_op=ALU.not_equal, fill=1.0, base=-n * NT,
                                 pattern=[[-1, NT + TB]], channel_multiplier=1).then_inc(made, 1)
                pool.wait_ge(made, 7 + n)

            def split(b, ch):
                y = y_in[:, ch % (CH // 2), :]
                if ch % (CH // 2) == 0:
                    wait(pool, y_loaded, b * 32 + (ch // (CH // 2) + 1) * 16)
                g_.tensor_tensor(yh[:, ch, 0:D], y, zero[:].to_broadcast([P, D]), ALU.add).then_inc(y_split, 1)
                wait(pool, y_split, b * (2 * CH) + (ch * 2 + 1))
                g_.tensor_tensor(yl[:, ch, 0:D], y, yh[:, ch, 0:D].bitcast(F32), ALU.subtract).then_inc(y_split, 1)

            for ch in range(CH):
                split(0, ch)
            with pool.Fori(1, B) as b:
                for ch in range(CH):
                    pool.wait_ge(gone, b * STEPS + (ch - (CH - 1)))
                    split(b, ch)

        @block.tensor
        def _(pe):
            pe.wait_ge(neg_ready, 2)
            nc.tensor.transpose(psL[0][0:2 * NT, 0:P], negtop[:].bitcast(F32), c["ident"][:]).then_inc(top_turned, 1)
            pe.wait_ge(tops_ready, 1)

            def score(b, s):
                half, ch = divmod(s, CH)
                g = b * STEPS + s
                wait(pe, exp_ready, g - 3)
                if ch == 0:
                    wait(pe, shift_ready, b * HALVES + (half + 1))
                cols = slice(ch * P, (ch + 1) * P)
                first = True
                for kd in range(KD):
                    for pp, xp in (("ph", "xh"), ("ph", "xl"), ("pl", "xh")):
                        nc.tensor.matmul(psL[ch % 4][:], st[pp][:, kd, cols],
                                         st[xp][:, kd, bass.ds(b * (TB * P) + half * (MB * P), MB * P)],
                                         start=first, stop=False)
                        first = False
                nc.tensor.matmul(psL[ch % 4][:], ones[:], shift[half][:].rearrange("p a t -> p (a t)"),
                                 start=False, stop=True).then_inc(logits, 1)

            def contract(b, s):
                half, ch = divmod(s, CH)
                g = b * STEPS + s
                wait(pe, lo_ready, g + 1)
                if half == 0:
                    wait(pe, y_split, b * (2 * CH) + (2 * ch + 2))
                if ch == 0:
                    wait(pe, summed, b * TB + half * MB)
                for a in range(MB):
                    sub = slice(a * P, (a + 1) * P)
                    for n, (ep, yp) in enumerate(((eh, yh), (eh, yl), (el, yh))):
                        last = nc.tensor.matmul(psO[a][:, 0:W], ep[ch % 4][:, sub], yp[:, ch, :],
                                                start=ch == 0 and n == 0, stop=ch == CH - 1 and n == 2)
                last.then_inc(gone, 1)

            def step(b, s, fresh=False, draining=False):
                if not draining:
                    score(b, s)
                if s >= LAG and not draining:
                    contract(b, s - LAG)
                if s < LAG and not fresh:
                    contract(b - 1, s - LAG + STEPS)

            for s in range(STEPS):
                step(0, s, fresh=True)
            with pe.Fori(1, B) as b:
                for s in range(STEPS):
                    step(b, s)
            for s in range(LAG):
                step(B, s, draining=True)

        @block.scalar
        def _(act):
            def step(i, s):
                g = i * 4 + s
                wait(act, logits, g + 1)
                wait(act, lo_ready, g - 1)
                nc.scalar.activation(e[s % 2][:], psL[s][:], ACT.Exp).then_inc(exp_ready, 1)

            for s in range(4):
                step(0, s)
            with act.Fori(1, B * STEPS // 4) as i:
                for s in range(4):
                    step(i, s)

        @block.vector
        def _(dve):
            v = nc.vector
            v.tensor_reduce(top[:], st["rowmax"][:], X, ALU.max).then_inc(top_ready, 1)
            dve.wait_ge(top_ready, 1)
            v.tensor_scalar(negtop[:, 0:NT], top[:], -1.0, None, ALU.mult).then_inc(neg_ready, 1)
            dve.wait_ge(neg_ready, 1)
            v.scalar_tensor_tensor(negtop[:, NT:], top[:], -1.0, negtop[:, 0:NT].bitcast(F32), ALU.mult, ALU.subtract).then_inc(neg_ready, 1)
            dve.wait_ge(top_turned, 1)
            v.tensor_copy(tops[:], psL[0][0:2 * NT, 0:P]).then_inc(tops_ready, 1)
            dve.wait_ge(tops_ready, 1)
            dve.wait_ge(made, 8)

            def spread(b, half):
                v.tensor_tensor(shift[half][:], tops[:].unsqueeze(1).to_broadcast([2 * NT, MB, P]),
                                mask[:, bass.ds(b * TB + half * MB, MB)].unsqueeze(2).to_broadcast([2 * NT, MB, P]),
                                ALU.mult).then_inc(shift_ready, 1)

            spread(0, 0)
            def row(t):
                return x[:, bass.ds(t, 1), :].rearrange("p a d -> p (a d)")

            def collect(b, half):
                t0 = b * TB + half * MB
                wait(dve, gone, b * STEPS + (half * CH + CH))
                for a in range(MB):
                    v.reciprocal(rden[:, a:a + 1], psO[a][:, D:D + 1]).then_inc(rden_ready, 1)
                wait(dve, rden_ready, t0 + MB)
                for a in range(MB):
                    v.scalar_tensor_tensor(xo[:, a, :], psO[a][:, 0:D], rden[:, a:a + 1], row(t0 + a), ALU.mult, ALU.add).then_inc(summed, 1)

            def moments(b, half):
                t0 = b * TB + half * MB
                wait(dve, summed, t0 + MB)
                for a in range(MB):
                    v.bn_stats(stats[:, a, :], xo[:, a, :]).then_inc(stat, 1)

            def norm(b, half):
                t0 = b * TB + half * MB
                n = [0]
                wait(dve, stat, t0 + MB)

                def link(ins):
                    n[0] += 1
                    ins.then_inc(chain, 1)
                    dve.wait_ge(chain, b * (HALVES * NORM_LINKS) + (half * NORM_LINKS + n[0]))

                norm_steps(v, link, stats[:], mean[:], rstd[:], var[:], tmp[:], magic[:])
                for a in range(MB):
                    v.tensor_scalar(row(t0 + a), xo[:, a, :], mean[:, a:a + 1], rstd[:, a:a + 1], ALU.subtract, ALU.mult).then_inc(normed, 1)

            def step(b, s, fresh=False):
                half, ch = divmod(s, CH)
                g = b * STEPS + s
                wait(dve, exp_ready, g + 1)
                wait(dve, gone, g - 3)
                v.tensor_copy(eh[s % 4][:], e[s % 2][:]).then_inc(hi_ready, 1)
                wait(dve, hi_ready, g + 1)
                v.tensor_tensor(el[s % 4][:], e[s % 2][:], eh[s % 4][:].bitcast(F32), ALU.subtract).then_inc(lo_ready, 1)
                if s == LAG + 2:
                    spread(b, 1)
                if s == CH + LAG + 2:
                    spread(b + 1, 0)
                if half > 0 or not fresh:
                    before = (b, half - 1) if half > 0 else (b - 1, HALVES - 1)
                    if ch == LAG - 1:
                        collect(*before)
                    if ch == LAG:
                        moments(*before)
                    if ch == LAG + 1:
                        norm(*before)

            for s in range(STEPS):
                step(0, s, fresh=True)
            with dve.Fori(1, B) as b:
                for s in range(STEPS):
                    step(b, s)
            collect(B - 1, HALVES - 1)
            moments(B - 1, HALVES - 1)
            norm(B - 1, HALVES - 1)


def program(nc, x_in, router_w, router_b, w1, w2, w_attn, phi, w_slot, b_slot, out):
    x1_dram = nc.dram_tensor("x1_rows", [NT * P, D], F32, kind="Internal").ap()
    ys_dram = nc.dram_tensor("sorted_y", [SLOTS * P, D], F32, kind="Internal").ap()
    y_dram = nc.dram_tensor("slot_y", [B, N, PS, D], F32, kind="Internal").ap()
    with ExitStack() as ctx:
        c = {}
        route = routing_tables(nc, ctx)
        with ExitStack() as held:
            constants(nc, ctx, held, c)
            weights = Weights(nc, held, w1, w2)
            with ExitStack() as first:
                m = Scope(nc, first, "first")
                x1 = m.sb("x", [P, NT, D])
                stats = m.sb("stats", [P, NT, 6])
                dilated_attention(nc, c, x_in, x1, stats)
                normalise_and_route(nc, c, x1, stats, router_w, router_b, x1_dram, route, weights)
            experts(nc, c, weights, route, x1_dram, ys_dram)
        x = Scope(nc, ctx, "last").sb("x", [P, NT, D])
        linear_attention(nc, c, route, x1_dram, ys_dram, w_attn, x)
        state = soft_state(nc, ctx)
        turn_tokens(nc, c, state, x, phi)
        dispatch(nc, c, state, x, w_slot, b_slot, y_dram)
        combine(nc, c, state, x, y_dram, out)


def kernel(L0_attn_x, L0_ffn_router_w, L0_ffn_router_b, L0_ffn_w1, L0_ffn_w2, L1_attn_W, L1_ffn_phi, L1_ffn_W, L1_ffn_b):
    import numpy as np
    import concourse.bacc as bacc
    from concourse.bass_utils import run_bass_kernel_spmd

    nc = bacc.Bacc("TRN2", target_bir_lowering=False, num_devices=1)
    given = {"x": L0_attn_x, "router_w": L0_ffn_router_w, "router_b": L0_ffn_router_b, "w1": L0_ffn_w1, "w2": L0_ffn_w2,
             "w_attn": L1_attn_W, "phi": L1_ffn_phi, "w_slot": L1_ffn_W, "b_slot": L1_ffn_b}
    arrays, args = {}, []
    for name, value in given.items():
        a = np.ascontiguousarray(value)
        arrays[f"in_{name}"] = a
        args.append(nc.dram_tensor(f"in_{name}", a.shape, mybir.dt.from_np(a.dtype), kind="ExternalInput").ap())
    args.append(nc.dram_tensor("out", (B, S, D), F32, kind="ExternalOutput").ap())
    program(nc, *args)
    return run_bass_kernel_spmd(nc, [arrays], core_ids=[0]).results[0]["out"]
```

```python
from contextlib import ExitStack

import concourse.bass as bass
from concourse import mybir

ALU = mybir.AluOpType
ACT = mybir.ActivationFunctionType
X = mybir.AxisListType.X
F32 = mybir.dt.float32
F32R = mybir.dt.float32r
BF16 = mybir.dt.bfloat16
I32 = mybir.dt.int32

P = 128
B, S, D = 4, 1024, 256
KD = D // P
SEG = 256
NSEG = B * S // SEG
NT = B * S // P
TB = NT // B
NH, HD = 16, 16
UH = 4
UPS = NH // UH
HG = P // HD // UH
NE, FF = 8, 1024
SLOTS = NT + NE - 1
LN_EPS = 1e-5


def wait(eng, sem, count):
    if not isinstance(count, int) or count > 0:
        eng.wait_ge(sem, count)


def stages(step, lag, period, fresh, draining):
    k = step - lag
    if k < 0:
        return None if fresh else k
    return None if draining else k


def norm_steps(v, link, stats, mean, rstd, var, tmp, magic):
    link(v.tensor_tensor(mean, stats[:, :, 1], stats[:, :, 4], ALU.add),
         v.tensor_tensor(var, stats[:, :, 1], stats[:, :, 4], ALU.subtract),
         v.tensor_tensor(tmp, stats[:, :, 2], stats[:, :, 5], ALU.add))
    link(v.tensor_scalar(mean, mean, 0.5, None, ALU.mult),
         v.scalar_tensor_tensor(var, var, 0.25, var, ALU.mult, ALU.mult),
         v.tensor_scalar(tmp, tmp, 1.0 / D, LN_EPS, ALU.mult, ALU.add))
    link(v.tensor_tensor(var, var, tmp, ALU.add))
    link(v.tensor_scalar(magic, var.bitcast(I32), 1, None, ALU.logical_shift_right))
    link(v.tensor_scalar(rstd.bitcast(I32), magic, -1.0, 1597463007.0, ALU.mult, ALU.add))
    for _ in range(3):
        link(v.tensor_tensor(tmp, rstd, rstd, ALU.mult))
        link(v.scalar_tensor_tensor(tmp, tmp, -0.5, var, ALU.mult, ALU.mult))
        link(v.scalar_tensor_tensor(rstd, tmp, 1.5, rstd, ALU.add, ALU.mult))


NORM_LINKS = 18


class Scope:

    def __init__(self, nc, ctx, tag):
        self.nc, self.ctx, self.tag = nc, ctx, tag

    def sb(self, name, shape, dt=F32):
        return self.ctx.enter_context(self.nc.sbuf_tensor(f"{self.tag}_{name}", shape, dt))

    def ps(self, name, shape, dt=F32):
        return self.ctx.enter_context(self.nc.psum_tensor(f"{self.tag}_{name}", shape, dt))

    def sem(self, name):
        return self.ctx.enter_context(self.nc.semaphore(f"{self.tag}_{name}"))


def constants(nc, ctx, held, c):
    c["ident"] = Scope(nc, ctx, "const").sb("ident", [P, P])
    m = Scope(nc, held, "const")
    c["headmask"] = m.sb("headmask", [P, HG * UH])
    c["pick_raw"] = m.sb("pick_raw", [2 * UH, UH, P])
    c["pick"] = m.sb("pick", [2 * UH, UH, P], F32R)
    c["eidx"] = m.sb("eidx", [P, NE])
    c["tri"] = m.sb("tri", [P, P])
    c["ones"] = m.sb("ones", [P, P])
    c["iota_r"] = m.sb("iota_r", [P, P])
    c["iota_s"] = m.sb("iota_s", [P, SLOTS + 1])
    c["iota_t"] = m.sb("iota_t", [P, NT])
    c["iota_p"] = m.sb("iota_p", [P, 1])
    filled = m.sem("filled")
    with nc.Block() as block:
        @block.gpsimd
        def _(pool):
            g = nc.gpsimd
            n = 0
            for key, value in (("ident", 0.0), ("headmask", 1.0), ("pick_raw", 0.0), ("ones", 1.0), ("tri", 1.0)):
                g.memset(c[key][:], value).then_inc(filled, 1)
                n += 1
            g.iota(c["iota_r"][:], [[1, P]], base=0, channel_multiplier=0, allow_small_or_imprecise_dtypes=True).then_inc(filled, 1)
            g.iota(c["iota_s"][:], [[1, SLOTS + 1]], base=0, channel_multiplier=0, allow_small_or_imprecise_dtypes=True).then_inc(filled, 1)
            g.iota(c["iota_t"][:], [[1, NT]], base=0, channel_multiplier=0, allow_small_or_imprecise_dtypes=True).then_inc(filled, 1)
            g.iota(c["iota_p"][:], [[1, 1]], base=0, channel_multiplier=1, allow_small_or_imprecise_dtypes=True).then_inc(filled, 1)
            g.iota(c["eidx"][:], [[1, NE]], base=-NE, channel_multiplier=0, allow_small_or_imprecise_dtypes=True).then_inc(filled, 1)
            n += 5
            pool.wait_ge(filled, n)
            g.affine_select(out=c["ident"][:], in_=c["ident"][:], compare_op=ALU.not_equal, fill=1.0,
                            base=0, pattern=[[-1, P]], channel_multiplier=1).then_inc(filled, 1)
            g.affine_select(out=c["tri"][:], in_=c["tri"][:], compare_op=ALU.is_gt, fill=0.0,
                            base=0, pattern=[[1, P]], channel_multiplier=-1).then_inc(filled, 1)
            g.affine_select(out=c["headmask"][:], in_=c["headmask"][:], compare_op=ALU.is_ge, fill=0.0,
                            base=0, pattern=[[-HD, HG * UH]], channel_multiplier=1).then_inc(filled, 1)
            pick = c["pick_raw"][:]
            g.affine_select(out=pick, in_=pick, compare_op=ALU.not_equal, fill=1.0,
                            base=0, pattern=[[-1, UH], [0, P]], channel_multiplier=1).then_inc(filled, 1)
            pool.wait_ge(filled, n + 4)
            g.affine_select(out=c["headmask"][:], in_=c["headmask"][:], compare_op=ALU.is_ge, fill=0.0,
                            base=HD - 1, pattern=[[HD, HG * UH]], channel_multiplier=-1).then_inc(filled, 1)
            g.affine_select(out=pick, in_=pick, compare_op=ALU.not_equal, fill=1.0,
                            base=-UH, pattern=[[-1, UH], [0, P]], channel_multiplier=1).then_inc(filled, 1)
            pool.wait_ge(filled, n + 6)
            g.tensor_copy(c["pick"][:], pick).then_inc(filled, 1)
            pool.wait_ge(filled, n + 7)


def dilated_attention(nc, c, x_dram, x1, stats):
    LS, LM, LA, LO = 2, 3, 4, 5
    OW = UH * (HD + 1)
    ctx = ExitStack()
    m = Scope(nc, ctx, "att")
    with ctx:
        xe = [m.sb(f"xe{i}", [P, D]) for i in range(2)]
        xaug = [m.sb(f"xaug{i}", [P, NH, HD + 1]) for i in range(2)]
        xT = [m.sb(f"xT{i}", [P, KD, P]) for i in range(2)]
        xm = [m.sb(f"xm{i}", [P, UH, P]) for i in range(UPS)]
        prob = [m.sb(f"prob{i}", [P, UH, P]) for i in range(UPS)]
        mx = [m.sb(f"mx{i}", [P, UH]) for i in range(UPS)]
        negmax = [m.sb(f"negmax{i}", [P, 2 * UH], F32R) for i in range(UPS)]
        shift = [m.sb(f"shift{i}", [2 * UH, P], F32R) for i in range(UPS)]
        rden = [m.sb(f"rden{i}", [P, UH]) for i in range(UPS)]
        heads = [m.sb(f"heads{i}", [P, D]) for i in range(2)]
        small = [m.sb(f"small{i}", [P, 4]) for i in range(2)]
        psS = [m.ps(f"psS{i}", [P, UH, P]) for i in range(UPS)]
        psT = m.ps("psT", [P, KD, P])
        psM = m.ps("psM", [2 * UH, P])
        psO = [m.ps(f"psO{i}", [P, 512]) for i in range(2)]
        loaded, aug_ready, xT_raw, xT_ready, xm_ready = (m.sem(s) for s in ("loaded", "aug_ready", "xT_raw", "xT_ready", "xm_ready"))
        scored, max_ready, hi_ready, negmax_ready, max_turned, shift_ready, shifted, prob_ready, out_raw, rden_ready, heads_ready, fin = (
            m.sem(s) for s in ("scored", "max_ready", "hi_ready", "negmax_ready", "max_turned", "shift_ready", "shifted",
                               "prob_ready", "out_raw", "rden_ready", "heads_ready", "fin"))
        ones_set = m.sem("ones_set")
        even_loaded = [m.sem(f"even_loaded{i}") for i in range(2)]
        block = ctx.enter_context(nc.Block())

        @block.sync
        def _(sp):
            src = x_dram.rearrange("b (g p w) d -> p (b g) (w d)", p=P, w=2)
            dst = x1[:].rearrange("p (g w) d -> p g (w d)", w=2)

            def load(i, segs):
                wait(sp, loaded, i * 16)
                sp.dma_start(dst[:, bass.ds(segs[0], 2), :], src[:, bass.ds(segs[0], 2), :]).then_inc(loaded, 16)
                for q in range(2):
                    if not isinstance(i, int):
                        sp.wait_ge(xT_raw, i * 2 + (q - 1))
                    sp.dma_start(xe[q][:], src[:, bass.ds(segs[q], 1), 0:D].rearrange("p a d -> p (a d)")).then_inc(even_loaded[q], 16)

            load(0, (0, 1))
            with sp.Fori(1, NSEG // 2) as i:
                load(i, (sp.snap(i * 2), sp.snap(i * 2 + 1)))

        @block.gpsimd
        def _(pool):
            def masks(i):
                for k in range(2 * UPS):
                    q, g = divmod(k, UPS)
                    half, part = divmod(g, HG)
                    if g == 0:
                        wait(pool, xT_ready, i * 2 + (q + 1))
                    wait(pool, scored, i * 8 + (k - UPS + 1))
                    nc.gpsimd.tensor_tensor(
                        xm[g][:], xT[q][:, half, :].unsqueeze(1).to_broadcast([P, UH, P]),
                        c["headmask"][:, part * UH:(part + 1) * UH].unsqueeze(2).to_broadcast([P, UH, P]),
                        ALU.mult).then_inc(xm_ready, 1)

            masks(0)
            with pool.Fori(1, NSEG // 2) as i:
                masks(i)

        @block.tensor
        def _(pe):
            def step(i, k, fresh=False, draining=False):
                def unit(lag):
                    j = stages(k, lag, 8, fresh, draining)
                    return (None, 0, 0) if j is None else (i * 8 + j, (j % 8) // UPS, j % UPS)

                u, q, g = unit(LS)
                if u is not None:
                    wait(pe, xm_ready, u + 1)
                    wait(pe, prob_ready, u - (UPS - 1))
                    nc.tensor.matmul(psS[g][:].rearrange("p a b -> p (a b)"), xT[q][:, g // HG, :],
                                     xm[g][:].rearrange("p a b -> p (a b)"), start=True, stop=True).then_inc(scored, 1)
                u, q, g = unit(LM)
                if u is not None:
                    wait(pe, negmax_ready, u + 1)
                    wait(pe, shift_ready, u)
                    nc.tensor.transpose(psM[:], negmax[g][:].bitcast(F32), c["ident"][:]).then_inc(max_turned, 1)
                u, q, g = unit(LA)
                if u is not None:
                    wait(pe, shift_ready, u + 1)
                    for j in range(UH):
                        last = nc.tensor.matmul(psS[g][:, j, :], c["pick"][:, j, :], shift[g][:], start=False, stop=True,
                                                skip_group_check=True)
                    last.then_inc(shifted, 1)
                u, q, g = unit(LO)
                if u is not None:
                    wait(pe, prob_ready, u + 1)
                    if g == 0:
                        wait(pe, aug_ready, i * 2 + (k - LO) // UPS + 1)
                    wait(pe, heads_ready, u - 1)
                    for j in range(UH):
                        last = nc.tensor.matmul(psO[g % 2][:, j * OW:(j + 1) * OW], prob[g][:, j, :],
                                                xaug[q][:, g * UH:(g + 1) * UH, :].rearrange("p h d -> p (h d)"),
                                                start=True, stop=True)
                    last.then_inc(out_raw, 1)
                if k % UPS == 0 and not draining:
                    q = k // UPS
                    seg = i * 2 + q
                    wait(pe, even_loaded[q], i * 16 + 16)
                    wait(pe, xT_ready, seg)
                    for half in range(KD):
                        last = nc.tensor.transpose(psT[:, half, :], xe[q][:, half * P:(half + 1) * P], c["ident"][:])
                    last.then_inc(xT_raw, 1)

            for k in range(8):
                step(0, k, fresh=True)
            with pe.Fori(1, NSEG // 2) as i:
                for k in range(8):
                    step(i, k)
            for k in range(LO):
                step(NSEG // 2, k, draining=True)

        @block.scalar
        def _(act):
            act.wait_ge(ones_set, 2)

            def step(i, k, fresh=False, draining=False):
                j = stages(k, LA, 8, fresh, draining)
                if j is not None:
                    u, g = i * 8 + j, j % UPS
                    wait(act, shifted, u + 1)
                    wait(act, out_raw, u - (UPS - 1))
                    nc.scalar.activation(prob[g][:], psS[g][:], ACT.Exp, scale=HD ** -0.5).then_inc(prob_ready, 1)
                q = k // UPS
                seg = i * 2 + q
                if k % UPS == LO - UPS and not draining:
                    act.wait_ge(loaded, i * 16 + 16)
                    wait(act, out_raw, (seg - 1) * UPS)
                    nc.scalar.activation(xaug[q][:, :, 0:HD],
                                         x1[:, bass.ds(seg * 2, 1), :].rearrange("p a (h d) -> p (a h) d", d=HD),
                                         ACT.Copy).then_inc(aug_ready, 1)
                if k % UPS == 0 and not draining:
                    wait(act, xT_raw, seg + 1)
                    wait(act, scored, (seg - 1) * UPS + 1)
                    nc.scalar.activation(xT[q][:], psT[:], ACT.Copy).then_inc(xT_ready, 1)

            for k in range(8):
                step(0, k, fresh=True)
            with act.Fori(1, NSEG // 2) as i:
                for k in range(8):
                    step(i, k)
            for k in range(LA):
                step(NSEG // 2, k, draining=True)

        @block.vector
        def _(dve):
            for q in range(2):
                nc.vector.memset(xaug[q][:, :, HD:HD + 1], 1.0).then_inc(ones_set, 1)

            def finish(seg, q):
                row = x1[:, bass.ds(seg * 2, 1), :].rearrange("p a d -> p (a d)")
                den, rec, alpha = (small[q][:, n:n + 1] for n in range(3))
                wait(dve, heads_ready, seg * UPS + UPS)
                nc.vector.tensor_reduce(den, heads[q][:], X, ALU.add).then_inc(fin, 1)
                wait(dve, fin, seg * 4 + 1)
                nc.vector.reciprocal(rec, den).then_inc(fin, 1)
                wait(dve, fin, seg * 4 + 2)
                nc.vector.tensor_tensor(alpha, den, rec, ALU.mult).then_inc(fin, 1)
                wait(dve, fin, seg * 4 + 3)
                nc.vector.scalar_tensor_tensor(row, heads[q][:], alpha, row, ALU.mult, ALU.add).then_inc(fin, 1)

            def row_stats(seg, w):
                nc.vector.bn_stats(stats[:, bass.ds(seg * 2 + w, 1), :].rearrange("p a d -> p (a d)"),
                                   x1[:, bass.ds(seg * 2 + w, 1), :].rearrange("p a d -> p (a d)"))

            def step(i, k, fresh=False, draining=False):
                def unit(lag):
                    j = stages(k, lag, 8, fresh, draining)
                    return (None, 0, 0) if j is None else (i * 8 + j, (j % 8) // UPS, j % UPS)

                u, q, g = unit(LS)
                done = (k - 1 - LO) // UPS if (k - 1 - LO) % UPS == UPS - 1 and (k > LO or not fresh) else None
                if u is not None:
                    if done is not None:
                        wait(dve, fin, (i * 2 + done) * 4 + 4)
                    wait(dve, scored, u + 1)
                    wait(dve, max_turned, u - (UPS - 1))
                    nc.vector.tensor_reduce(mx[g][:], psS[g][:], X, ALU.max).then_inc(max_ready, 1)
                    if done is not None:
                        row_stats(i * 2 + done, 0)
                        row_stats(i * 2 + done, 1)
                    wait(dve, max_ready, u + 1)
                    nc.vector.tensor_scalar(negmax[g][:, 0:UH], mx[g][:], -1.0, None, ALU.mult).then_inc(hi_ready, 1)
                    wait(dve, hi_ready, u + 1)
                    nc.vector.scalar_tensor_tensor(negmax[g][:, UH:2 * UH], mx[g][:], -1.0, negmax[g][:, 0:UH].bitcast(F32),
                                                   ALU.mult, ALU.subtract).then_inc(negmax_ready, 1)
                u, q, g = unit(LM)
                if u is not None:
                    wait(dve, max_turned, u + 1)
                    wait(dve, shifted, u - (UPS - 1))
                    nc.vector.tensor_copy(shift[g][:], psM[:]).then_inc(shift_ready, 1)
                u, q, g = unit(LO)
                if u is not None:
                    wait(dve, out_raw, u + 1)
                    o = psO[g % 2][:, 0:UH * (OW + HD + 1)].rearrange("p (h d) -> p h d", h=UH)
                    nc.vector.reciprocal(rden[g][:].unsqueeze(2), o[:, :, HD:HD + 1]).then_inc(rden_ready, 1)
                    wait(dve, rden_ready, u + 1)
                    nc.vector.tensor_tensor(heads[q][:, g * UH * HD:(g + 1) * UH * HD].rearrange("p (h d) -> p h d", h=UH),
                                            o[:, :, 0:HD], rden[g][:].unsqueeze(2).to_broadcast([P, UH, HD]),
                                            ALU.mult).then_inc(heads_ready, 1)
                    if g == UPS - 1:
                        finish(i * 2 + (k - LO) // UPS, q)

            for k in range(8):
                step(0, k, fresh=True)
            with dve.Fori(1, NSEG // 2) as i:
                for k in range(8):
                    step(i, k)
            for k in range(LO):
                step(NSEG // 2, k, draining=True)
            dve.wait_ge(fin, NSEG * 4)
            for w in range(2):
                row_stats(NSEG - 1, w)


NCOL = SLOTS + 1


def normalise_and_route(nc, c, x1, stats, router_w, router_b, x1_dram, route, weights):
    ctx = ExitStack()
    m = Scope(nc, ctx, "route")
    XB = 3
    with ctx:
        mean = m.sb("mean", [P, NT])
        rstd = m.sb("rstd", [P, NT])
        var = m.sb("var", [P, NT])
        tmp = m.sb("tmp", [P, NT])
        magic = m.sb("magic", [P, NT], I32)
        xT = [m.sb(f"xT{i}", [P, 2, KD, P]) for i in range(XB)]
        rw = m.sb("rw", [P, KD, NE])
        rb = m.sb("rb", [P, NE])
        logit = m.sb("logit", [P, NT, NE])
        best = m.sb("best", [P, NT])
        expd = m.sb("expd", [P, NT, NE])
        cand = m.sb("cand", [P, NT, NE])
        bidx = m.sb("bidx", [P, NT])
        onehot = m.sb("onehot", [P, NT, NE])
        PADT = NT // 2
        count = [m.sb(f"count{i}", [P, PADT + NT, NE]) for i in range(2)]
        tiles = [m.sb(f"tiles{i}", [P, NE // 2 + NE]) for i in range(2)]
        nt_f = m.sb("nt_f", [P, NE])
        nt_i = m.sb("nt_i", [P, NE], I32)
        base = m.sb("base", [P, NE])
        place = m.sb("place", [P, NT])
        ptile_i = m.sb("ptile_i", [P, NT], I32)
        ptile = m.sb("ptile", [P, NT])
        prow = m.sb("prow", [P, NT])
        past = m.sb("past", [P, NCOL, NE - 1])
        sexp = m.sb("sexp", [P, NCOL])
        rows1 = m.sb("rows1", [P, NT, P], BF16)
        slots1 = m.sb("slots1", [P, NT, NCOL])
        ids = m.sb("ids", [P, NT, 2 * NCOL], BF16)
        psX = [m.ps(f"psX{i}", [P, 2, KD, P]) for i in range(XB)]
        psR = m.ps("psR", [P, NT, NE])
        psA = m.ps("psA", [P, NT, NE])
        psB = m.ps("psB", [P, NT, NE])
        psI = m.ps("psI", [P, 2 * NCOL])
        (w_loaded, chain, kept, turned, xT_ready, routed, diff_ready, exp_ready,
         onehot_ready, counted, tables_ready, gathered, stored) = (m.sem(s) for s in (
             "w_loaded", "chain", "kept", "turned", "xT_ready", "routed", "diff_ready",
             "exp_ready", "onehot_ready", "counted", "tables_ready", "gathered", "stored"))
        block = ctx.enter_context(nc.Block())

        @block.sync
        def _(sp):
            sp.dma_start(rw[:], router_w.rearrange("(k p) e -> p k e", p=P)).then_inc(w_loaded, 16)
            sp.dma_start(rb[:], router_b.partition_broadcast(P)).then_inc(w_loaded, 16)
            weights.load(sp, 0)
            for b in range(B):
                sp.wait_ge(kept, (b + 1) * TB)
                sp.dma_start(x1_dram.rearrange("(t p) d -> p t d", p=P)[:, b * TB:(b + 1) * TB, :],
                             x1[:, b * TB:(b + 1) * TB, :]).then_inc(stored, 16)
            sp.wait_ge(stored, 16 * B)

        @block.gpsimd
        def _(pool):
            weights.divide(pool, 0)

        @block.tensor
        def _(pe):
            def turn(i):
                wait(pe, kept, i * 2 + 2)
                wait(pe, xT_ready, i - XB + 1)
                for a in range(2):
                    for k in range(KD):
                        last = nc.tensor.transpose(psX[i % XB][:, a, k, :], x1[:, 2 * i + a, k * P:(k + 1) * P], c["ident"][:])
                last.then_inc(turned, 1)

            def score(i):
                wait(pe, xT_ready, i + 1)
                for a in range(2):
                    for k in range(KD):
                        last = nc.tensor.matmul(psR[:, 2 * i + a, :], xT[i % XB][:, a, k, :], rw[:, k, :], start=k == 0, stop=k == KD - 1)
                last.then_inc(routed, 1)

            pe.wait_ge(w_loaded, 32)
            for i in range(NT // 2):
                turn(i)
                if i > 0:
                    score(i - 1)
            score(NT // 2 - 1)
            pe.wait_ge(onehot_ready, 1)
            nc.tensor.matmul(psA[:].rearrange("p t e -> p (t e)"), c["tri"][:], onehot[:].rearrange("p t e -> p (t e)"),
                             start=True, stop=True).then_inc(counted, 1)
            nc.tensor.matmul(psB[:].rearrange("p t e -> p (t e)"), c["ones"][:], onehot[:].rearrange("p t e -> p (t e)"),
                             start=True, stop=True).then_inc(counted, 1)
            pe.wait_ge(tables_ready, 3)
            for t in range(NT):
                last = nc.tensor.matmul(psI[:], rows1[:, t, :], ids[:, t, :], start=t == 0, stop=t == NT - 1)
            last.then_inc(gathered, 1)

        @block.scalar
        def _(act):
            for i in range(NT // 2):
                act.wait_ge(turned, i + 1)
                wait(act, routed, i - XB + 1)
                nc.scalar.activation(xT[i % XB][:], psX[i % XB][:], ACT.Copy).then_inc(xT_ready, 1)
            act.wait_ge(diff_ready, 1)
            nc.scalar.activation(expd[:], expd[:], ACT.Exp).then_inc(exp_ready, 1)

        @block.vector
        def _(dve):
            v = nc.vector
            n = [0]

            def link(*steps):
                n[0] += len(steps)
                for ins in steps:
                    ins.then_inc(chain, 1)
                dve.wait_ge(chain, n[0])

            norm_steps(v, link, stats[:], mean[:], rstd[:], var[:], tmp[:], magic[:])

            for t in range(NT):
                v.tensor_scalar(x1[:, t, :], x1[:, t, :], mean[:, t:t + 1], rstd[:, t:t + 1], ALU.subtract, ALU.mult).then_inc(kept, 1)
            dve.wait_ge(w_loaded, 32)
            dve.wait_ge(routed, NT // 2)
            link(v.tensor_tensor(logit[:], psR[:], rb[:].unsqueeze(1).to_broadcast([P, NT, NE]), ALU.add))
            link(v.tensor_reduce(best[:], logit[:], X, ALU.max))
            bc = lambda ap: ap.unsqueeze(2).to_broadcast([P, NT, NE])
            over_t = lambda ap: ap.unsqueeze(1).to_broadcast([P, NT, NE])
            v.tensor_tensor(expd[:], logit[:], bc(best[:]), ALU.subtract).then_inc(diff_ready, 1)
            dve.wait_ge(diff_ready, 1)
            link(v.tensor_tensor(cand[:], logit[:], bc(best[:]), ALU.is_ge))
            link(v.tensor_tensor(cand[:], cand[:], over_t(c["eidx"][:]), ALU.mult))
            link(v.tensor_reduce(bidx[:], cand[:], X, ALU.min))
            v.tensor_tensor(onehot[:], bc(bidx[:]), over_t(c["eidx"][:]), ALU.is_equal).then_inc(onehot_ready, 1)
            dve.wait_ge(exp_ready, 1)
            link(v.tensor_reduce(tmp[:], expd[:], X, ALU.add))
            v.reciprocal(route["prob"][:], tmp[:])
            for i in range(2):
                link(v.memset(count[i][:, 0:PADT, :], 0.0))
                link(v.memset(tiles[i][:, 0:NE // 2], 0.0))
            dve.wait_ge(counted, 2)
            link(v.tensor_copy(count[0][:, PADT:, :], psB[:]))
            a, shift = 0, 1
            while shift < NT:
                link(v.tensor_tensor(count[1 - a][:, PADT:, :], count[a][:, PADT:, :],
                                     count[a][:, PADT - shift:PADT + NT - shift, :], ALU.add))
                a, shift = 1 - a, 2 * shift
            total = count[a][:, PADT + NT - 1, :]
            link(v.tensor_scalar(nt_i[:], total, float(P - 1), None, ALU.add))
            link(v.tensor_scalar(nt_i[:], nt_i[:], 7, None, ALU.logical_shift_right))
            link(v.tensor_scalar(nt_f[:], nt_i[:], 1.0, None, ALU.max))
            half = NE // 2
            link(v.tensor_copy(tiles[0][:, half:], nt_f[:]))
            e, shift = 0, 1
            while shift < NE:
                link(v.tensor_tensor(tiles[1 - e][:, half:], tiles[e][:, half:], tiles[e][:, half - shift:half + NE - shift], ALU.add))
                e, shift = 1 - e, 2 * shift
            ends = tiles[e][:, half:]
            link(v.tensor_copy(route["ends"][:], ends))
            link(v.tensor_tensor(base[:], ends, nt_f[:], ALU.subtract))
            link(v.tensor_scalar(base[:], base[:], float(P), None, ALU.mult))
            run = count[1 - a][:, PADT:, :]
            link(v.tensor_tensor(run, count[a][:, PADT:, :], psB[:], ALU.subtract))
            link(v.tensor_tensor(run, run, psA[:], ALU.add))
            link(v.tensor_tensor(run, run, over_t(base[:]), ALU.add))
            link(v.tensor_tensor(run, run, onehot[:], ALU.mult))
            link(v.tensor_reduce(place[:], run, X, ALU.add))
            link(v.tensor_copy(route["place"][:], place[:]))
            link(v.tensor_scalar(ptile_i[:], route["place"][:], 7, None, ALU.logical_shift_right))
            link(v.tensor_copy(ptile[:], ptile_i[:]))
            link(v.scalar_tensor_tensor(prow[:], ptile[:], -float(P), place[:], ALU.mult, ALU.add))
            v.tensor_tensor(rows1[:], prow[:].unsqueeze(2).to_broadcast([P, NT, P]),
                            c["iota_r"][:].unsqueeze(1).to_broadcast([P, NT, P]), ALU.is_equal).then_inc(tables_ready, 1)
            link(v.tensor_tensor(slots1[:], ptile[:].unsqueeze(2).to_broadcast([P, NT, NCOL]),
                                 c["iota_s"][:].unsqueeze(1).to_broadcast([P, NT, NCOL]), ALU.is_equal))
            v.tensor_scalar(ids[:, :, 0:NCOL], slots1[:], c["iota_p"][:], None, ALU.mult).then_inc(tables_ready, 1)
            v.tensor_tensor(ids[:, :, NCOL:], slots1[:], c["iota_t"][:].unsqueeze(2).to_broadcast([P, NT, NCOL]),
                            ALU.mult).then_inc(tables_ready, 1)
            link(v.tensor_tensor(past[:], c["iota_s"][:].unsqueeze(2).to_broadcast([P, NCOL, NE - 1]),
                                 ends[:, 0:NE - 1].unsqueeze(1).to_broadcast([P, NCOL, NE - 1]), ALU.is_ge))
            link(v.tensor_reduce(sexp[:], past[:], X, ALU.add))
            link(v.tensor_copy(route["expert"][:], sexp[:]))
            link(v.tensor_scalar(route["buffer"][:], route["expert"][:], 1, None, ALU.bitwise_and))
            dve.wait_ge(gathered, 1)
            link(v.tensor_copy(slots1[:, 0, :], psI[:, 0:NCOL]))
            link(v.scalar_tensor_tensor(route["token"][:], psI[:, NCOL:], float(P), slots1[:, 0, :], ALU.mult, ALU.add))


def routing_tables(nc, ctx):
    m = Scope(nc, ctx, "table")
    return {"prob": m.sb("prob", [P, NT]), "place": m.sb("place", [P, NT], I32), "ends": m.sb("ends", [P, NE], I32),
            "expert": m.sb("expert", [P, NCOL], I32), "buffer": m.sb("buffer", [P, NCOL], I32),
            "token": m.sb("token", [P, NCOL], I32)}


NB = 512
FK = FF // P


class Weights:

    def __init__(self, nc, ctx, w1_dram, w2_dram):
        m = Scope(nc, ctx, "w")
        self.nc, self.w1_dram, self.w2_dram = nc, w1_dram, w2_dram
        self.raw1 = m.sb("raw1", [P, KD, 2 * FF])
        self.raw2 = m.sb("raw2", [P, FK, D])
        self.hi1 = m.sb("hi1", [P, 2, KD * 2 * FF], F32R)
        self.lo1 = m.sb("lo1", [P, 2, KD * 2 * FF], F32R)
        self.hi2 = m.sb("hi2", [P, 2, FK * D], F32R)
        self.lo2 = m.sb("lo2", [P, 2, FK * D], F32R)
        self.zero = m.sb("zero", [P, 1])
        self.loaded1, self.loaded2, self.zeroed = m.sem("loaded1"), m.sem("loaded2"), m.sem("zeroed")
        self.split = m.sem("split")

    def load(self, sp, e):
        wait(sp, self.split, 4 * e)
        sp.dma_start(self.raw1[:], self.w1_dram[e].rearrange("(k p) f -> p k f", p=P)).then_inc(self.loaded1, 16)
        sp.dma_start(self.raw2[:], self.w2_dram[e].rearrange("(k p) d -> p k d", p=P)).then_inc(self.loaded2, 16)

    def divide(self, pool, e):
        g, n = self.nc.gpsimd, 4 * e
        if e == 0:
            g.memset(self.zero[:], 0.0).then_inc(self.zeroed, 1)
            pool.wait_ge(self.zeroed, 1)
        for loaded, raw, hi, lo in ((self.loaded1, self.raw1, self.hi1, self.lo1), (self.loaded2, self.raw2, self.hi2, self.lo2)):
            flat = raw[:].rearrange("p k f -> p (k f)")
            pool.wait_ge(loaded, 16 * (e + 1))
            g.tensor_tensor(hi[:, e % 2, :], flat, self.zero[:].to_broadcast([P, flat.shape[1]]), ALU.add).then_inc(self.split, 1)
            pool.wait_ge(self.split, n + 1)
            g.tensor_tensor(lo[:, e % 2, :], flat, hi[:, e % 2, :].bitcast(F32), ALU.subtract).then_inc(self.split, 1)
            n += 2


def experts(nc, c, w, route, x1_dram, ys_dram):
    ctx = ExitStack()
    m = Scope(nc, ctx, "moe")
    FIRST = 8
    with ctx:
        xg = m.sb("xg", [P, NCOL, D])
        xs = m.sb("xs", [P, D])
        xh = m.sb("xh", [P, KD, P], F32R)
        xl = m.sb("xl", [P, KD, P], F32R)
        act_a = m.sb("act_a", [P, FF])
        hs = m.sb("hs", [P, FF])
        hh = m.sb("hh", [P, FK, P], F32R)
        hl = m.sb("hl", [P, FK, P], F32R)
        yo = [m.sb(f"yo{i}", [P, D]) for i in range(2)]
        psH = m.ps("psH", [P, 4, NB])
        psHT = m.ps("psHT", [P, FK, P])
        psX = m.ps("psX", [P, NB])
        psY = m.ps("psY", [P, NB])
        psXv = psX[:, 0:KD * P].rearrange("p (k t) -> p k t", k=KD)
        (xs_ready, x_turned, xh_ready, xl_ready, a_ready, g_ready, silu_ready, hs_ready, h_turned, hh_ready,
         hl_ready, y_raw, yo_ready) = (m.sem(s) for s in (
             "xs_ready", "x_turned", "xh_ready", "xl_ready", "a_ready", "g_ready", "silu_ready", "hs_ready",
             "h_turned", "hh_ready", "hl_ready", "y_raw", "yo_ready"))
        gathered = [m.sem(f"gathered{i}") for i in range(4)]
        stored = [m.sem(f"stored{i}") for i in range(2)]
        block = ctx.enter_context(nc.Block())

        def tiles(eng, step):
            for t in range(4):
                step(t, t % 4)
            with eng.Fori(1, SLOTS // 4) as i:
                for q in range(4):
                    step(i * 4 + q, q)
            for t in range(SLOTS // 4 * 4, SLOTS + 2):
                step(t, t % 4)

        def before(t, q, n):
            return (t - q) * (16 // n)

        ys_tiles = ys_dram.rearrange("(t p) d -> t p d", p=P)

        def live(t):
            return not isinstance(t, int) or 0 <= t < SLOTS

        @block.sync
        def _(sp):
            for e in range(1, NE):
                w.load(sp, e)

        @block.gpsimd
        def _(pool):
            def gather(slot):
                q = slot % 4
                wait(pool, gathered[q], 16 * (slot // 4))
                nc.gpsimd.indirect_dma_start(xg[:, slot, :], None, x1_dram,
                                             bass.IndirectOffsetOnAxis(route["token"][:, slot:slot + 1], 0)).then_inc(gathered[q], 16)

            for slot in range(FIRST):
                gather(slot)
            w.divide(pool, 1)
            for slot in range(FIRST, SLOTS):
                gather(slot)
            for e in range(2, NE):
                w_free = pool.value_load(route["ends"][0:1, e - 2:e - 1], min_val=1, max_val=SLOTS)
                pool.wait_ge(yo_ready, w_free)
                w.divide(pool, e)

        @block.tensor
        def _(pe):
            def buffer_of(t):
                return pe.value_load(route["buffer"][0:1, bass.ds(t, 1)], min_val=0, max_val=1)

            def step(s, q):
                t = s - 1
                if live(t):
                    e = pe.value_load(route["expert"][0:1, bass.ds(t, 1)], min_val=0, max_val=NE - 1)
                    b = buffer_of(t)
                    pe.wait_ge(xl_ready, t + 1)
                    pe.wait_ge(w.split, e * 4 + 4)
                    wait(pe, silu_ready, t)
                    for n in range(4):
                        if n == 2:
                            wait(pe, hs_ready, t)
                        first = True
                        for k in range(KD):
                            cols = slice(k * 2 * FF + n * NB, k * 2 * FF + (n + 1) * NB)
                            for xpart, wpart in ((xh, w.hi1), (xh, w.lo1), (xl, w.hi1)):
                                last = nc.tensor.matmul(psH[:, n, :], xpart[:, k, :],
                                                        wpart[:, bass.ds(b, 1), cols].rearrange("p a f -> p (a f)"),
                                                        start=first, stop=k == KD - 1 and xpart is xl)
                                first = False
                        if n == 1:
                            last.then_inc(a_ready, 1)
                    last.then_inc(g_ready, 1)
                t = s
                if live(t):
                    pe.wait_ge(xs_ready, t + 1)
                    wait(pe, xl_ready, t)
                    for k in range(KD):
                        last = nc.tensor.transpose(psXv[:, k, :], xs[:, k * P:(k + 1) * P], c["ident"][:])
                    last.then_inc(x_turned, 1)
                t = s - 2
                if live(t):
                    b = buffer_of(t)
                    pe.wait_ge(hl_ready, t + 1)
                    wait(pe, yo_ready, t)
                    first = True
                    for k in range(FK):
                        for hpart, wpart in ((hh, w.hi2), (hh, w.lo2), (hl, w.hi2)):
                            last = nc.tensor.matmul(psY[:, 0:D], hpart[:, k, :],
                                                    wpart[:, bass.ds(b, 1), k * D:(k + 1) * D].rearrange("p a f -> p (a f)"),
                                                    start=first, stop=k == FK - 1 and hpart is hl)
                            first = False
                    last.then_inc(y_raw, 1)
                t = s - 1
                if live(t):
                    pe.wait_ge(hs_ready, t + 1)
                    wait(pe, hl_ready, t)
                    for k in range(FK):
                        last = nc.tensor.transpose(psHT[:, k, :], hs[:, k * P:(k + 1) * P], c["ident"][:])
                    last.then_inc(h_turned, 1)

            tiles(pe, step)

        @block.scalar
        def _(act):
            def step(s, q):
                t = s - 3
                if live(t):
                    act.wait_ge(yo_ready, t + 1)
                    act.dma_start(ys_tiles[bass.ds(t, 1), :, :].rearrange("a p d -> (a p) d"), yo[1 - q % 2][:]).then_inc(stored[1 - q % 2], 16)
                t = s - 1
                if live(t):
                    act.wait_ge(a_ready, t + 1)
                    wait(act, hs_ready, t)
                    nc.scalar.activation(act_a[:], psH[:, 0:2, :].rearrange("p a b -> p (a b)"), ACT.Silu).then_inc(silu_ready, 1)
                t = s
                if live(t):
                    act.wait_ge(x_turned, t + 1)
                    wait(act, g_ready, t)
                    nc.scalar.activation(xh[:], psXv, ACT.Copy).then_inc(xh_ready, 1)
                t = s - 2
                if live(t):
                    act.wait_ge(y_raw, t + 1)
                    wait(act, stored[q % 2], before(t, q % 2, 2))
                    nc.scalar.activation(yo[q % 2][:], psY[:, 0:D], ACT.Copy).then_inc(yo_ready, 1)
                t = s - 1
                if live(t):
                    act.wait_ge(h_turned, t + 1)
                    wait(act, y_raw, t)
                    nc.scalar.activation(hh[:], psHT[:], ACT.Copy).then_inc(hh_ready, 1)

            tiles(act, step)
            act.wait_ge(yo_ready, SLOTS)
            act.dma_start(ys_tiles[SLOTS - 1], yo[(SLOTS - 1) % 2][:]).then_inc(stored[(SLOTS - 1) % 2], 16)
            act.wait_ge(stored[0], before(SLOTS + 1, 0, 2))
            act.wait_ge(stored[1], before(SLOTS, 1, 2))

        @block.vector
        def _(dve):
            v = nc.vector

            def step(s, q):
                t = s
                if live(t):
                    dve.wait_ge(gathered[q], before(t, q, 4) + 16)
                    wait(dve, x_turned, t)
                    v.tensor_copy(xs[:], xg[:, bass.ds(t, 1), :].rearrange("p a d -> p (a d)")).then_inc(xs_ready, 1)
                t = s - 1
                if live(t):
                    dve.wait_ge(silu_ready, t + 1)
                    dve.wait_ge(g_ready, t + 1)
                    wait(dve, h_turned, t)
                    v.tensor_tensor(hs[:], psH[:, 2:4, :].rearrange("p a b -> p (a b)"), act_a[:], ALU.mult).then_inc(hs_ready, 1)
                t = s
                if live(t):
                    dve.wait_ge(xh_ready, t + 1)
                    v.tensor_tensor(xl[:], psXv, xh[:].bitcast(F32), ALU.subtract).then_inc(xl_ready, 1)
                t = s - 1
                if live(t):
                    dve.wait_ge(hh_ready, t + 1)
                    v.tensor_tensor(hl[:], psHT[:], hh[:].bitcast(F32), ALU.subtract).then_inc(hl_ready, 1)

            tiles(dve, step)


EPS = 1e-6


def linear_attention(nc, c, route, x1_dram, ys_dram, w_dram, x):
    ctx = ExitStack()
    m = Scope(nc, ctx, "lin")
    with ctx:
        yg = m.sb("yg", [P, NT, D])
        xb = m.sb("xb", [P, TB, D])
        xh = m.sb("xh", [P, KD, TB, P], F32R)
        xl = m.sb("xl", [P, KD, TB, P], F32R)
        w_raw = m.sb("w_raw", [P, KD, 3 * D])
        wh = m.sb("wh", [P, KD, 3 * D], F32R)
        wl = m.sb("wl", [P, KD, 3 * D], F32R)
        qT = m.sb("qT", [P, KD, TB * P])
        qe = [m.sb(f"qe{i}", [P, NB]) for i in range(3)]
        qr = [m.sb(f"qr{i}", [P, NB]) for i in range(3)]
        ke = [m.sb(f"ke{i}", [P, D]) for i in range(3)]
        kr = [m.sb(f"kr{i}", [P, D]) for i in range(3)]
        kk = [m.sb(f"kk{i}", [P, D]) for i in range(3)]
        v1 = [m.sb(f"v1{i}", [P, D + 1]) for i in range(3)]
        kv = m.sb("kv", [P, KD, D + 1])
        z = [m.sb(f"z{i}", [P, 2]) for i in range(2)]
        xo = m.sb("xo", [P, TB, D])
        stats = [m.sb(f"stats{i}", [P, TB, 6]) for i in range(2)]
        mean, var, rstd, tmp = (m.sb(s, [P, TB]) for s in ("mean", "var", "rstd", "tmp"))
        magic = m.sb("magic", [P, TB], I32)
        psW = [m.ps(f"psW{i}", [P, NB]) for i in range(2)]
        psK = [m.ps(f"psK{i}", [P, 2 * D]) for i in range(2)]
        psC = [m.ps(f"psC{i}", [P, NB]) for i in range(KD)]
        psO = [m.ps(f"psO{i}", [P, NB]) for i in range(2)]
        names = ("w_loaded", "w_split", "summed", "turned", "xh_ready", "xl_ready", "q_raw", "q_read", "q_ready",
                 "k_raw", "kv_read", "k_ready", "added", "kv_ready", "o_raw", "z_ready", "o_ready", "ones_set",
                 "stat_in", "stat_out", "normed", "chain")
        (w_loaded, w_split, summed, turned, xh_ready, xl_ready, q_raw, q_read, q_ready,
         k_raw, kv_read, k_ready, added, kv_ready, o_raw, z_ready, o_ready, ones_set,
         stat_in, stat_out, normed, chain) = (m.sem(s) for s in names)
        x_loaded = [m.sem(f"x_loaded{i}") for i in range(B)]
        gathered = [m.sem(f"gathered{i}") for i in range(B)]
        block = ctx.enter_context(nc.Block())
        NQ = KD * 2

        def turned_view(t):
            return psW[t % 2][:, 0:KD * P].rearrange("p (k t) -> p k t", k=KD)

        @block.sync
        def _(sp):
            rows = x1_dram.rearrange("(t p) d -> p t d", p=P)
            for b in range(B):
                if b == 1:
                    sp.wait_ge(gathered[0], 16 * TB)
                sp.dma_start(x[:, b * TB:(b + 1) * TB, :], rows[:, b * TB:(b + 1) * TB, :]).then_inc(x_loaded[b], 16)
                if b == 0:
                    sp.dma_start(w_raw[:], w_dram.rearrange("(k p) f -> p k f", p=P)).then_inc(w_loaded, 16)

        @block.gpsimd
        def _(pool):
            for t in range(NT):
                nc.gpsimd.indirect_dma_start(yg[:, t, :], None, ys_dram,
                                             bass.IndirectOffsetOnAxis(route["place"][:, t:t + 1], 0)).then_inc(gathered[t // TB], 16)

        @block.tensor
        def _(pe):
            def turn(s, j):
                t = s * TB + j
                wait(pe, normed, t + 1)
                wait(pe, q_read, 2 * s * NQ)
                wait(pe, xl_ready, t - 1)
                for k in range(KD):
                    last = nc.tensor.transpose(turned_view(t)[:, k, :], x[:, t, k * P:(k + 1) * P], c["ident"][:])
                last.then_inc(turned, 1)

            def project(s):
                wait(pe, xl_ready, (s + 1) * TB)
                for n in range(NQ):
                    chunk, half = divmod(n, 2)
                    wait(pe, q_read, 2 * (s * NQ + n - 1))
                    for k in range(KD):
                        for a, (xpart, wpart) in enumerate(((xh, wh), (xh, wl), (xl, wh))):
                            last = nc.tensor.matmul(psW[n % 2][:], wpart[:, k, chunk * P:(chunk + 1) * P],
                                                    xpart[:, k, half * (TB // 2):(half + 1) * (TB // 2), :].rearrange("p j t -> p (j t)"),
                                                    start=k == 0 and a == 0, stop=k == KD - 1 and a == 2)
                    last.then_inc(q_raw, 1)
                wait(pe, kv_ready, s)

                def add_up(j):
                    t = s * TB + j
                    wait(pe, k_ready, t + 1)
                    wait(pe, kv_read, 3 * (t + 1))
                    for chunk in range(KD):
                        last = nc.tensor.matmul(psC[chunk][:, 0:D + 1], kk[t % 3][:, chunk * P:(chunk + 1) * P], v1[t % 3][:],
                                                start=j == 0, stop=j == TB - 1)
                    last.then_inc(added, 1)

                for j in range(TB):
                    t = s * TB + j
                    wait(pe, kv_read, 3 * (t - 1))
                    for k in range(KD):
                        for a, (xpart, wpart) in enumerate(((xh, wh), (xh, wl), (xl, wh))):
                            last = nc.tensor.matmul(psK[j % 2][:], xpart[:, k, j, :], wpart[:, k, D:3 * D],
                                                    start=k == 0 and a == 0, stop=k == KD - 1 and a == 2)
                    last.then_inc(k_raw, 1)
                    if j > 0:
                        add_up(j - 1)
                add_up(TB - 1)

            def attend(s, j):
                t = s * TB + j
                wait(pe, kv_ready, s + 1)
                wait(pe, q_ready, s * NQ + NQ)
                wait(pe, o_ready, t - 1)
                for chunk in range(KD):
                    last = nc.tensor.matmul(psO[t % 2][:, 0:D + 1], qT[:, chunk, j * P:(j + 1) * P], kv[:, chunk, :],
                                            start=chunk == 0, stop=chunk == KD - 1)
                last.then_inc(o_raw, 1)

            for s in range(B + 1):
                for j in range(TB):
                    if s < B:
                        turn(s, j)
                    if s > 0:
                        attend(s - 1, j)
                if s == 0:
                    pe.wait_ge(w_split, 2)
                if s < B:
                    project(s)

        @block.scalar
        def _(act):
            a_ = nc.scalar
            act.wait_ge(ones_set, 3)
            for s in range(B):
                for j in range(TB):
                    t = s * TB + j
                    wait(act, turned, t + 1)
                    wait(act, k_raw, s * TB)
                    a_.activation(xh[:, :, j, :], turned_view(t), ACT.Copy).then_inc(xh_ready, 1)
                for n in range(NQ):
                    g = s * NQ + n
                    wait(act, q_raw, g + 1)
                    wait(act, q_ready, g - 2)
                    a_.activation(qe[g % 3][:], psW[n % 2][:], ACT.Exp).then_inc(q_read, 1)
                    a_.activation(qr[g % 3][:], psW[n % 2][:], ACT.Relu).then_inc(q_read, 1)
                for j in range(TB):
                    t = s * TB + j
                    wait(act, k_raw, t + 1)
                    wait(act, k_ready, t - 2)
                    a_.activation(ke[t % 3][:], psK[j % 2][:, 0:D], ACT.Exp).then_inc(kv_read, 1)
                    a_.activation(kr[t % 3][:], psK[j % 2][:, 0:D], ACT.Relu).then_inc(kv_read, 1)
                    wait(act, added, t - 2)
                    a_.activation(v1[t % 3][:, 0:D], psK[j % 2][:, D:2 * D], ACT.Copy).then_inc(kv_read, 1)
                wait(act, added, s * TB + TB)
                wait(act, o_raw, s * TB)
                for chunk in range(KD):
                    last = a_.activation(kv[:, chunk, :], psC[chunk][:, 0:D + 1], ACT.Copy)
                last.then_inc(kv_ready, 1)

        @block.vector
        def _(dve):
            v = nc.vector
            n = [0]

            def link(*steps):
                n[0] += len(steps)
                for ins in steps:
                    ins.then_inc(chain, 1)
                dve.wait_ge(chain, n[0])

            def root(which):
                norm_steps(v, link, stats[which][:], mean[:], rstd[:], var[:], tmp[:], magic[:])

            def residual(s, j):
                t = s * TB + j
                dve.wait_ge(gathered[s], 16 * TB)
                dve.wait_ge(x_loaded[s], 16)
                v.scalar_tensor_tensor(xb[:, j, :], yg[:, t, :], route["prob"][:, t:t + 1], x[:, t, :], ALU.mult, ALU.add).then_inc(summed, 1)
                if j > 0:
                    moments(t - 1, j - 1)

            def moments(t, j):
                wait(dve, summed, t + 1)
                v.bn_stats(stats[0][:, j, :], xb[:, j, :]).then_inc(stat_in, 1)

            def norm_in(s):
                moments(s * TB + TB - 1, TB - 1)
                wait(dve, stat_in, s * TB + TB)
                root(0)
                for j in range(TB):
                    v.tensor_scalar(x[:, s * TB + j, :], xb[:, j, :], mean[:, j:j + 1], rstd[:, j:j + 1],
                                    ALU.subtract, ALU.mult).then_inc(normed, 1)

            def rest(s, j):
                t = s * TB + j
                wait(dve, xh_ready, t + 1)
                v.tensor_tensor(xl[:, :, j, :], turned_view(t), xh[:, :, j, :].bitcast(F32), ALU.subtract).then_inc(xl_ready, 1)

            def queries(s):
                wait(dve, o_raw, s * TB)
                for i in range(NQ):
                    chunk, half = divmod(i, 2)
                    g = s * NQ + i
                    wait(dve, q_read, 2 * (g + 1))
                    v.scalar_tensor_tensor(qT[:, chunk, half * NB:(half + 1) * NB], qe[g % 3][:], 1.0, qr[g % 3][:],
                                           ALU.min, ALU.add).then_inc(q_ready, 1)

            def keys(s, j):
                t = s * TB + j
                wait(dve, added, t - 2)
                wait(dve, kv_read, 3 * t + 2)
                v.scalar_tensor_tensor(kk[t % 3][:], ke[t % 3][:], 1.0, kr[t % 3][:], ALU.min, ALU.add).then_inc(k_ready, 1)

            def output(s, j):
                t = s * TB + j
                zz = z[t % 2]
                wait(dve, o_raw, t + 1)
                v.tensor_scalar(zz[:, 0:1], psO[t % 2][:, D:D + 1], EPS, None, ALU.add).then_inc(z_ready, 1)
                wait(dve, z_ready, 2 * t + 1)
                v.reciprocal(zz[:, 1:2], zz[:, 0:1]).then_inc(z_ready, 1)
                wait(dve, z_ready, 2 * t + 2)
                v.scalar_tensor_tensor(xo[:, j, :], psO[t % 2][:, 0:D], zz[:, 1:2], x[:, t, :], ALU.mult, ALU.add).then_inc(o_ready, 1)
                wait(dve, o_ready, t + 1)
                v.bn_stats(stats[1][:, j, :], xo[:, j, :]).then_inc(stat_out, 1)

            def norm_out(s):
                wait(dve, stat_out, s * TB + TB)
                root(1)
                for j in range(TB):
                    v.tensor_scalar(x[:, s * TB + j, :], xo[:, j, :], mean[:, j:j + 1], rstd[:, j:j + 1], ALU.subtract, ALU.mult)

            for i in range(3):
                v.memset(v1[i][:, D:D + 1], 1.0).then_inc(ones_set, 1)
            dve.wait_ge(w_loaded, 16)
            v.tensor_copy(wh[:], w_raw[:]).then_inc(w_split, 1)
            dve.wait_ge(w_split, 1)
            v.tensor_tensor(wl[:], w_raw[:], wh[:].bitcast(F32), ALU.subtract).then_inc(w_split, 1)
            for s in range(B + 1):
                if s > 0:
                    queries(s - 1)
                for j in range(TB):
                    if s > 0:
                        keys(s - 1, j)
                    if s < B:
                        residual(s, j)
                if s < B:
                    norm_in(s)
                for j in range(TB):
                    if s < B:
                        rest(s, j)
                    if s > 0:
                        output(s - 1, j)
                if s > 0:
                    norm_out(s - 1)


N, PS = 64, 32
NP = N * PS
BLK = 256
NBLK = NP // BLK
NPB = BLK // PS
MC = TB
CH = NP // P
MB = 4


def soft_state(nc, ctx):
    m = Scope(nc, ctx, "soft")
    return {"xh": m.sb("xh", [P, KD, NT * P], F32R), "xl": m.sb("xl", [P, KD, NT * P], F32R),
            "ph": m.sb("ph", [P, KD, NP], F32R), "pl": m.sb("pl", [P, KD, NP], F32R),
            "rowmax": m.sb("rowmax", [P, NT, NBLK])}


def turn_tokens(nc, c, st, x, phi_dram):
    ctx = ExitStack()
    m = Scope(nc, ctx, "turn")
    with ctx:
        phi = m.sb("phi", [P, KD, NP])
        psX = [m.ps(f"psX{i}", [P, 2, KD, P]) for i in range(4)]
        loaded, split, turned, hi, lo = (m.sem(s) for s in ("loaded", "split", "turned", "hi", "lo"))
        block = ctx.enter_context(nc.Block())

        @block.sync
        def _(sp):
            sp.dma_start(phi[:], phi_dram.rearrange("(k p) n s -> p k (n s)", p=P)).then_inc(loaded, 16)

        @block.gpsimd
        def _(pool):
            pool.wait_ge(split, 1)
            nc.gpsimd.tensor_tensor(st["pl"][:], phi[:], st["ph"][:].bitcast(F32), ALU.subtract)

        @block.tensor
        def _(pe):
            for g in range(NT // 2):
                wait(pe, lo, g - 3)
                for a in range(2):
                    for k in range(KD):
                        last = nc.tensor.transpose(psX[g % 4][:, a, k, :], x[:, 2 * g + a, k * P:(k + 1) * P], c["ident"][:])
                last.then_inc(turned, 1)

        def view(part, g):
            return st[part][:, :, bass.ds(g * 2 * P, 2 * P)].rearrange("p k (a t) -> p a k t", a=2)

        @block.scalar
        def _(act):
            with act.Fori(0, NT // 8) as i:
                for q in range(4):
                    act.wait_ge(turned, i * 4 + (q + 1))
                    nc.scalar.activation(view("xh", i * 4 + q), psX[q][:], ACT.Copy).then_inc(hi, 1)

        @block.vector
        def _(dve):
            dve.wait_ge(loaded, 16)
            nc.vector.tensor_copy(st["ph"][:], phi[:]).then_inc(split, 1)
            with dve.Fori(0, NT // 8) as i:
                for q in range(4):
                    dve.wait_ge(hi, i * 4 + (q + 1))
                    nc.vector.tensor_tensor(view("xl", i * 4 + q), psX[q][:], view("xh", i * 4 + q).bitcast(F32),
                                            ALU.subtract).then_inc(lo, 1)


def dispatch(nc, c, st, x, w_dram, b_dram, y_dram):
    LAG = 3
    ctx = ExitStack()
    m = Scope(nc, ctx, "disp")
    with ctx:
        e = [m.sb(f"e{i}", [P, B, BLK]) for i in range(4)]
        t2 = [m.sb(f"t2{i}", [P, 2, BLK]) for i in range(2)]
        top = [m.sb(f"top{i}", [P, BLK]) for i in range(2)]
        s2 = [m.sb(f"s2{i}", [P, 2, BLK]) for i in range(2)]
        rs = [m.sb(f"rs{i}", [P, BLK]) for i in range(2)]
        slots = m.sb("slots", [P, KD, NPB, B, PS])
        wt = m.sb("wt", [P, KD, NPB, D])
        bt = m.sb("bt", [P, NPB, D])
        yb = m.sb("yb", [P, NPB, D])
        psL = [m.ps(f"psL{i}", [P, B, BLK]) for i in range(2)]
        psS = [m.ps(f"psS{i}", [P, B, BLK]) for i in range(KD)]
        names = ("w_loaded", "b_loaded", "logits", "copied", "pair_max", "top_ready", "less", "exp_ready", "pair_sum", "sum_ready",
                 "rsum_ready", "share_ready", "gone", "slots_ready", "y_raw", "y_ready", "stored")
        (w_loaded, b_loaded, logits, copied, pair_max, top_ready, less, exp_ready, pair_sum, sum_ready,
         rsum_ready, share_ready, gone, slots_ready, y_raw, y_ready, stored) = (m.sem(s) for s in names)
        block = ctx.enter_context(nc.Block())
        HALF = NPB // 2
        EVAC = LAG - 1
        y_step = {4: 0, 5: 1}
        l_bank = (0, 1, 0, 1, 0, 0, 0, 1)
        Y_BANK = 1

        @block.sync
        def _(sp):
            def load(first):
                for kd in range(KD):
                    sp.dma_start(wt[:, kd], w_dram[bass.ds(first, NPB), kd * P:(kd + 1) * P, :].rearrange("n p e -> p n e")).then_inc(w_loaded, 16)
                sp.dma_start(bt[:], b_dram[bass.ds(first, NPB), :].partition_broadcast(P)).then_inc(b_loaded, 16)

            def store(k, first):
                sp.wait_ge(y_ready, k * 2 + 2)
                for b in range(B):
                    sp.dma_start(y_dram[b, bass.ds(first, NPB), :, :].rearrange("n s e -> s n e"),
                                 yb[b * PS:(b + 1) * PS, :, :]).then_inc(stored, 16)

            load(0)
            with sp.Fori(1, NBLK) as k:
                here, last = sp.snap(k * NPB), sp.snap((k - 1) * NPB)
                store(k - 1, last)
                sp.wait_ge(stored, k * (16 * B))
                load(here)
            store(NBLK - 1, (NBLK - 1) * NPB)
            sp.wait_ge(stored, NBLK * 16 * B)

        @block.tensor
        def _(pe):
            def score(k, mc):
                g = k * MC + mc
                wait(pe, copied, g - 1 if mc < 5 else g if mc < 7 else g - 3)
                if mc == 7:
                    wait(pe, y_ready, k * 2)
                p = l_bank[mc]
                for b in range(B):
                    t = b * TB + mc
                    for kd in range(KD):
                        for a, (xp, pp) in enumerate((("xh", "ph"), ("xh", "pl"), ("xl", "ph"))):
                            last = nc.tensor.matmul(psL[p][:, b, :], st[xp][:, kd, t * P:(t + 1) * P],
                                                    st[pp][:, kd, bass.ds(k * BLK, BLK)],
                                                    start=b % 2 == 0 and kd == 0 and a == 0, stop=kd == KD - 1 and a == 2,
                                                    skip_group_check=True)
                last.then_inc(logits, 1)

            def contract(k, mc):
                g = k * MC + mc
                wait(pe, share_ready, g + 1)
                if mc == 0:
                    wait(pe, slots_ready, k * KD)
                for kd in range(KD):
                    for b in range(B):
                        last = nc.tensor.matmul(psS[kd][:, b, :], x[:, b * TB + mc, kd * P:(kd + 1) * P], e[mc % 4][:, b, :],
                                                start=mc == 0 and b % 2 == 0, stop=mc == MC - 1, skip_group_check=True)
                last.then_inc(gone, 1)

            def expert(k, h, copies):
                wait(pe, w_loaded, k * (16 * KD) + 16 * KD)
                wait(pe, slots_ready, k * KD + KD)
                wait(pe, copied, copies)
                if h == 1:
                    wait(pe, y_ready, k * 2 + 1)
                for i in range(HALF):
                    for kd in range(KD):
                        last = nc.tensor.matmul(psL[Y_BANK][:, i, :], slots[:, kd, h * HALF + i, :, :].rearrange("p b s -> p (b s)"),
                                                wt[:, kd, h * HALF + i, :], start=kd == 0 and i % 2 == 0, stop=kd == KD - 1,
                                                skip_group_check=True)
                last.then_inc(y_raw, 1)

            def step(k, mc, fresh=False, draining=False):
                if not draining:
                    score(k, mc)
                if mc >= LAG and not draining:
                    contract(k, mc - LAG)
                if mc < LAG and not fresh:
                    contract(k - 1, mc - LAG + MC)
                if mc in y_step and not fresh:
                    expert(k - 1, y_step[mc], NBLK * MC if draining else k * MC + 4)

            for mc in range(MC):
                step(0, mc, fresh=True)
            with pe.Fori(1, NBLK) as k:
                for mc in range(MC):
                    step(k, mc)
            for mc in range(MC):
                step(NBLK, mc, draining=True)

        @block.scalar
        def _(act):
            def step(k, mc, fresh=False, draining=False):
                g = k * MC + mc
                if not draining:
                    wait(act, less, g + 1)
                    nc.scalar.activation(e[mc % 4][:], e[mc % 4][:], ACT.Exp).then_inc(exp_ready, 1)
                if mc == EVAC and not fresh:
                    wait(act, gone, k * MC)
                    for kd in range(KD):
                        nc.scalar.activation(slots[:, kd].rearrange("p n b s -> p b n s"),
                                             psS[kd][:].rearrange("p b (n s) -> p b n s", s=PS), ACT.Copy).then_inc(slots_ready, 1)

            for mc in range(MC):
                step(0, mc, fresh=True)
            with act.Fori(1, NBLK) as k:
                for mc in range(MC):
                    step(k, mc)
            step(NBLK, EVAC, draining=True)

        @block.gpsimd
        def _(pool):
            def share(g, q):
                wait(pool, rsum_ready, g + 1)
                nc.gpsimd.tensor_tensor(e[q % 4][:], e[q % 4][:], rs[q % 2][:].unsqueeze(1).to_broadcast([P, B, BLK]),
                                        ALU.mult).then_inc(share_ready, 1)

            def step(k, mc, fresh=False):
                g = k * MC + mc
                wait(pool, top_ready, g + 1)
                nc.gpsimd.tensor_tensor(e[mc % 4][:], e[mc % 4][:], top[mc % 2][:].unsqueeze(1).to_broadcast([P, B, BLK]),
                                        ALU.subtract).then_inc(less, 1)
                if mc > 0 or not fresh:
                    share(g - 1, mc + 7)

            for mc in range(MC):
                step(0, mc, fresh=True)
            with pool.Fori(1, NBLK) as k:
                for mc in range(MC):
                    step(k, mc)
            share(NBLK * MC - 1, MC - 1)

        @block.vector
        def _(dve):
            v = nc.vector

            def sums(g, q):
                wait(dve, exp_ready, g + 1)
                v.tensor_tensor(s2[q % 2][:], e[q % 4][:, 0:2, :], e[q % 4][:, 2:4, :], ALU.add).then_inc(pair_sum, 1)
                wait(dve, pair_sum, g + 1)
                wait(dve, share_ready, g - 1)
                v.tensor_tensor(rs[q % 2][:], s2[q % 2][:, 0, :], s2[q % 2][:, 1, :], ALU.add).then_inc(sum_ready, 1)
                wait(dve, sum_ready, g + 1)
                v.reciprocal(rs[q % 2][:], rs[q % 2][:]).then_inc(rsum_ready, 1)

            def copy_y(k, h):
                wait(dve, y_raw, k * 2 + (h + 1))
                wait(dve, b_loaded, k * 16 + 16)
                v.tensor_tensor(yb[:, h * HALF:(h + 1) * HALF, :], psL[Y_BANK][:], bt[:, h * HALF:(h + 1) * HALF, :],
                                ALU.add).then_inc(y_ready, 1)

            def step(k, mc, fresh=False, draining=False):
                g = k * MC + mc
                if mc - 1 in y_step and not fresh:
                    copy_y(k - 1, y_step[mc - 1])
                if draining:
                    return
                wait(dve, logits, g + 1)
                wait(dve, gone, g - 3)
                for b in range(B):
                    last = v.tensor_scalar(e[mc % 4][:, b, :], psL[l_bank[mc]][:, b, :], 1.0, None, ALU.mult, ALU.max,
                                           accum_out=st["rowmax"][:, b * TB + mc, bass.ds(k, 1)])
                last.then_inc(copied, 1)
                wait(dve, copied, g + 1)
                v.tensor_tensor(t2[mc % 2][:], e[mc % 4][:, 0:2, :], e[mc % 4][:, 2:4, :], ALU.max).then_inc(pair_max, 1)
                wait(dve, pair_max, g + 1)
                wait(dve, less, g - 1)
                v.tensor_tensor(top[mc % 2][:], t2[mc % 2][:, 0, :], t2[mc % 2][:, 1, :], ALU.max).then_inc(top_ready, 1)
                if mc > 0 or not fresh:
                    sums(g - 1, mc + 7)

            for mc in range(MC):
                step(0, mc, fresh=True)
            with dve.Fori(1, NBLK) as k:
                for mc in range(MC):
                    step(k, mc)
            sums(NBLK * MC - 1, MC - 1)
            for mc in range(MC):
                step(NBLK, mc, draining=True)


def combine(nc, c, st, x, y_dram, out_dram):
    LAG = 2
    W = D + 2
    HALVES = TB // MB
    STEPS = HALVES * CH
    ctx = ExitStack()
    m = Scope(nc, ctx, "comb")
    with ctx:
        top = m.sb("top", [P, NT])
        negtop = m.sb("negtop", [P, 2 * NT], F32R)
        tops = m.sb("tops", [2 * NT, P])
        mask = m.sb("mask", [2 * NT, NT + TB])
        ones = m.sb("ones", [2 * NT, P], F32R)
        shift = [m.sb(f"shift{i}", [2 * NT, MB, P], F32R) for i in range(2)]
        zero = m.sb("zero", [P, 1])
        y_in = m.sb("y_in", [P, CH // 2, D])
        yh = m.sb("yh", [P, CH, W], F32R)
        yl = m.sb("yl", [P, CH, W], F32R)
        e = [m.sb(f"e{i}", [P, MB * P]) for i in range(2)]
        eh = [m.sb(f"eh{i}", [P, MB * P], F32R) for i in range(4)]
        el = [m.sb(f"el{i}", [P, MB * P], F32R) for i in range(4)]
        rden = m.sb("rden", [P, MB])
        xo = m.sb("xo", [P, MB, D])
        stats = m.sb("stats", [P, MB, 6])
        mean, var, rstd, tmp = (m.sb(s, [P, MB]) for s in ("mean", "var", "rstd", "tmp"))
        magic = m.sb("magic", [P, MB], I32)
        psL = [m.ps(f"psL{i}", [P, MB * P]) for i in range(4)]
        psO = [m.ps(f"psO{i}", [P, 512]) for i in range(MB)]
        names = ("made", "chain", "top_ready", "neg_ready", "top_turned", "tops_ready", "shift_ready", "y_loaded", "y_split",
                 "logits", "exp_ready", "hi_ready", "lo_ready", "gone", "rden_ready", "summed", "stat", "normed", "stored")
        (made, chain, top_ready, neg_ready, top_turned, tops_ready, shift_ready, y_loaded, y_split,
         logits, exp_ready, hi_ready, lo_ready, gone, rden_ready, summed, stat, normed, stored) = (m.sem(s) for s in names)
        block = ctx.enter_context(nc.Block())

        @block.sync
        def _(sp):
            dst = out_dram.rearrange("b (g p w) d -> p (b g) w d", p=P, w=2)

            def load(b):
                y = y_dram[b].rearrange("n s e -> (n s) e").rearrange("(c p) e -> p c e", p=P)
                for h in range(2):
                    wait(sp, y_split, b * (2 * CH) + h * CH)
                    sp.dma_start(y_in[:], y[:, h * CH // 2:(h + 1) * CH // 2, :]).then_inc(y_loaded, 16)

            def store(mb):
                sp.wait_ge(normed, mb * MB + MB)
                sp.dma_start(dst[:, mb * MB // 2:(mb + 1) * MB // 2, :, :],
                             x[:, mb * MB:(mb + 1) * MB, :].rearrange("p (g w) d -> p g w d", w=2)).then_inc(stored, 16)

            load(0)
            for b in range(B):
                if b + 1 < B:
                    load(b + 1)
                if b > 0:
                    store(2 * b - 2)
                    store(2 * b - 1)
            store(B * HALVES - 2)
            store(B * HALVES - 1)
            sp.wait_ge(stored, B * HALVES * 16)

        @block.gpsimd
        def _(pool):
            g_ = nc.gpsimd
            g_.memset(mask[:], 0.0).then_inc(made, 1)
            g_.memset(ones[:].bitcast(F32), 1.0).then_inc(made, 1)
            g_.memset(zero[:], 0.0).then_inc(made, 1)
            g_.memset(yh[:, :, D:D + 1].bitcast(F32), 1.0).then_inc(made, 1)
            g_.memset(yh[:, :, D + 1:W].bitcast(F32), 0.0).then_inc(made, 1)
            g_.memset(yl[:, :, D:W].bitcast(F32), 0.0).then_inc(made, 1)
            pool.wait_ge(made, 6)
            for n in range(2):
                g_.affine_select(out=mask[:], in_=mask[:], compare_op=ALU.not_equal, fill=1.0, base=-n * NT,
                                 pattern=[[-1, NT + TB]], channel_multiplier=1).then_inc(made, 1)
                pool.wait_ge(made, 7 + n)

            def split(b, ch):
                y = y_in[:, ch % (CH // 2), :]
                if ch % (CH // 2) == 0:
                    wait(pool, y_loaded, b * 32 + (ch // (CH // 2) + 1) * 16)
                g_.tensor_tensor(yh[:, ch, 0:D], y, zero[:].to_broadcast([P, D]), ALU.add).then_inc(y_split, 1)
                wait(pool, y_split, b * (2 * CH) + (ch * 2 + 1))
                g_.tensor_tensor(yl[:, ch, 0:D], y, yh[:, ch, 0:D].bitcast(F32), ALU.subtract).then_inc(y_split, 1)

            for ch in range(CH):
                split(0, ch)
            with pool.Fori(1, B) as b:
                for ch in range(CH):
                    pool.wait_ge(gone, b * STEPS + (ch - (CH - 1)))
                    split(b, ch)

        @block.tensor
        def _(pe):
            pe.wait_ge(neg_ready, 2)
            nc.tensor.transpose(psL[0][0:2 * NT, 0:P], negtop[:].bitcast(F32), c["ident"][:]).then_inc(top_turned, 1)
            pe.wait_ge(tops_ready, 1)

            def score(b, s):
                half, ch = divmod(s, CH)
                g = b * STEPS + s
                wait(pe, exp_ready, g - 3)
                if ch == 0:
                    wait(pe, shift_ready, b * HALVES + (half + 1))
                cols = slice(ch * P, (ch + 1) * P)
                first = True
                for kd in range(KD):
                    for pp, xp in (("ph", "xh"), ("ph", "xl"), ("pl", "xh")):
                        nc.tensor.matmul(psL[ch % 4][:], st[pp][:, kd, cols],
                                         st[xp][:, kd, bass.ds(b * (TB * P) + half * (MB * P), MB * P)],
                                         start=first, stop=False)
                        first = False
                nc.tensor.matmul(psL[ch % 4][:], ones[:], shift[half][:].rearrange("p a t -> p (a t)"),
                                 start=False, stop=True).then_inc(logits, 1)

            def contract(b, s):
                half, ch = divmod(s, CH)
                g = b * STEPS + s
                wait(pe, lo_ready, g + 1)
                if half == 0:
                    wait(pe, y_split, b * (2 * CH) + (2 * ch + 2))
                if ch == 0:
                    wait(pe, summed, b * TB + half * MB)
                for a in range(MB):
                    sub = slice(a * P, (a + 1) * P)
                    for n, (ep, yp) in enumerate(((eh, yh), (eh, yl), (el, yh))):
                        last = nc.tensor.matmul(psO[a][:, 0:W], ep[ch % 4][:, sub], yp[:, ch, :],
                                                start=ch == 0 and n == 0, stop=ch == CH - 1 and n == 2)
                last.then_inc(gone, 1)

            def step(b, s, fresh=False, draining=False):
                if not draining:
                    score(b, s)
                if s >= LAG and not draining:
                    contract(b, s - LAG)
                if s < LAG and not fresh:
                    contract(b - 1, s - LAG + STEPS)

            for s in range(STEPS):
                step(0, s, fresh=True)
            with pe.Fori(1, B) as b:
                for s in range(STEPS):
                    step(b, s)
            for s in range(LAG):
                step(B, s, draining=True)

        @block.scalar
        def _(act):
            def step(i, s):
                g = i * 4 + s
                wait(act, logits, g + 1)
                wait(act, lo_ready, g - 1)
                nc.scalar.activation(e[s % 2][:], psL[s][:], ACT.Exp).then_inc(exp_ready, 1)

            for s in range(4):
                step(0, s)
            with act.Fori(1, B * STEPS // 4) as i:
                for s in range(4):
                    step(i, s)

        @block.vector
        def _(dve):
            v = nc.vector
            v.tensor_reduce(top[:], st["rowmax"][:], X, ALU.max).then_inc(top_ready, 1)
            dve.wait_ge(top_ready, 1)
            v.tensor_scalar(negtop[:, 0:NT], top[:], -1.0, None, ALU.mult).then_inc(neg_ready, 1)
            dve.wait_ge(neg_ready, 1)
            v.scalar_tensor_tensor(negtop[:, NT:], top[:], -1.0, negtop[:, 0:NT].bitcast(F32), ALU.mult, ALU.subtract).then_inc(neg_ready, 1)
            dve.wait_ge(top_turned, 1)
            v.tensor_copy(tops[:], psL[0][0:2 * NT, 0:P]).then_inc(tops_ready, 1)
            dve.wait_ge(tops_ready, 1)
            dve.wait_ge(made, 8)

            def spread(b, half):
                v.tensor_tensor(shift[half][:], tops[:].unsqueeze(1).to_broadcast([2 * NT, MB, P]),
                                mask[:, bass.ds(b * TB + half * MB, MB)].unsqueeze(2).to_broadcast([2 * NT, MB, P]),
                                ALU.mult).then_inc(shift_ready, 1)

            spread(0, 0)
            def row(t):
                return x[:, bass.ds(t, 1), :].rearrange("p a d -> p (a d)")

            def collect(b, half):
                t0 = b * TB + half * MB
                wait(dve, gone, b * STEPS + (half * CH + CH))
                for a in range(MB):
                    v.reciprocal(rden[:, a:a + 1], psO[a][:, D:D + 1]).then_inc(rden_ready, 1)
                wait(dve, rden_ready, t0 + MB)
                for a in range(MB):
                    v.scalar_tensor_tensor(xo[:, a, :], psO[a][:, 0:D], rden[:, a:a + 1], row(t0 + a), ALU.mult, ALU.add).then_inc(summed, 1)

            def moments(b, half):
                t0 = b * TB + half * MB
                wait(dve, summed, t0 + MB)
                for a in range(MB):
                    v.bn_stats(stats[:, a, :], xo[:, a, :]).then_inc(stat, 1)

            def norm(b, half):
                t0 = b * TB + half * MB
                n = [0]
                wait(dve, stat, t0 + MB)

                def link(*steps):
                    n[0] += len(steps)
                    for ins in steps:
                        ins.then_inc(chain, 1)
                    dve.wait_ge(chain, b * (HALVES * NORM_LINKS) + (half * NORM_LINKS + n[0]))

                norm_steps(v, link, stats[:], mean[:], rstd[:], var[:], tmp[:], magic[:])
                for a in range(MB):
                    v.tensor_scalar(row(t0 + a), xo[:, a, :], mean[:, a:a + 1], rstd[:, a:a + 1], ALU.subtract, ALU.mult).then_inc(normed, 1)

            def step(b, s, fresh=False):
                half, ch = divmod(s, CH)
                g = b * STEPS + s
                wait(dve, exp_ready, g + 1)
                wait(dve, gone, g - 3)
                v.tensor_copy(eh[s % 4][:], e[s % 2][:]).then_inc(hi_ready, 1)
                wait(dve, hi_ready, g + 1)
                v.tensor_tensor(el[s % 4][:], e[s % 2][:], eh[s % 4][:].bitcast(F32), ALU.subtract).then_inc(lo_ready, 1)
                if s == LAG + 2:
                    spread(b, 1)
                if s == CH + LAG + 2:
                    spread(b + 1, 0)
                if half > 0 or not fresh:
                    before = (b, half - 1) if half > 0 else (b - 1, HALVES - 1)
                    if ch == LAG - 1:
                        collect(*before)
                    if ch == LAG:
                        moments(*before)
                    if ch == LAG + 1:
                        norm(*before)

            for s in range(STEPS):
                step(0, s, fresh=True)
            with dve.Fori(1, B) as b:
                for s in range(STEPS):
                    step(b, s)
            collect(B - 1, HALVES - 1)
            moments(B - 1, HALVES - 1)
            norm(B - 1, HALVES - 1)


def program(nc, x_in, router_w, router_b, w1, w2, w_attn, phi, w_slot, b_slot, out):
    x1_dram = nc.dram_tensor("x1_rows", [NT * P, D], F32, kind="Internal").ap()
    ys_dram = nc.dram_tensor("sorted_y", [SLOTS * P, D], F32, kind="Internal").ap()
    y_dram = nc.dram_tensor("slot_y", [B, N, PS, D], F32, kind="Internal").ap()
    with ExitStack() as ctx:
        c = {}
        route = routing_tables(nc, ctx)
        with ExitStack() as held:
            constants(nc, ctx, held, c)
            weights = Weights(nc, held, w1, w2)
            with ExitStack() as first:
                m = Scope(nc, first, "first")
                x1 = m.sb("x", [P, NT, D])
                stats = m.sb("stats", [P, NT, 6])
                dilated_attention(nc, c, x_in, x1, stats)
                normalise_and_route(nc, c, x1, stats, router_w, router_b, x1_dram, route, weights)
            experts(nc, c, weights, route, x1_dram, ys_dram)
        x = Scope(nc, ctx, "last").sb("x", [P, NT, D])
        linear_attention(nc, c, route, x1_dram, ys_dram, w_attn, x)
        state = soft_state(nc, ctx)
        turn_tokens(nc, c, state, x, phi)
        dispatch(nc, c, state, x, w_slot, b_slot, y_dram)
        combine(nc, c, state, x, y_dram, out)


def kernel(L0_attn_x, L0_ffn_router_w, L0_ffn_router_b, L0_ffn_w1, L0_ffn_w2, L1_attn_W, L1_ffn_phi, L1_ffn_W, L1_ffn_b):
    import numpy as np
    import concourse.bacc as bacc
    from concourse.bass_utils import run_bass_kernel_spmd

    nc = bacc.Bacc("TRN2", target_bir_lowering=False, num_devices=1)
    given = {"x": L0_attn_x, "router_w": L0_ffn_router_w, "router_b": L0_ffn_router_b, "w1": L0_ffn_w1, "w2": L0_ffn_w2,
             "w_attn": L1_attn_W, "phi": L1_ffn_phi, "w_slot": L1_ffn_W, "b_slot": L1_ffn_b}
    arrays, args = {}, []
    for name, value in given.items():
        a = np.ascontiguousarray(value)
        arrays[f"in_{name}"] = a
        args.append(nc.dram_tensor(f"in_{name}", a.shape, mybir.dt.from_np(a.dtype), kind="ExternalInput").ap())
    args.append(nc.dram_tensor("out", (B, S, D), F32, kind="ExternalOutput").ap())
    program(nc, *args)
    return run_bass_kernel_spmd(nc, [arrays], core_ids=[0]).results[0]["out"]
```

```python
from contextlib import ExitStack

import concourse.bass as bass
from concourse import mybir

ALU = mybir.AluOpType
ACT = mybir.ActivationFunctionType
X = mybir.AxisListType.X
F32 = mybir.dt.float32
F32R = mybir.dt.float32r
BF16 = mybir.dt.bfloat16
I32 = mybir.dt.int32

P = 128
B, S, D = 4, 1024, 256
KD = D // P
SEG = 256
NSEG = B * S // SEG
NT = B * S // P
TB = NT // B
NH, HD = 16, 16
UH = 4
UPS = NH // UH
HG = P // HD // UH
NE, FF = 8, 1024
SLOTS = NT + NE - 1
LN_EPS = 1e-5


def wait(eng, sem, count):
    if not isinstance(count, int) or count > 0:
        eng.wait_ge(sem, count)


def stages(step, lag, period, fresh, draining):
    k = step - lag
    if k < 0:
        return None if fresh else k
    return None if draining else k


def norm_steps(v, link, stats, mean, rstd, var, tmp, magic):
    link(v.tensor_tensor(mean, stats[:, :, 1], stats[:, :, 4], ALU.add),
         v.tensor_tensor(var, stats[:, :, 1], stats[:, :, 4], ALU.subtract),
         v.tensor_tensor(tmp, stats[:, :, 2], stats[:, :, 5], ALU.add))
    link(v.tensor_scalar(mean, mean, 0.5, None, ALU.mult),
         v.scalar_tensor_tensor(var, var, 0.25, var, ALU.mult, ALU.mult),
         v.tensor_scalar(tmp, tmp, 1.0 / D, LN_EPS, ALU.mult, ALU.add))
    link(v.tensor_tensor(var, var, tmp, ALU.add))
    link(v.tensor_scalar(magic, var.bitcast(I32), 1, None, ALU.logical_shift_right))
    link(v.tensor_scalar(rstd.bitcast(I32), magic, -1.0, 1597463007.0, ALU.mult, ALU.add))
    for _ in range(3):
        link(v.tensor_tensor(tmp, rstd, rstd, ALU.mult))
        link(v.scalar_tensor_tensor(tmp, tmp, -0.5, var, ALU.mult, ALU.mult))
        link(v.scalar_tensor_tensor(rstd, tmp, 1.5, rstd, ALU.add, ALU.mult))


NORM_LINKS = 18


class Scope:

    def __init__(self, nc, ctx, tag):
        self.nc, self.ctx, self.tag = nc, ctx, tag

    def sb(self, name, shape, dt=F32):
        return self.ctx.enter_context(self.nc.sbuf_tensor(f"{self.tag}_{name}", shape, dt))

    def ps(self, name, shape, dt=F32):
        return self.ctx.enter_context(self.nc.psum_tensor(f"{self.tag}_{name}", shape, dt))

    def sem(self, name):
        return self.ctx.enter_context(self.nc.semaphore(f"{self.tag}_{name}"))


def constants(nc, ctx, held, c):
    c["ident"] = Scope(nc, ctx, "const").sb("ident", [P, P])
    m = Scope(nc, held, "const")
    c["headmask"] = m.sb("headmask", [P, HG * UH])
    c["pick_raw"] = m.sb("pick_raw", [2 * UH, UH // 2, P])
    c["pick"] = m.sb("pick", [2 * UH, UH // 2, P], F32R)
    c["parity"] = m.sb("parity", [2 * UH, 2])
    c["eidx"] = m.sb("eidx", [P, NE])
    c["tri"] = m.sb("tri", [P, P])
    c["ones"] = m.sb("ones", [P, P])
    c["iota_r"] = m.sb("iota_r", [P, P])
    c["iota_s"] = m.sb("iota_s", [P, SLOTS + 1])
    c["iota_t"] = m.sb("iota_t", [P, NT])
    c["iota_p"] = m.sb("iota_p", [P, 1])
    c["filled"] = m.sem("filled")


CONSTANT_STEPS = 24


def fill_constants(nc, c, pool):
    filled = c["filled"]
    g = nc.gpsimd
    n = 0
    for key, value in (("ident", 0.0), ("headmask", 1.0), ("pick_raw", 0.0), ("parity", 0.0), ("ones", 1.0), ("tri", 1.0)):
        g.memset(c[key][:], value).then_inc(filled, 1)
        n += 1
    g.iota(c["iota_r"][:], [[1, P]], base=0, channel_multiplier=0, allow_small_or_imprecise_dtypes=True).then_inc(filled, 1)
    g.iota(c["iota_s"][:], [[1, SLOTS + 1]], base=0, channel_multiplier=0, allow_small_or_imprecise_dtypes=True).then_inc(filled, 1)
    g.iota(c["iota_t"][:], [[1, NT]], base=0, channel_multiplier=0, allow_small_or_imprecise_dtypes=True).then_inc(filled, 1)
    g.iota(c["iota_p"][:], [[1, 1]], base=0, channel_multiplier=1, allow_small_or_imprecise_dtypes=True).then_inc(filled, 1)
    g.iota(c["eidx"][:], [[1, NE]], base=-NE, channel_multiplier=0, allow_small_or_imprecise_dtypes=True).then_inc(filled, 1)
    n += 5
    pool.wait_ge(filled, n)
    g.affine_select(out=c["ident"][:], in_=c["ident"][:], compare_op=ALU.not_equal, fill=1.0,
                    base=0, pattern=[[-1, P]], channel_multiplier=1).then_inc(filled, 1)
    g.affine_select(out=c["tri"][:], in_=c["tri"][:], compare_op=ALU.is_gt, fill=0.0,
                    base=0, pattern=[[1, P]], channel_multiplier=-1).then_inc(filled, 1)
    g.affine_select(out=c["headmask"][:], in_=c["headmask"][:], compare_op=ALU.is_ge, fill=0.0,
                    base=0, pattern=[[-HD, HG * UH]], channel_multiplier=1).then_inc(filled, 1)
    n += 3
    for i in range(4):
        for key, base, pattern in (("pick_raw", i // 2 * UH + i % 2, [[-2, UH // 2], [0, P]]), ("parity", 2 * i, [[-1, 2]])):
            g.affine_select(out=c[key][:], in_=c[key][:], compare_op=ALU.not_equal, fill=1.0,
                            base=-base, pattern=pattern, channel_multiplier=1).then_inc(filled, 1)
        n += 2
        pool.wait_ge(filled, n)
    g.affine_select(out=c["headmask"][:], in_=c["headmask"][:], compare_op=ALU.is_ge, fill=0.0,
                    base=HD - 1, pattern=[[HD, HG * UH]], channel_multiplier=-1).then_inc(filled, 1)
    pool.wait_ge(filled, n + 1)
    g.tensor_copy(c["pick"][:], c["pick_raw"][:]).then_inc(filled, 1)
    pool.wait_ge(filled, n + 2)
    assert n + 2 == CONSTANT_STEPS


def dilated_attention(nc, c, x_dram, x1, stats, weights):
    LS, LM, LA, LO = 2, 3, 4, 5
    OW = UH * (HD + 1)
    ctx = ExitStack()
    m = Scope(nc, ctx, "att")
    with ctx:
        xe = [m.sb(f"xe{i}", [P, D]) for i in range(2)]
        xaug = [m.sb(f"xaug{i}", [P, NH, HD + 1]) for i in range(2)]
        xT = [m.sb(f"xT{i}", [P, KD, P]) for i in range(2)]
        xm = [m.sb(f"xm{i}", [P, UH, P]) for i in range(UPS)]
        prob = [m.sb(f"prob{i}", [P, UH, P]) for i in range(UPS)]
        mx = [m.sb(f"mx{i}", [P, UH]) for i in range(UPS)]
        negmax = [m.sb(f"negmax{i}", [P, 2 * UH], F32R) for i in range(UPS)]
        shift = [m.sb(f"shift{i}", [2 * UH, 2, P], F32R) for i in range(UPS)]
        rden = [m.sb(f"rden{i}", [P, UH]) for i in range(UPS)]
        heads = [m.sb(f"heads{i}", [P, D]) for i in range(2)]
        small = [m.sb(f"small{i}", [P, 4]) for i in range(2)]
        psS = [m.ps(f"psS{i}", [P, UH, P]) for i in range(UPS)]
        psT = m.ps("psT", [P, KD, P])
        psM = m.ps("psM", [2 * UH, P])
        psO = [m.ps(f"psO{i}", [P, 512]) for i in range(2)]
        loaded, aug_ready, xT_raw, xT_ready, xm_ready = (m.sem(s) for s in ("loaded", "aug_ready", "xT_raw", "xT_ready", "xm_ready"))
        scored, max_ready, hi_ready, negmax_ready, max_turned, shift_ready, shifted, prob_ready, out_raw, rden_ready, heads_ready, fin = (
            m.sem(s) for s in ("scored", "max_ready", "hi_ready", "negmax_ready", "max_turned", "shift_ready", "shifted",
                               "prob_ready", "out_raw", "rden_ready", "heads_ready", "fin"))
        ones_set = m.sem("ones_set")
        even_loaded = [m.sem(f"even_loaded{i}") for i in range(2)]
        block = ctx.enter_context(nc.Block())

        @block.sync
        def _(sp):
            src = x_dram.rearrange("b (g p w) d -> p (b g) (w d)", p=P, w=2)
            dst = x1[:].rearrange("p (g w) d -> p g (w d)", w=2)

            def load(i, segs):
                wait(sp, loaded, i * 16)
                sp.dma_start(dst[:, bass.ds(segs[0], 2), :], src[:, bass.ds(segs[0], 2), :]).then_inc(loaded, 16)
                for q in range(2):
                    if not isinstance(i, int):
                        sp.wait_ge(xT_raw, i * 2 + (q - 1))
                    sp.dma_start(xe[q][:], src[:, bass.ds(segs[q], 1), 0:D].rearrange("p a d -> p (a d)")).then_inc(even_loaded[q], 16)

            load(0, (0, 1))
            weights.load(sp, 0)
            with sp.Fori(1, NSEG // 2) as i:
                load(i, (sp.snap(i * 2), sp.snap(i * 2 + 1)))

        @block.gpsimd
        def _(pool):
            def masks(i):
                for k in range(2 * UPS):
                    q, g = divmod(k, UPS)
                    half, part = divmod(g, HG)
                    if g == 0:
                        wait(pool, xT_ready, i * 2 + (q + 1))
                    wait(pool, scored, i * 8 + (k - UPS + 1))
                    nc.gpsimd.tensor_tensor(
                        xm[g][:], xT[q][:, half, :].unsqueeze(1).to_broadcast([P, UH, P]),
                        c["headmask"][:, part * UH:(part + 1) * UH].unsqueeze(2).to_broadcast([P, UH, P]),
                        ALU.mult).then_inc(xm_ready, 1)

            fill_constants(nc, c, pool)
            masks(0)
            with pool.Fori(1, NSEG // 2) as i:
                masks(i)

        @block.tensor
        def _(pe):
            def step(i, k, fresh=False, draining=False):
                def unit(lag):
                    j = stages(k, lag, 8, fresh, draining)
                    return (None, 0, 0) if j is None else (i * 8 + j, (j % 8) // UPS, j % UPS)

                u, q, g = unit(LS)
                if u is not None:
                    wait(pe, xm_ready, u + 1)
                    wait(pe, prob_ready, u - (UPS - 1))
                    nc.tensor.matmul(psS[g][:].rearrange("p a b -> p (a b)"), xT[q][:, g // HG, :],
                                     xm[g][:].rearrange("p a b -> p (a b)"), start=True, stop=True).then_inc(scored, 1)
                u, q, g = unit(LM)
                if u is not None:
                    wait(pe, negmax_ready, u + 1)
                    wait(pe, shift_ready, u)
                    nc.tensor.transpose(psM[:], negmax[g][:].bitcast(F32), c["ident"][:]).then_inc(max_turned, 1)
                u, q, g = unit(LA)
                if u is not None:
                    wait(pe, shift_ready, u + 1)
                    for n in range(UH // 2):
                        last = nc.tensor.matmul(psS[g][:, 2 * n:2 * n + 2, :].rearrange("p a t -> p (a t)"), c["pick"][:, n, :],
                                                shift[g][:].rearrange("p a t -> p (a t)"), start=False, stop=True,
                                                skip_group_check=True)
                    last.then_inc(shifted, 1)
                u, q, g = unit(LO)
                if u is not None:
                    wait(pe, prob_ready, u + 1)
                    if g == 0:
                        wait(pe, aug_ready, i * 2 + (k - LO) // UPS + 1)
                    wait(pe, heads_ready, u - 1)
                    for j in range(UH):
                        last = nc.tensor.matmul(psO[g % 2][:, j * OW:(j + 1) * OW], prob[g][:, j, :],
                                                xaug[q][:, g * UH:(g + 1) * UH, :].rearrange("p h d -> p (h d)"),
                                                start=True, stop=True)
                    last.then_inc(out_raw, 1)
                if k % UPS == 0 and not draining:
                    q = k // UPS
                    seg = i * 2 + q
                    wait(pe, even_loaded[q], i * 16 + 16)
                    wait(pe, xT_ready, seg)
                    for half in range(KD):
                        last = nc.tensor.transpose(psT[:, half, :], xe[q][:, half * P:(half + 1) * P], c["ident"][:])
                    last.then_inc(xT_raw, 1)

            pe.wait_ge(c["filled"], CONSTANT_STEPS)
            for k in range(8):
                step(0, k, fresh=True)
            with pe.Fori(1, NSEG // 2) as i:
                for k in range(8):
                    step(i, k)
            for k in range(LO):
                step(NSEG // 2, k, draining=True)

        @block.scalar
        def _(act):
            act.wait_ge(ones_set, 2)

            def step(i, k, fresh=False, draining=False):
                j = stages(k, LS, 8, fresh, draining)
                if j is not None:
                    u, g = i * 8 + j, j % UPS
                    wait(act, max_ready, u + 1)
                    wait(act, max_turned, u - (UPS - 1))
                    nc.scalar.activation(negmax[g][:, 0:UH], mx[g][:], ACT.Copy, scale=-1.0).then_inc(hi_ready, 1)
                j = stages(k, LA, 8, fresh, draining)
                if j is not None:
                    u, g = i * 8 + j, j % UPS
                    wait(act, shifted, u + 1)
                    wait(act, out_raw, u - (UPS - 1))
                    nc.scalar.activation(prob[g][:], psS[g][:], ACT.Exp, scale=HD ** -0.5).then_inc(prob_ready, 1)
                q = k // UPS
                seg = i * 2 + q
                if k % UPS == LO - UPS and not draining:
                    act.wait_ge(loaded, i * 16 + 16)
                    wait(act, out_raw, (seg - 1) * UPS)
                    nc.scalar.activation(xaug[q][:, :, 0:HD],
                                         x1[:, bass.ds(seg * 2, 1), :].rearrange("p a (h d) -> p (a h) d", d=HD),
                                         ACT.Copy).then_inc(aug_ready, 1)
                if k % UPS == 0 and not draining:
                    wait(act, xT_raw, seg + 1)
                    wait(act, scored, (seg - 1) * UPS + 1)
                    nc.scalar.activation(xT[q][:], psT[:], ACT.Copy).then_inc(xT_ready, 1)

            for k in range(8):
                step(0, k, fresh=True)
            with act.Fori(1, NSEG // 2) as i:
                for k in range(8):
                    step(i, k)
            for k in range(LA):
                step(NSEG // 2, k, draining=True)

        @block.vector
        def _(dve):
            dve.wait_ge(c["filled"], CONSTANT_STEPS)
            for q in range(2):
                nc.vector.memset(xaug[q][:, :, HD:HD + 1], 1.0).then_inc(ones_set, 1)

            def finish(seg, q):
                row = x1[:, bass.ds(seg * 2, 1), :].rearrange("p a d -> p (a d)")
                den, rec, alpha = (small[q][:, n:n + 1] for n in range(3))
                wait(dve, heads_ready, seg * UPS + UPS)
                nc.vector.tensor_reduce(den, heads[q][:], X, ALU.add).then_inc(fin, 1)
                wait(dve, fin, seg * 4 + 1)
                nc.vector.reciprocal(rec, den).then_inc(fin, 1)
                wait(dve, fin, seg * 4 + 2)
                nc.vector.tensor_tensor(alpha, den, rec, ALU.mult).then_inc(fin, 1)
                wait(dve, fin, seg * 4 + 3)
                nc.vector.scalar_tensor_tensor(row, heads[q][:], alpha, row, ALU.mult, ALU.add).then_inc(fin, 1)

            def row_stats(seg, w):
                nc.vector.bn_stats(stats[:, bass.ds(seg * 2 + w, 1), :].rearrange("p a d -> p (a d)"),
                                   x1[:, bass.ds(seg * 2 + w, 1), :].rearrange("p a d -> p (a d)"))

            def step(i, k, fresh=False, draining=False):
                def unit(lag):
                    j = stages(k, lag, 8, fresh, draining)
                    return (None, 0, 0) if j is None else (i * 8 + j, (j % 8) // UPS, j % UPS)

                u, q, g = unit(LS)
                done = (k - 1 - LO) // UPS if (k - 1 - LO) % UPS == UPS - 1 and (k > LO or not fresh) else None
                if u is not None:
                    if done is not None:
                        wait(dve, fin, (i * 2 + done) * 4 + 4)
                    wait(dve, scored, u + 1)
                    wait(dve, max_turned, u - (UPS - 1))
                    nc.vector.tensor_reduce(mx[g][:], psS[g][:], X, ALU.max).then_inc(max_ready, 1)
                    if done is not None:
                        row_stats(i * 2 + done, 0)
                        row_stats(i * 2 + done, 1)
                low = (u, g)
                u, q, g = unit(LM)
                if u is not None:
                    wait(dve, max_turned, u + 1)
                    wait(dve, shifted, u - (UPS - 1))
                    nc.vector.tensor_tensor(shift[g][:], psM[:].unsqueeze(1).to_broadcast([2 * UH, 2, P]),
                                            c["parity"][:].unsqueeze(2).to_broadcast([2 * UH, 2, P]),
                                            ALU.mult).then_inc(shift_ready, 1)
                u, g = low
                if u is not None:
                    wait(dve, hi_ready, u + 1)
                    nc.vector.scalar_tensor_tensor(negmax[g][:, UH:2 * UH], mx[g][:], -1.0, negmax[g][:, 0:UH].bitcast(F32),
                                                   ALU.mult, ALU.subtract).then_inc(negmax_ready, 1)
                u, q, g = unit(LO)
                if u is not None:
                    wait(dve, out_raw, u + 1)
                    o = psO[g % 2][:, 0:UH * (OW + HD + 1)].rearrange("p (h d) -> p h d", h=UH)
                    nc.vector.reciprocal(rden[g][:].unsqueeze(2), o[:, :, HD:HD + 1]).then_inc(rden_ready, 1)
                    wait(dve, rden_ready, u + 1)
                    nc.vector.tensor_tensor(heads[q][:, g * UH * HD:(g + 1) * UH * HD].rearrange("p (h d) -> p h d", h=UH),
                                            o[:, :, 0:HD], rden[g][:].unsqueeze(2).to_broadcast([P, UH, HD]),
                                            ALU.mult).then_inc(heads_ready, 1)
                    if g == UPS - 1:
                        finish(i * 2 + (k - LO) // UPS, q)

            for k in range(8):
                step(0, k, fresh=True)
            with dve.Fori(1, NSEG // 2) as i:
                for k in range(8):
                    step(i, k)
            for k in range(LO):
                step(NSEG // 2, k, draining=True)
            dve.wait_ge(fin, NSEG * 4)
            for w in range(2):
                row_stats(NSEG - 1, w)


NCOL = SLOTS + 1


def normalise_and_route(nc, c, x1, stats, router_w, router_b, x1_dram, route, weights):
    ctx = ExitStack()
    m = Scope(nc, ctx, "route")
    XB = 3
    GT = 4
    with ctx:
        mean = m.sb("mean", [P, NT])
        rstd = m.sb("rstd", [P, NT])
        var = m.sb("var", [P, NT])
        tmp = m.sb("tmp", [P, NT])
        magic = m.sb("magic", [P, NT], I32)
        xT = [m.sb(f"xT{i}", [P, KD, GT, P]) for i in range(2)]
        logit_t = [m.sb(f"logit_t{i}", [NE, GT * P]) for i in range(2)]
        rw = m.sb("rw", [P, KD, NE])
        rb = m.sb("rb", [P, NE])
        logit = m.sb("logit", [P, NT, NE])
        best = m.sb("best", [P, NT])
        expd = m.sb("expd", [P, NT, NE])
        cand = m.sb("cand", [P, NT, NE])
        bidx = m.sb("bidx", [P, NT])
        onehot = m.sb("onehot", [P, NT, NE])
        PADT = NT // 2
        count = [m.sb(f"count{i}", [P, PADT + NT, NE]) for i in range(2)]
        tiles = [m.sb(f"tiles{i}", [P, NE // 2 + NE]) for i in range(2)]
        nt_f = m.sb("nt_f", [P, NE])
        nt_i = m.sb("nt_i", [P, NE], I32)
        base = m.sb("base", [P, NE])
        place = m.sb("place", [P, NT])
        ptile_i = m.sb("ptile_i", [P, NT], I32)
        ptile = m.sb("ptile", [P, NT])
        prow = m.sb("prow", [P, NT])
        past = m.sb("past", [P, NCOL, NE - 1])
        sexp = m.sb("sexp", [P, NCOL])
        rows1 = m.sb("rows1", [P, NT, P], BF16)
        slots1 = m.sb("slots1", [P, NT, NCOL])
        ids = m.sb("ids", [P, NT, 2 * NCOL], BF16)
        psX = [m.ps(f"psX{i}", [P, 2, KD, P]) for i in range(XB)]
        psL = [m.ps(f"psL{i}", [NE, GT * P]) for i in range(2)]
        psR = m.ps("psR", [P, NT, NE])
        psAB = m.ps("psAB", [P, 2, NT, NE])
        psA, psB = psAB[:, 0], psAB[:, 1]
        psI = m.ps("psI", [P, 2 * NCOL])
        (w_loaded, chain, kept, turned, xT_ready, scored, scores_ready, routed, diff_ready, exp_ready,
         onehot_ready, counted, tables_ready, gathered, stored) = (m.sem(s) for s in (
             "w_loaded", "chain", "kept", "turned", "xT_ready", "scored", "scores_ready", "routed", "diff_ready",
             "exp_ready", "onehot_ready", "counted", "tables_ready", "gathered", "stored"))
        block = ctx.enter_context(nc.Block())

        @block.sync
        def _(sp):
            sp.dma_start(rw[:], router_w.rearrange("(k p) e -> p k e", p=P)).then_inc(w_loaded, 16)
            sp.dma_start(rb[:], router_b.partition_broadcast(P)).then_inc(w_loaded, 16)
            weights.load(sp, 1)
            for b in range(B):
                sp.wait_ge(kept, (b + 1) * TB)
                sp.dma_start(x1_dram.rearrange("(t p) d -> p t d", p=P)[:, b * TB:(b + 1) * TB, :],
                             x1[:, b * TB:(b + 1) * TB, :]).then_inc(stored, 16)
            sp.wait_ge(stored, 16 * B)

        @block.gpsimd
        def _(pool):
            weights.divide_low(pool, 0)
            weights.divide_low(pool, 1)

        @block.tensor
        def _(pe):
            def turn(i):
                wait(pe, kept, i * 2 + 2)
                wait(pe, xT_ready, i - XB + 1)
                for a in range(2):
                    for k in range(KD):
                        last = nc.tensor.transpose(psX[i % XB][:, a, k, :], x1[:, 2 * i + a, k * P:(k + 1) * P], c["ident"][:])
                last.then_inc(turned, 1)

            def score(g):
                wait(pe, xT_ready, g * 2 + 2)
                wait(pe, scores_ready, g - 1)
                for k in range(KD):
                    last = nc.tensor.matmul(psL[g % 2][:], rw[:, k, :], xT[g % 2][:, k].rearrange("p a t -> p (a t)"),
                                            start=k == 0, stop=k == KD - 1)
                last.then_inc(scored, 1)

            def turn_back(g):
                wait(pe, scores_ready, g + 1)
                for a in range(GT):
                    last = nc.tensor.transpose(psR[:, g * GT + a, :], logit_t[g % 2][:, a * P:(a + 1) * P], c["ident"][0:NE, 0:NE])
                last.then_inc(routed, 1)

            pe.wait_ge(w_loaded, 32)
            for g in range(NT // GT + 2):
                if g < NT // GT:
                    turn(2 * g)
                    turn(2 * g + 1)
                if g > 1:
                    turn_back(g - 2)
                if 0 < g <= NT // GT:
                    score(g - 1)
            pe.wait_ge(onehot_ready, 1)
            nc.tensor.matmul(psA.rearrange("p t e -> p (t e)"), c["tri"][:], onehot[:].rearrange("p t e -> p (t e)"),
                             start=True, stop=True).then_inc(counted, 1)
            nc.tensor.matmul(psB.rearrange("p t e -> p (t e)"), c["ones"][:], onehot[:].rearrange("p t e -> p (t e)"),
                             start=True, stop=True).then_inc(counted, 1)
            pe.wait_ge(tables_ready, 3)
            for t in range(NT):
                last = nc.tensor.matmul(psI[:], rows1[:, t, :], ids[:, t, :], start=t == 0, stop=t == NT - 1)
            last.then_inc(gathered, 1)

        @block.scalar
        def _(act):
            weights.divide_high(act, 0)

            def out(g):
                act.wait_ge(scored, g + 1)
                wait(act, routed, g - 1)
                nc.scalar.activation(logit_t[g % 2][:], psL[g % 2][:], ACT.Copy).then_inc(scores_ready, 1)

            for i in range(NT // 2):
                g = i // 2
                act.wait_ge(turned, i + 1)
                wait(act, scored, g - 1)
                nc.scalar.activation(xT[g % 2][:, :, i % 2 * 2:i % 2 * 2 + 2, :].rearrange("p k a t -> p a k t"),
                                     psX[i % XB][:], ACT.Copy).then_inc(xT_ready, 1)
                if i % 2 == 1 and g > 0:
                    out(g - 1)
            out(NT // GT - 1)
            act.wait_ge(diff_ready, 1)
            nc.scalar.activation(expd[:], expd[:], ACT.Exp).then_inc(exp_ready, 1)
            weights.divide_high(act, 1)

        @block.vector
        def _(dve):
            v = nc.vector
            n = [0]

            def link(*steps):
                n[0] += len(steps)
                for ins in steps:
                    ins.then_inc(chain, 1)
                dve.wait_ge(chain, n[0])

            norm_steps(v, link, stats[:], mean[:], rstd[:], var[:], tmp[:], magic[:])

            for t in range(NT):
                v.tensor_scalar(x1[:, t, :], x1[:, t, :], mean[:, t:t + 1], rstd[:, t:t + 1], ALU.subtract, ALU.mult).then_inc(kept, 1)
            dve.wait_ge(w_loaded, 32)
            dve.wait_ge(routed, NT // GT)
            link(v.tensor_tensor(logit[:], psR[:], rb[:].unsqueeze(1).to_broadcast([P, NT, NE]), ALU.add))
            link(v.tensor_reduce(best[:], logit[:], X, ALU.max))
            bc = lambda ap: ap.unsqueeze(2).to_broadcast([P, NT, NE])
            over_t = lambda ap: ap.unsqueeze(1).to_broadcast([P, NT, NE])
            v.tensor_tensor(expd[:], logit[:], bc(best[:]), ALU.subtract).then_inc(diff_ready, 1)
            dve.wait_ge(diff_ready, 1)
            link(v.tensor_tensor(cand[:], logit[:], bc(best[:]), ALU.is_ge))
            link(v.tensor_tensor(cand[:], cand[:], over_t(c["eidx"][:]), ALU.mult))
            link(v.tensor_reduce(bidx[:], cand[:], X, ALU.min))
            v.tensor_tensor(onehot[:], bc(bidx[:]), over_t(c["eidx"][:]), ALU.is_equal).then_inc(onehot_ready, 1)
            dve.wait_ge(exp_ready, 1)
            link(v.tensor_reduce(tmp[:], expd[:], X, ALU.add))
            v.reciprocal(route["prob"][:], tmp[:])
            for i in range(2):
                link(v.memset(count[i][:, 0:PADT, :], 0.0))
                link(v.memset(tiles[i][:, 0:NE // 2], 0.0))
            dve.wait_ge(counted, 2)
            link(v.tensor_copy(count[0][:, PADT:, :], psB))
            a, shift = 0, 1
            while shift < NT:
                link(v.tensor_tensor(count[1 - a][:, PADT:, :], count[a][:, PADT:, :],
                                     count[a][:, PADT - shift:PADT + NT - shift, :], ALU.add))
                a, shift = 1 - a, 2 * shift
            total = count[a][:, PADT + NT - 1, :]
            link(v.tensor_scalar(nt_i[:], total, float(P - 1), None, ALU.add))
            link(v.tensor_scalar(nt_i[:], nt_i[:], 7, None, ALU.logical_shift_right))
            link(v.tensor_scalar(nt_f[:], nt_i[:], 1.0, None, ALU.max))
            half = NE // 2
            link(v.tensor_copy(tiles[0][:, half:], nt_f[:]))
            e, shift = 0, 1
            while shift < NE:
                link(v.tensor_tensor(tiles[1 - e][:, half:], tiles[e][:, half:], tiles[e][:, half - shift:half + NE - shift], ALU.add))
                e, shift = 1 - e, 2 * shift
            ends = tiles[e][:, half:]
            link(v.tensor_copy(route["ends"][:], ends))
            link(v.tensor_tensor(base[:], ends, nt_f[:], ALU.subtract))
            link(v.tensor_scalar(base[:], base[:], float(P), None, ALU.mult))
            run = count[1 - a][:, PADT:, :]
            link(v.tensor_tensor(run, count[a][:, PADT:, :], psB, ALU.subtract))
            link(v.tensor_tensor(run, run, psA, ALU.add))
            link(v.tensor_tensor(run, run, over_t(base[:]), ALU.add))
            link(v.tensor_tensor(run, run, onehot[:], ALU.mult))
            link(v.tensor_reduce(place[:], run, X, ALU.add))
            link(v.tensor_copy(route["place"][:], place[:]))
            link(v.tensor_scalar(ptile_i[:], route["place"][:], 7, None, ALU.logical_shift_right))
            link(v.tensor_copy(ptile[:], ptile_i[:]))
            link(v.scalar_tensor_tensor(prow[:], ptile[:], -float(P), place[:], ALU.mult, ALU.add))
            v.tensor_tensor(rows1[:], prow[:].unsqueeze(2).to_broadcast([P, NT, P]),
                            c["iota_r"][:].unsqueeze(1).to_broadcast([P, NT, P]), ALU.is_equal).then_inc(tables_ready, 1)
            link(v.tensor_tensor(slots1[:], ptile[:].unsqueeze(2).to_broadcast([P, NT, NCOL]),
                                 c["iota_s"][:].unsqueeze(1).to_broadcast([P, NT, NCOL]), ALU.is_equal))
            v.tensor_scalar(ids[:, :, 0:NCOL], slots1[:], c["iota_p"][:], None, ALU.mult).then_inc(tables_ready, 1)
            v.tensor_tensor(ids[:, :, NCOL:], slots1[:], c["iota_t"][:].unsqueeze(2).to_broadcast([P, NT, NCOL]),
                            ALU.mult).then_inc(tables_ready, 1)
            link(v.tensor_tensor(past[:], c["iota_s"][:].unsqueeze(2).to_broadcast([P, NCOL, NE - 1]),
                                 ends[:, 0:NE - 1].unsqueeze(1).to_broadcast([P, NCOL, NE - 1]), ALU.is_ge))
            link(v.tensor_reduce(sexp[:], past[:], X, ALU.add))
            link(v.tensor_copy(route["expert"][:], sexp[:]))
            link(v.tensor_scalar(route["buffer"][:], route["expert"][:], 1, None, ALU.bitwise_and))
            dve.wait_ge(gathered, 1)
            link(v.tensor_copy(slots1[:, 0, :], psI[:, 0:NCOL]))
            link(v.scalar_tensor_tensor(route["token"][:], psI[:, NCOL:], float(P), slots1[:, 0, :], ALU.mult, ALU.add))


def routing_tables(nc, ctx):
    m = Scope(nc, ctx, "table")
    return {"prob": m.sb("prob", [P, NT]), "place": m.sb("place", [P, NT], I32), "ends": m.sb("ends", [P, NE], I32),
            "expert": m.sb("expert", [P, NCOL], I32), "buffer": m.sb("buffer", [P, NCOL], I32),
            "token": m.sb("token", [P, NCOL], I32)}


NB = 512
FK = FF // P


class Weights:

    def __init__(self, nc, ctx, w1_dram, w2_dram):
        m = Scope(nc, ctx, "w")
        self.nc, self.w1_dram, self.w2_dram = nc, w1_dram, w2_dram
        self.raw1 = m.sb("raw1", [P, KD, 2 * FF])
        self.raw2 = m.sb("raw2", [P, FK, D])
        self.hi1 = m.sb("hi1", [P, 2, KD * 2 * FF], F32R)
        self.lo1 = m.sb("lo1", [P, 2, KD * 2 * FF], F32R)
        self.hi2 = m.sb("hi2", [P, 2, FK * D], F32R)
        self.lo2 = m.sb("lo2", [P, 2, FK * D], F32R)
        self.zero = m.sb("zero", [P, 1])
        self.loaded1, self.loaded2, self.zeroed = m.sem("loaded1"), m.sem("loaded2"), m.sem("zeroed")
        self.split, self.high = m.sem("split"), m.sem("high")

    def load(self, sp, e):
        wait(sp, self.split, 4 * e)
        sp.dma_start(self.raw1[:], self.w1_dram[e].rearrange("(k p) f -> p k f", p=P)).then_inc(self.loaded1, 16)
        sp.dma_start(self.raw2[:], self.w2_dram[e].rearrange("(k p) d -> p k d", p=P)).then_inc(self.loaded2, 16)

    def parts(self):
        return ((self.loaded1, self.raw1, self.hi1, self.lo1), (self.loaded2, self.raw2, self.hi2, self.lo2))

    def divide_high(self, act, e):
        for loaded, raw, hi, _ in self.parts():
            act.wait_ge(loaded, 16 * (e + 1))
            self.nc.scalar.activation(hi[:, e, :], raw[:].rearrange("p k f -> p (k f)"), ACT.Copy).then_inc(self.high, 1)

    def divide_low(self, pool, e):
        for n, (_, raw, hi, lo) in enumerate(self.parts()):
            pool.wait_ge(self.high, 2 * e + n + 1)
            self.nc.gpsimd.tensor_tensor(lo[:, e, :], raw[:].rearrange("p k f -> p (k f)"), hi[:, e, :].bitcast(F32),
                                         ALU.subtract).then_inc(self.split, 2)

    def divide(self, pool, e):
        g, n = self.nc.gpsimd, 4 * e
        for loaded, raw, hi, lo in self.parts():
            flat = raw[:].rearrange("p k f -> p (k f)")
            pool.wait_ge(loaded, 16 * (e + 1))
            g.tensor_tensor(hi[:, e % 2, :], flat, self.zero[:].to_broadcast([P, flat.shape[1]]), ALU.add).then_inc(self.split, 1)
            pool.wait_ge(self.split, n + 1)
            g.tensor_tensor(lo[:, e % 2, :], flat, hi[:, e % 2, :].bitcast(F32), ALU.subtract).then_inc(self.split, 1)
            n += 2


def experts(nc, c, w, route, x1_dram, ys_dram):
    ctx = ExitStack()
    m = Scope(nc, ctx, "moe")
    with ctx:
        xg = m.sb("xg", [P, NCOL, D])
        xs = m.sb("xs", [P, D])
        xh = m.sb("xh", [P, KD, P], F32R)
        xl = m.sb("xl", [P, KD, P], F32R)
        act_a = m.sb("act_a", [P, FF])
        hs = m.sb("hs", [P, FF])
        hh = m.sb("hh", [P, FK, P], F32R)
        hl = m.sb("hl", [P, FK, P], F32R)
        yo = [m.sb(f"yo{i}", [P, D]) for i in range(2)]
        psH = m.ps("psH", [P, 4, NB])
        psHT = m.ps("psHT", [P, FK, P])
        psX = m.ps("psX", [P, NB])
        psY = m.ps("psY", [P, NB])
        psXv = psX[:, 0:KD * P].rearrange("p (k t) -> p k t", k=KD)
        (xs_ready, x_turned, xh_ready, xl_ready, a_ready, g_ready, silu_ready, hs_ready, h_turned, hh_ready,
         hl_ready, y_raw, yo_ready) = (m.sem(s) for s in (
             "xs_ready", "x_turned", "xh_ready", "xl_ready", "a_ready", "g_ready", "silu_ready", "hs_ready",
             "h_turned", "hh_ready", "hl_ready", "y_raw", "yo_ready"))
        gathered = [m.sem(f"gathered{i}") for i in range(4)]
        stored = [m.sem(f"stored{i}") for i in range(2)]
        block = ctx.enter_context(nc.Block())

        def tiles(eng, step):
            for t in range(4):
                step(t, t % 4)
            with eng.Fori(1, SLOTS // 4) as i:
                for q in range(4):
                    step(i * 4 + q, q)
            for t in range(SLOTS // 4 * 4, SLOTS + 2):
                step(t, t % 4)

        def before(t, q, n):
            return (t - q) * (16 // n)

        ys_tiles = ys_dram.rearrange("(t p) d -> t p d", p=P)

        def live(t):
            return not isinstance(t, int) or 0 <= t < SLOTS

        @block.sync
        def _(sp):
            for q in range(4):
                sp.wait_ge(gathered[q], 32)
            for e in range(2, NE):
                w.load(sp, e)

        @block.gpsimd
        def _(pool):
            def gather(slot):
                q = slot % 4
                wait(pool, gathered[q], 16 * (slot // 4))
                nc.gpsimd.indirect_dma_start(xg[:, slot, :], None, x1_dram,
                                             bass.IndirectOffsetOnAxis(route["token"][:, slot:slot + 1], 0)).then_inc(gathered[q], 16)

            for slot in range(SLOTS):
                gather(slot)
            nc.gpsimd.memset(w.zero[:], 0.0).then_inc(w.zeroed, 1)
            pool.wait_ge(w.zeroed, 1)
            for e in range(2, NE):
                w_free = pool.value_load(route["ends"][0:1, e - 2:e - 1], min_val=1, max_val=SLOTS)
                pool.wait_ge(yo_ready, w_free)
                w.divide(pool, e)

        @block.tensor
        def _(pe):
            def buffer_of(t):
                return pe.value_load(route["buffer"][0:1, bass.ds(t, 1)], min_val=0, max_val=1)

            def step(s, q):
                t = s - 1
                if live(t):
                    e = pe.value_load(route["expert"][0:1, bass.ds(t, 1)], min_val=0, max_val=NE - 1)
                    b = buffer_of(t)
                    pe.wait_ge(xl_ready, t + 1)
                    pe.wait_ge(w.split, e * 4 + 4)
                    wait(pe, silu_ready, t)
                    for n in range(4):
                        if n == 2:
                            wait(pe, hs_ready, t)
                        first = True
                        for k in range(KD):
                            cols = slice(k * 2 * FF + n * NB, k * 2 * FF + (n + 1) * NB)
                            for xpart, wpart in ((xh, w.hi1), (xh, w.lo1), (xl, w.hi1)):
                                last = nc.tensor.matmul(psH[:, n, :], xpart[:, k, :],
                                                        wpart[:, bass.ds(b, 1), cols].rearrange("p a f -> p (a f)"),
                                                        start=first, stop=k == KD - 1 and xpart is xl)
                                first = False
                        if n == 1:
                            last.then_inc(a_ready, 1)
                    last.then_inc(g_ready, 1)
                t = s
                if live(t):
                    pe.wait_ge(xs_ready, t + 1)
                    wait(pe, xl_ready, t)
                    for k in range(KD):
                        last = nc.tensor.transpose(psXv[:, k, :], xs[:, k * P:(k + 1) * P], c["ident"][:])
                    last.then_inc(x_turned, 1)
                t = s - 2
                if live(t):
                    b = buffer_of(t)
                    pe.wait_ge(hl_ready, t + 1)
                    wait(pe, yo_ready, t)
                    first = True
                    for k in range(FK):
                        for hpart, wpart in ((hh, w.hi2), (hh, w.lo2), (hl, w.hi2)):
                            last = nc.tensor.matmul(psY[:, 0:D], hpart[:, k, :],
                                                    wpart[:, bass.ds(b, 1), k * D:(k + 1) * D].rearrange("p a f -> p (a f)"),
                                                    start=first, stop=k == FK - 1 and hpart is hl)
                            first = False
                    last.then_inc(y_raw, 1)
                t = s - 1
                if live(t):
                    pe.wait_ge(hs_ready, t + 1)
                    wait(pe, hl_ready, t)
                    for k in range(FK):
                        last = nc.tensor.transpose(psHT[:, k, :], hs[:, k * P:(k + 1) * P], c["ident"][:])
                    last.then_inc(h_turned, 1)

            tiles(pe, step)

        @block.scalar
        def _(act):
            def step(s, q):
                t = s - 3
                if live(t):
                    act.wait_ge(yo_ready, t + 1)
                    act.dma_start(ys_tiles[bass.ds(t, 1), :, :].rearrange("a p d -> (a p) d"), yo[1 - q % 2][:]).then_inc(stored[1 - q % 2], 16)
                t = s - 1
                if live(t):
                    act.wait_ge(a_ready, t + 1)
                    wait(act, hs_ready, t)
                    nc.scalar.activation(act_a[:], psH[:, 0:2, :].rearrange("p a b -> p (a b)"), ACT.Silu).then_inc(silu_ready, 1)
                t = s
                if live(t):
                    act.wait_ge(x_turned, t + 1)
                    wait(act, g_ready, t)
                    nc.scalar.activation(xh[:], psXv, ACT.Copy).then_inc(xh_ready, 1)
                t = s - 2
                if live(t):
                    act.wait_ge(y_raw, t + 1)
                    wait(act, stored[q % 2], before(t, q % 2, 2))
                    nc.scalar.activation(yo[q % 2][:], psY[:, 0:D], ACT.Copy).then_inc(yo_ready, 1)
                t = s - 1
                if live(t):
                    act.wait_ge(h_turned, t + 1)
                    wait(act, y_raw, t)
                    nc.scalar.activation(hh[:], psHT[:], ACT.Copy).then_inc(hh_ready, 1)

            tiles(act, step)
            act.wait_ge(yo_ready, SLOTS)
            act.dma_start(ys_tiles[SLOTS - 1], yo[(SLOTS - 1) % 2][:]).then_inc(stored[(SLOTS - 1) % 2], 16)
            act.wait_ge(stored[0], before(SLOTS + 1, 0, 2))
            act.wait_ge(stored[1], before(SLOTS, 1, 2))

        @block.vector
        def _(dve):
            v = nc.vector

            def step(s, q):
                t = s
                if live(t):
                    dve.wait_ge(gathered[q], before(t, q, 4) + 16)
                    wait(dve, x_turned, t)
                    v.tensor_copy(xs[:], xg[:, bass.ds(t, 1), :].rearrange("p a d -> p (a d)")).then_inc(xs_ready, 1)
                t = s - 1
                if live(t):
                    dve.wait_ge(silu_ready, t + 1)
                    dve.wait_ge(g_ready, t + 1)
                    wait(dve, h_turned, t)
                    v.tensor_tensor(hs[:], psH[:, 2:4, :].rearrange("p a b -> p (a b)"), act_a[:], ALU.mult).then_inc(hs_ready, 1)
                t = s
                if live(t):
                    dve.wait_ge(xh_ready, t + 1)
                    v.tensor_tensor(xl[:], psXv, xh[:].bitcast(F32), ALU.subtract).then_inc(xl_ready, 1)
                t = s - 1
                if live(t):
                    dve.wait_ge(hh_ready, t + 1)
                    v.tensor_tensor(hl[:], psHT[:], hh[:].bitcast(F32), ALU.subtract).then_inc(hl_ready, 1)

            tiles(dve, step)


EPS = 1e-6
N, PS = 64, 32
NP = N * PS
BLK = 256
NBLK = NP // BLK
NPB = BLK // PS
MC = TB
CH = NP // P
MB = 4


def linear_attention(nc, c, route, x1_dram, ys_dram, w_dram, phi_dram, x, ph, pl):
    LAG = 2
    KB = 4
    ctx = ExitStack()
    m = Scope(nc, ctx, "lin")
    with ctx:
        phi = m.sb("phi", [P, KD, NP])
        yg = m.sb("yg", [P, NT, D])
        zero = m.sb("zero", [P, 1])
        xb = m.sb("xb", [P, TB, D])
        xh = m.sb("xh", [P, KD, TB, P], F32R)
        xl = m.sb("xl", [P, KD, TB, P], F32R)
        w_raw = m.sb("w_raw", [P, KD, 3 * D])
        wh = m.sb("wh", [P, KD, 3 * D], F32R)
        wl = m.sb("wl", [P, KD, 3 * D], F32R)
        qT = m.sb("qT", [P, KD, TB * P])
        qe = [m.sb(f"qe{i}", [P, NB]) for i in range(3)]
        qr = [m.sb(f"qr{i}", [P, NB]) for i in range(3)]
        ke = [m.sb(f"ke{i}", [P, D]) for i in range(KB)]
        kr = [m.sb(f"kr{i}", [P, D]) for i in range(KB)]
        kk = [m.sb(f"kk{i}", [P, D]) for i in range(KB)]
        v1 = [m.sb(f"v1{i}", [P, D + 1]) for i in range(KB)]
        kv = m.sb("kv", [P, KD, D + 1])
        z = [m.sb(f"z{i}", [P, 2]) for i in range(2)]
        xo = m.sb("xo", [P, TB, D])
        stats = [m.sb(f"stats{i}", [P, TB, 6]) for i in range(2)]
        var, tmp = m.sb("var", [P, TB]), m.sb("tmp", [P, TB])
        mean, rstd = ([m.sb(f"{s}{i}", [P, TB]) for i in range(2)] for s in ("mean", "rstd"))
        magic = m.sb("magic", [P, TB], I32)
        psW = [m.ps(f"psW{i}", [P, NB]) for i in range(2)]
        psK = [m.ps(f"psK{i}", [P, 2 * D]) for i in range(2)]
        psC = [m.ps(f"psC{i}", [P, NB]) for i in range(KD)]
        psO = [m.ps(f"psO{i}", [P, NB]) for i in range(2)]
        names = ("w_loaded", "w_split", "summed", "turned", "xh_ready", "xl_ready", "q_raw", "q_read", "q_ready",
                 "k_raw", "kv_read", "k_ready", "added", "kv_ready", "o_raw", "z_ready", "o_ready", "ones_set",
                 "stat_in", "stat_out", "normed", "finished", "chain")
        (w_loaded, w_split, summed, turned, xh_ready, xl_ready, q_raw, q_read, q_ready,
         k_raw, kv_read, k_ready, added, kv_ready, o_raw, z_ready, o_ready, ones_set,
         stat_in, stat_out, normed, finished, chain) = (m.sem(s) for s in names)
        phi_loaded, phi_split = m.sem("phi_loaded"), m.sem("phi_split")
        x_loaded = [m.sem(f"x_loaded{i}") for i in range(B)]
        gathered = [m.sem(f"gathered{i}") for i in range(TB + B - 1)]
        block = ctx.enter_context(nc.Block())
        NQ = KD * 2

        def turned_view(t):
            bank = (psW + psO)[t % 4] if t < TB else psW[t % 2]
            return bank[:, 0:KD * P].rearrange("p (k t) -> p k t", k=KD)

        @block.sync
        def _(sp):
            rows = x1_dram.rearrange("(t p) d -> p t d", p=P)
            for b in range(B):
                if b == 2:
                    sp.dma_start(phi[:], phi_dram.rearrange("(k p) n s -> p k (n s)", p=P)).then_inc(phi_loaded, 16)
                if b == 1:
                    sp.wait_ge(gathered[TB - 1], 16)
                sp.dma_start(x[:, b * TB:(b + 1) * TB, :], rows[:, b * TB:(b + 1) * TB, :]).then_inc(x_loaded[b], 16)
                if b == 0:
                    sp.dma_start(w_raw[:], w_dram.rearrange("(k p) f -> p k f", p=P)).then_inc(w_loaded, 16)

        def finish(eng, s, j):
            eng.tensor_scalar(x[:, s * TB + j, :], xo[:, j, :], mean[1][:, j:j + 1], rstd[1][:, j:j + 1],
                              ALU.subtract, ALU.mult).then_inc(finished, 1)

        @block.gpsimd
        def _(pool):
            for t in range(NT):
                nc.gpsimd.indirect_dma_start(yg[:, t, :], None, ys_dram,
                                             bass.IndirectOffsetOnAxis(route["place"][:, t:t + 1], 0)).then_inc(gathered[t if t < TB else TB - 1 + t // TB], 16)
            g_ = nc.gpsimd
            pool.wait_ge(phi_loaded, 16)
            g_.memset(zero[:], 0.0).then_inc(phi_split, 1)
            pool.wait_ge(phi_split, 1)
            n = KD * NP
            flat, hi, lo = (a[:].rearrange("p k n -> p (k n)") for a in (phi, ph, pl))
            g_.tensor_tensor(hi, flat, zero[:].to_broadcast([P, n]), ALU.add).then_inc(phi_split, 1)
            pool.wait_ge(phi_split, 2)
            g_.tensor_tensor(lo, flat, hi.bitcast(F32), ALU.subtract)
            for s in range(B - 1):
                pool.wait_ge(chain, (2 * s + 3) * NORM_LINKS)
                for j in range(TB):
                    finish(g_, s, j)

        @block.tensor
        def _(pe):
            def turn(s, j):
                t = s * TB + j
                wait(pe, normed, t + 1)
                wait(pe, q_read, 2 * s * NQ)
                wait(pe, xl_ready, t - 3 if t < TB else t - 1)
                for k in range(KD):
                    last = nc.tensor.transpose(turned_view(t)[:, k, :], x[:, t, k * P:(k + 1) * P], c["ident"][:])
                last.then_inc(turned, 1)

            def project(s):
                wait(pe, xl_ready, (s + 1) * TB)
                wait(pe, kv_ready, s)

                def query(n):
                    chunk, half = divmod(n, 2)
                    wait(pe, q_read, 2 * (s * NQ + n - 1))
                    for k in range(KD):
                        for a, (xpart, wpart) in enumerate(((xh, wh), (xh, wl), (xl, wh))):
                            last = nc.tensor.matmul(psW[n % 2][:], wpart[:, k, chunk * P:(chunk + 1) * P],
                                                    xpart[:, k, half * (TB // 2):(half + 1) * (TB // 2), :].rearrange("p j t -> p (j t)"),
                                                    start=k == 0 and a == 0, stop=k == KD - 1 and a == 2)
                    last.then_inc(q_raw, 1)

                def add_up(j):
                    t = s * TB + j
                    wait(pe, k_ready, t + 1)
                    wait(pe, kv_read, 3 * (t + 1))
                    for chunk in range(KD):
                        last = nc.tensor.matmul(psC[chunk][:, 0:D + 1], kk[t % KB][:, chunk * P:(chunk + 1) * P], v1[t % KB][:],
                                                start=j == 0, stop=j == TB - 1)
                    last.then_inc(added, 1)

                for j in range(TB):
                    t = s * TB + j
                    wait(pe, kv_read, 3 * (t - 1))
                    for k in range(KD):
                        for a, (xpart, wpart) in enumerate(((xh, wh), (xh, wl), (xl, wh))):
                            last = nc.tensor.matmul(psK[j % 2][:], xpart[:, k, j, :], wpart[:, k, D:3 * D],
                                                    start=k == 0 and a == 0, stop=k == KD - 1 and a == 2)
                    last.then_inc(k_raw, 1)
                    if j % 2 == 1:
                        query(j // 2)
                    if j >= LAG:
                        add_up(j - LAG)
                for j in range(TB - LAG, TB):
                    add_up(j)

            def attend(s, j):
                t = s * TB + j
                wait(pe, kv_ready, s + 1)
                wait(pe, q_ready, s * NQ + NQ)
                wait(pe, o_ready, t - 1)
                for chunk in range(KD):
                    last = nc.tensor.matmul(psO[t % 2][:, 0:D + 1], qT[:, chunk, j * P:(j + 1) * P], kv[:, chunk, :],
                                            start=chunk == 0, stop=chunk == KD - 1)
                last.then_inc(o_raw, 1)

            for s in range(B + 1):
                for j in range(TB):
                    if s > 0:
                        attend(s - 1, j)
                    if s < B:
                        turn(s, j)
                if s == 0:
                    pe.wait_ge(w_split, 2)
                if s < B:
                    project(s)

        @block.scalar
        def _(act):
            a_ = nc.scalar
            act.wait_ge(ones_set, KB)
            for s in range(B):
                for j in range(TB):
                    t = s * TB + j
                    wait(act, turned, t + 1)
                    wait(act, k_raw, s * TB)
                    a_.activation(xh[:, :, j, :], turned_view(t), ACT.Copy).then_inc(xh_ready, 1)
                for j in range(TB):
                    t = s * TB + j
                    wait(act, k_raw, t + 1)
                    wait(act, k_ready, t - KB + 1)
                    a_.activation(ke[t % KB][:], psK[j % 2][:, 0:D], ACT.Exp).then_inc(kv_read, 1)
                    a_.activation(kr[t % KB][:], psK[j % 2][:, 0:D], ACT.Relu).then_inc(kv_read, 1)
                    wait(act, added, t - KB + 1)
                    a_.activation(v1[t % KB][:, 0:D], psK[j % 2][:, D:2 * D], ACT.Copy).then_inc(kv_read, 1)
                    if j % 2 == 1:
                        n = j // 2
                        g = s * NQ + n
                        wait(act, q_raw, g + 1)
                        wait(act, q_ready, g - 2)
                        a_.activation(qe[g % 3][:], psW[n % 2][:], ACT.Exp).then_inc(q_read, 1)
                        a_.activation(qr[g % 3][:], psW[n % 2][:], ACT.Relu).then_inc(q_read, 1)
                wait(act, added, s * TB + TB)
                wait(act, o_raw, s * TB)
                for chunk in range(KD):
                    last = a_.activation(kv[:, chunk, :], psC[chunk][:, 0:D + 1], ACT.Copy)
                last.then_inc(kv_ready, 1)

        @block.vector
        def _(dve):
            v = nc.vector
            n = [0]

            def link(*steps):
                n[0] += len(steps)
                for ins in steps:
                    ins.then_inc(chain, 1)
                dve.wait_ge(chain, n[0])

            def root(which):
                norm_steps(v, link, stats[which][:], mean[which][:], rstd[which][:], var[:], tmp[:], magic[:])

            def residual(s, j):
                t = s * TB + j
                dve.wait_ge(gathered[t if s == 0 else TB - 1 + s], 16 if s == 0 else 16 * TB)
                dve.wait_ge(x_loaded[s], 16)
                v.scalar_tensor_tensor(xb[:, j, :], yg[:, t, :], route["prob"][:, t:t + 1], x[:, t, :], ALU.mult, ALU.add).then_inc(summed, 1)
                if j > 0:
                    moments(t - 1, j - 1)

            def moments(t, j):
                wait(dve, summed, t + 1)
                v.bn_stats(stats[0][:, j, :], xb[:, j, :]).then_inc(stat_in, 1)

            def root_in(s):
                moments(s * TB + TB - 1, TB - 1)
                wait(dve, stat_in, s * TB + TB)
                root(0)

            def norm_in(s, j):
                v.tensor_scalar(x[:, s * TB + j, :], xb[:, j, :], mean[0][:, j:j + 1], rstd[0][:, j:j + 1],
                                ALU.subtract, ALU.mult).then_inc(normed, 1)

            def rest(s, j):
                t = s * TB + j
                wait(dve, xh_ready, t + 1)
                v.tensor_tensor(xl[:, :, j, :], turned_view(t), xh[:, :, j, :].bitcast(F32), ALU.subtract).then_inc(xl_ready, 1)

            def query(s, i):
                wait(dve, o_raw, s * TB)
                chunk, half = divmod(i, 2)
                g = s * NQ + i
                wait(dve, q_read, 2 * (g + 1))
                v.scalar_tensor_tensor(qT[:, chunk, half * NB:(half + 1) * NB], qe[g % 3][:], 1.0, qr[g % 3][:],
                                       ALU.min, ALU.add).then_inc(q_ready, 1)

            def keys(s, j):
                t = s * TB + j
                wait(dve, added, t - KB + 1)
                wait(dve, kv_read, 3 * t + 2)
                v.scalar_tensor_tensor(kk[t % KB][:], ke[t % KB][:], 1.0, kr[t % KB][:], ALU.min, ALU.add).then_inc(k_ready, 1)

            def add_eps(s, j):
                t = s * TB + j
                wait(dve, o_raw, t + 1)
                v.tensor_scalar(z[t % 2][:, 0:1], psO[t % 2][:, D:D + 1], EPS, None, ALU.add).then_inc(z_ready, 1)

            def invert(s, j):
                t = s * TB + j
                wait(dve, z_ready, 2 * t + 1)
                v.reciprocal(z[t % 2][:, 1:2], z[t % 2][:, 0:1]).then_inc(z_ready, 1)

            def output(s, j):
                t = s * TB + j
                wait(dve, z_ready, 2 * t + 2)
                if j == 0:
                    wait(dve, finished, s * TB)
                v.scalar_tensor_tensor(xo[:, j, :], psO[t % 2][:, 0:D], z[t % 2][:, 1:2], x[:, t, :], ALU.mult, ALU.add).then_inc(o_ready, 1)

            def output_moments(s, j):
                wait(dve, o_ready, s * TB + j + 1)
                v.bn_stats(stats[1][:, j, :], xo[:, j, :]).then_inc(stat_out, 1)

            def root_out(s):
                wait(dve, stat_out, s * TB + TB)
                wait(dve, finished, s * TB)
                root(1)

            for i in range(KB):
                v.memset(v1[i][:, D:D + 1], 1.0).then_inc(ones_set, 1)
            for s in range(B + 1):
                for j in range(TB):
                    if s > 1 and j == 1:
                        root_out(s - 2)
                    if s > 0:
                        keys(s - 1, j)
                        if j % 2 == 1:
                            query(s - 1, j // 2)
                    if s < B and j < TB // 2:
                        residual(s, 2 * j)
                        residual(s, 2 * j + 1)
                    if s == 0 and j == TB // 2 - 1:
                        dve.wait_ge(w_loaded, 16)
                        v.tensor_copy(wh[:], w_raw[:]).then_inc(w_split, 1)
                        dve.wait_ge(w_split, 1)
                        v.tensor_tensor(wl[:], w_raw[:], wh[:].bitcast(F32), ALU.subtract).then_inc(w_split, 1)
                    if s < B and j == TB // 2:
                        root_in(s)
                        norm_in(s, 0)
                        norm_in(s, 1)
                    if s < B and j > TB // 2:
                        for a in range(2):
                            norm_in(s, 2 * (j - TB // 2) + a)
                for j in range(TB):
                    if s > 0:
                        add_eps(s - 1, j)
                    if s < B:
                        rest(s, j)
                    if s > 0:
                        invert(s - 1, j)
                        if j > 0:
                            output_moments(s - 1, j - 1)
                        output(s - 1, j)
                if s > 0:
                    output_moments(s - 1, TB - 1)
            root_out(B - 1)
            for j in range(TB):
                finish(v, B - 1, j)


def dispatch(nc, c, ph, pl, x, rowmax, w_dram, b_dram, l_dram, y_dram):
    LAG = 3
    ctx = ExitStack()
    m = Scope(nc, ctx, "disp")
    with ctx:
        xh = m.sb("xh", [P, KD, NT * P], F32R)
        xl = m.sb("xl", [P, KD, NT * P], F32R)
        e = [m.sb(f"e{i}", [P, B, BLK]) for i in range(4)]
        raw = [m.sb(f"raw{i}", [P, B, BLK]) for i in range(4)]
        pm = m.sb("pm", [P, 2, BLK])
        s2 = m.sb("s2", [P, 2, BLK])
        top = [m.sb(f"top{i}", [P, BLK]) for i in range(2)]
        rs = [m.sb(f"rs{i}", [P, BLK]) for i in range(2)]
        slots = m.sb("slots", [P, KD, NPB, B, PS])
        wt = m.sb("wt", [P, KD, NPB, D])
        bt = m.sb("bt", [P, NPB, D])
        yb = m.sb("yb", [P, NPB // 2, D])
        psL = [m.ps(f"psL{i}", [P, B, BLK]) for i in range(2)]
        psS = [m.ps(f"psS{i}", [P, B, BLK]) for i in range(KD)]
        names = ("w_loaded", "b_loaded", "logits", "copied", "pair_max", "top_ready", "less", "exp_ready", "pair_sum", "sum_ready",
                 "rsum_ready", "share_ready", "gone", "slots_ready", "y_raw", "y_ready", "stored")
        (w_loaded, b_loaded, logits, copied, pair_max, top_ready, less, exp_ready, pair_sum, sum_ready,
         rsum_ready, share_ready, gone, slots_ready, y_raw, y_ready, stored) = (m.sem(s) for s in names)
        turned, hi, lo = (m.sem(s) for s in ("turned", "hi", "lo"))
        kept = [m.sem(f"kept{i}") for i in range(4)]
        block = ctx.enter_context(nc.Block())
        HALF = NPB // 2
        EVAC = LAG - 1
        y_step = {4: 0, 5: 1}
        l_bank = (0, 1, 0, 1, 0, 0, 0, 1)
        Y_BANK = 1
        PIECES, AT_ONCE = NT // 2, 4

        def pieces(step):
            return range(step * AT_ONCE, min((step + 1) * AT_ONCE, PIECES))

        def piece_bank(g):
            return psS[g % 4 // 2][:, g % 2 * 2:g % 2 * 2 + 2, :].rearrange("p a (k t) -> p a k t", k=KD)

        def piece(part, g):
            b = g % 2 * 2
            return part[:].rearrange("p k (b j t) -> p b k j t", b=B, j=TB)[:, b:b + 2, :, g // 2, :]

        @block.sync
        def _(sp):
            def load(first):
                for kd in range(KD):
                    sp.dma_start(wt[:, kd], w_dram[bass.ds(first, NPB), kd * P:(kd + 1) * P, :].rearrange("n p e -> p n e")).then_inc(w_loaded, 16)
                sp.dma_start(bt[:], b_dram[bass.ds(first, NPB), :].partition_broadcast(P)).then_inc(b_loaded, 16)

            def store(k, first, h):
                wait(sp, y_ready, k * 2 + (h + 1))
                for b in range(B):
                    sp.dma_start(y_dram[b, bass.ds(first, HALF), :, :].rearrange("n s e -> s n e"),
                                 yb[b * PS:(b + 1) * PS, :, :]).then_inc(stored, 16)

            logits_of = l_dram.rearrange("(b j) p n -> j p b n", b=B)

            def keep(k, mc, first):
                wait(sp, copied, k * MC + (mc + 1))
                sp.dma_start(logits_of[mc, :, :, bass.ds(first, BLK)], raw[mc % 4][:]).then_inc(kept[mc % 4], 16)

            load(0)
            for mc in range(MC):
                keep(0, mc, 0)
            with sp.Fori(1, NBLK) as k:
                here, cols = sp.snap(k * NPB), sp.snap(k * BLK)
                last = [sp.snap((k - 1) * NPB + h * HALF) for h in range(2)]
                for mc in range(MC):
                    keep(k, mc, cols)
                    if mc - 1 in y_step:
                        store(k - 1, last[y_step[mc - 1]], y_step[mc - 1])
                load(here)
            for h in range(2):
                store(NBLK - 1, (NBLK - 1) * NPB + h * HALF, h)
            sp.wait_ge(stored, NBLK * 2 * 16 * B)
            for q in range(4):
                sp.wait_ge(kept[q], NBLK * (MC // 4) * 16)

        @block.tensor
        def _(pe):
            def turn(g):
                wait(pe, lo, g - 3)
                for a in range(2):
                    for kd in range(KD):
                        t = (g % 2 * 2 + a) * TB + g // 2
                        last = nc.tensor.transpose(piece_bank(g)[:, a, kd, :], x[:, t, kd * P:(kd + 1) * P], c["ident"][:])
                last.then_inc(turned, 1)

            def score(k, mc):
                g = k * MC + mc
                if isinstance(k, int) and k == 0:
                    wait(pe, lo, 2 * mc + 2)
                wait(pe, copied, g - 1 if mc < 5 else g if mc < 7 else g - 3)
                if mc == 7:
                    wait(pe, y_ready, k * 2)
                p = l_bank[mc]
                for b in range(B):
                    t = b * TB + mc
                    for kd in range(KD):
                        for a, (xp, pp) in enumerate(((xh, ph), (xh, pl), (xl, ph))):
                            last = nc.tensor.matmul(psL[p][:, b, :], xp[:, kd, t * P:(t + 1) * P],
                                                    pp[:, kd, bass.ds(k * BLK, BLK)],
                                                    start=b % 2 == 0 and kd == 0 and a == 0, stop=kd == KD - 1 and a == 2,
                                                    skip_group_check=True)
                last.then_inc(logits, 1)

            def contract(k, mc):
                g = k * MC + mc
                wait(pe, share_ready, g + 1)
                if isinstance(k, int) and k == 0 and mc == 0:
                    wait(pe, lo, PIECES)
                if mc == 0:
                    wait(pe, slots_ready, k * KD)
                for kd in range(KD):
                    for b in range(B):
                        last = nc.tensor.matmul(psS[kd][:, b, :], x[:, b * TB + mc, kd * P:(kd + 1) * P], e[mc % 4][:, b, :],
                                                start=mc == 0 and b % 2 == 0, stop=mc == MC - 1, skip_group_check=True)
                last.then_inc(gone, 1)

            def expert(k, h, copies):
                wait(pe, w_loaded, k * (16 * KD) + 16 * KD)
                wait(pe, slots_ready, k * KD + KD)
                wait(pe, copied, copies)
                if h == 1:
                    wait(pe, y_ready, k * 2 + 1)
                for i in range(HALF):
                    for kd in range(KD):
                        last = nc.tensor.matmul(psL[Y_BANK][:, i, :], slots[:, kd, h * HALF + i, :, :].rearrange("p b s -> p (b s)"),
                                                wt[:, kd, h * HALF + i, :], start=kd == 0 and i % 2 == 0, stop=kd == KD - 1,
                                                skip_group_check=True)
                last.then_inc(y_raw, 1)

            def step(k, mc, fresh=False, draining=False):
                if fresh:
                    for g in pieces(mc + 1):
                        turn(g)
                if not draining:
                    score(k, mc)
                if mc >= LAG and not draining:
                    contract(k, mc - LAG)
                if mc < LAG and not fresh:
                    contract(k - 1, mc - LAG + MC)
                if mc in y_step and not fresh:
                    expert(k - 1, y_step[mc], NBLK * MC if draining else k * MC + 4)

            for g in pieces(0):
                turn(g)
            for mc in range(MC):
                step(0, mc, fresh=True)
            with pe.Fori(1, NBLK) as k:
                for mc in range(MC):
                    step(k, mc)
            for mc in range(MC):
                step(NBLK, mc, draining=True)

        @block.scalar
        def _(act):
            def high(n):
                wait(act, turned, n + 1)
                nc.scalar.activation(piece(xh, n), piece_bank(n), ACT.Copy).then_inc(hi, 1)

            for n in pieces(0):
                high(n)

            def step(k, mc, fresh=False, draining=False):
                if fresh:
                    for n in pieces(mc + 1):
                        high(n)
                g = k * MC + mc
                if not draining:
                    wait(act, less, g + 1)
                    nc.scalar.activation(e[mc % 4][:], e[mc % 4][:], ACT.Exp).then_inc(exp_ready, 1)
                if mc == EVAC and not fresh:
                    wait(act, gone, k * MC)
                    for kd in range(KD):
                        nc.scalar.activation(slots[:, kd].rearrange("p n b s -> p b n s"),
                                             psS[kd][:].rearrange("p b (n s) -> p b n s", s=PS), ACT.Copy).then_inc(slots_ready, 1)

            for mc in range(MC):
                step(0, mc, fresh=True)
            with act.Fori(1, NBLK) as k:
                for mc in range(MC):
                    step(k, mc)
            step(NBLK, EVAC, draining=True)

        @block.gpsimd
        def _(pool):
            def share(g, q):
                wait(pool, rsum_ready, g + 1)
                nc.gpsimd.tensor_tensor(e[q % 4][:], e[q % 4][:], rs[q % 2][:].unsqueeze(1).to_broadcast([P, B, BLK]),
                                        ALU.mult).then_inc(share_ready, 1)

            def step(k, mc, fresh=False):
                g = k * MC + mc
                wait(pool, top_ready, g + 1)
                wait(pool, gone, g - 3)
                nc.gpsimd.tensor_tensor(e[mc % 4][:], raw[mc % 4][:], top[mc % 2][:].unsqueeze(1).to_broadcast([P, B, BLK]),
                                        ALU.subtract).then_inc(less, 1)
                if mc > 0 or not fresh:
                    share(g - 1, mc + 7)

            for mc in range(MC):
                step(0, mc, fresh=True)
            with pool.Fori(1, NBLK) as k:
                for mc in range(MC):
                    step(k, mc)
            share(NBLK * MC - 1, MC - 1)

        @block.vector
        def _(dve):
            v = nc.vector

            def low(n):
                wait(dve, hi, n + 1)
                v.tensor_tensor(piece(xl, n), piece_bank(n), piece(xh, n).bitcast(F32), ALU.subtract).then_inc(lo, 1)

            for n in pieces(0):
                low(n)

            def sums(g, q):
                wait(dve, exp_ready, g + 1)
                wait(dve, sum_ready, g)
                v.tensor_tensor(s2[:], e[q % 4][:, 0:2, :], e[q % 4][:, 2:4, :], ALU.add).then_inc(pair_sum, 1)
                wait(dve, pair_sum, g + 1)
                wait(dve, share_ready, g - 1)
                v.tensor_tensor(rs[q % 2][:], s2[:, 0, :], s2[:, 1, :], ALU.add).then_inc(sum_ready, 1)
                wait(dve, sum_ready, g + 1)
                v.reciprocal(rs[q % 2][:], rs[q % 2][:]).then_inc(rsum_ready, 1)

            def copy_y(k, h):
                wait(dve, y_raw, k * 2 + (h + 1))
                wait(dve, b_loaded, k * 16 + 16)
                wait(dve, stored, k * (2 * 16 * B) + h * (16 * B))
                v.tensor_tensor(yb[:], psL[Y_BANK][:], bt[:, h * HALF:(h + 1) * HALF, :],
                                ALU.add).then_inc(y_ready, 1)

            def step(k, mc, fresh=False, draining=False):
                g = k * MC + mc
                if mc - 1 in y_step and not fresh:
                    copy_y(k - 1, y_step[mc - 1])
                if draining:
                    return
                wait(dve, logits, g + 1)
                wait(dve, less, g - 3)
                wait(dve, kept[mc % 4], k * (MC // 4 * 16) + mc // 4 * 16)
                for b in range(B):
                    last = v.tensor_scalar(raw[mc % 4][:, b, :], psL[l_bank[mc]][:, b, :], 1.0, None, ALU.mult, ALU.max,
                                           accum_out=rowmax[:, b * TB + mc, bass.ds(k, 1)])
                last.then_inc(copied, 1)
                wait(dve, copied, g + 1)
                wait(dve, top_ready, g)
                v.tensor_tensor(pm[:], raw[mc % 4][:, 0:2, :], raw[mc % 4][:, 2:4, :], ALU.max).then_inc(pair_max, 1)
                wait(dve, pair_max, g + 1)
                wait(dve, less, g - 1)
                v.tensor_tensor(top[mc % 2][:], pm[:, 0, :], pm[:, 1, :], ALU.max).then_inc(top_ready, 1)
                if fresh:
                    for n in pieces(mc + 1):
                        low(n)
                if mc > 0 or not fresh:
                    sums(g - 1, mc + 7)

            for mc in range(MC):
                step(0, mc, fresh=True)
            with dve.Fori(1, NBLK) as k:
                for mc in range(MC):
                    step(k, mc)
            sums(NBLK * MC - 1, MC - 1)
            for mc in range(MC):
                step(NBLK, mc, draining=True)


def combine(nc, c, x, rowmax, l_dram, y_dram, out_dram):
    LAG = 2
    QS = CH // 4
    STEPS = TB * QS
    LB = 4
    EB = 4
    ctx = ExitStack()
    m = Scope(nc, ctx, "comb")
    with ctx:
        negtop = m.sb("negtop", [P, NT])
        y_in = m.sb("y_in", [P, CH, D])
        zero = m.sb("zero", [P, 1])
        yh = m.sb("yh", [P, 2, CH * D], F32R)
        yl = m.sb("yl", [P, 2, CH * D], F32R)
        e = [m.sb(f"e{i}", [P, NP]) for i in range(LB)]
        den = m.sb("den", [P, TB])
        eh = [m.sb(f"eh{i}", [P, 4, P], F32R) for i in range(EB)]
        el = [m.sb(f"el{i}", [P, 4, P], F32R) for i in range(EB)]
        rden = m.sb("rden", [P, 2])
        xo = m.sb("xo", [P, TB, D])
        stats = m.sb("stats", [P, TB, 6])
        mean, var, rstd, tmp = (m.sb(s, [P, TB // 2]) for s in ("mean", "var", "rstd", "tmp"))
        magic = m.sb("magic", [P, TB // 2], I32)
        psT = [m.ps(f"psT{i}", [P, 4, P]) for i in range(EB)]
        psO = [m.ps(f"psO{i}", [P, 512]) for i in range(2)]
        names = ("chain", "zeroed", "top_ready", "y_loaded", "yh_ready", "y_split", "exp_ready", "turned", "hi_ready", "lo_ready", "gone",
                 "rden_ready", "summed", "stat", "normed", "stored")
        (chain, zeroed, top_ready, y_loaded, yh_ready, y_split, exp_ready, turned, hi_ready, lo_ready, gone,
         rden_ready, summed, stat, normed, stored) = (m.sem(s) for s in names)
        l_loaded = [m.sem(f"l_loaded{i}") for i in range(LB)]
        block = ctx.enter_context(nc.Block())
        FIRST_SPLIT = 2 * QS
        HT = TB // 2

        @block.sync
        def _(sp):
            dst = out_dram.rearrange("b (g p w) d -> p (b g) w d", p=P, w=2)

            def load_y(b):
                wait(sp, y_split, FIRST_SPLIT + (b - 1) * (2 * CH) if b > 0 else 0)
                sp.dma_start(y_in[:], y_dram[b].rearrange("n s e -> (n s) e").rearrange("(c p) e -> p c e", p=P)).then_inc(y_loaded, 16)

            def store(h):
                sp.wait_ge(normed, h * HT + HT)
                sp.dma_start(dst[:, h * HT // 2:(h + 1) * HT // 2, :, :],
                             x[:, h * HT:(h + 1) * HT, :].rearrange("p (g w) d -> p g w d", w=2)).then_inc(stored, 16)

            for t in range(NT):
                if t == 1:
                    load_y(0)
                b, j = divmod(t, TB)
                wait(sp, turned, (t - LB + 1) * QS)
                sp.dma_start(e[t % LB][:], l_dram[t]).then_inc(l_loaded[t % LB], 16)
                if j == 4 and b + 1 < B:
                    load_y(b + 1)
                if b > 0 and j in (0, 4):
                    store((b - 1) * 2 + j // 4)
            for h in (2 * B - 2, 2 * B - 1):
                store(h)
            sp.wait_ge(stored, 2 * B * 16)

        @block.gpsimd
        def _(pool):
            g_ = nc.gpsimd
            g_.memset(zero[:], 0.0).then_inc(zeroed, 1)
            pool.wait_ge(zeroed, 1)
            for b in range(1, B):
                pool.wait_ge(y_loaded, b * 16 + 16)
                for ch in range(CH):
                    cols = slice(ch * D, (ch + 1) * D)
                    wait(pool, gone, (b - 1) * STEPS)
                    g_.tensor_tensor(yh[:, b % 2, cols], y_in[:, ch, :], zero[:].to_broadcast([P, D]), ALU.add).then_inc(y_split, 1)
                    pool.wait_ge(y_split, FIRST_SPLIT + ((b - 1) * CH + ch) * 2 + 1)
                    g_.tensor_tensor(yl[:, b % 2, cols], y_in[:, ch, :], yh[:, b % 2, cols].bitcast(F32), ALU.subtract).then_inc(y_split, 1)

        @block.tensor
        def _(pe):
            def turn(b, s):
                j, q = divmod(s, QS)
                if q == 0:
                    wait(pe, exp_ready, b * TB + (j + 1))
                wait(pe, lo_ready, b * STEPS + (s - EB + 1))
                for i in range(4):
                    ch = q * 4 + i
                    last = nc.tensor.transpose(psT[s % EB][:, i, :], e[j % LB][:, ch * P:(ch + 1) * P], c["ident"][:])
                last.then_inc(turned, 1)

            def contract(b, s, odd):
                j, q = divmod(s, QS)
                wait(pe, lo_ready, b * STEPS + (s + 1))
                if j == 0:
                    wait(pe, y_split, 2 * (q + 1) if isinstance(b, int) and b == 0 else
                         b * (2 * CH) + (FIRST_SPLIT - 2 * CH + (q + 1) * 8))
                if q == 0:
                    wait(pe, summed, b * TB + (j - 1))
                for i in range(4):
                    ch = q * 4 + i
                    for n, (ep, yp) in enumerate(((eh, yh), (eh, yl), (el, yh))):
                        last = nc.tensor.matmul(psO[j % 2][:, 0:D], ep[s % EB][:, i, :],
                                                yp[:, bass.ds(odd, 1), ch * D:(ch + 1) * D].rearrange("p a d -> p (a d)"),
                                                start=ch == 0 and n == 0, stop=ch == CH - 1 and n == 2)
                last.then_inc(gone, 1)

            def step(b, s, odd, odd_before, fresh=False, draining=False):
                if not draining:
                    turn(b, s)
                if s >= LAG and not draining:
                    contract(b, s - LAG, odd)
                if s < LAG and not fresh:
                    contract(b - 1, s - LAG + STEPS, odd_before)

            for s in range(STEPS):
                step(0, s, 0, None, fresh=True)
            with pe.Fori(1, B) as b:
                odd = pe.snap(b % 2)
                odd_before = pe.snap(1 - odd)
                for s in range(STEPS):
                    step(b, s, odd, odd_before)
            for s in range(LAG):
                step(B, s, None, (B - 1) % 2, draining=True)

        @block.scalar
        def _(act):
            def exponent(b, j):
                act.wait_ge(l_loaded[j % LB], b * (TB // LB * 16) + (j // LB + 1) * 16)
                wait(act, rden_ready, b * TB + (j - TB + 1))
                nc.scalar.activation(e[j % LB][:], e[j % LB][:], ACT.Exp, bias=negtop[:, bass.ds(b * TB + j, 1)],
                                     accum_out=den[:, j:j + 1]).then_inc(exp_ready, 1)

            def step(b, s, last=False):
                j, q = divmod(s, QS)
                wait(act, turned, b * STEPS + (s + 1))
                wait(act, gone, b * STEPS + (s - EB + 1))
                nc.scalar.activation(eh[s % EB][:], psT[s % EB][:], ACT.Copy).then_inc(hi_ready, 1)
                if q == 1 and not (last and j == TB - 1):
                    exponent(b if j + 1 < TB else b + 1, (j + 1) % TB)

            act.wait_ge(top_ready, 2)
            exponent(0, 0)
            act.wait_ge(y_loaded, 16)
            for q in range(QS):
                step(0, q)
                nc.scalar.activation(yh[:, 0, q * 4 * D:(q + 1) * 4 * D], y_in[:, q * 4:(q + 1) * 4, :].rearrange("p c d -> p (c d)"),
                                     ACT.Copy).then_inc(yh_ready, 1)
            for s in range(QS, STEPS):
                step(0, s)
            with act.Fori(1, B - 1) as b:
                for s in range(STEPS):
                    step(b, s)
            for s in range(STEPS):
                step(B - 1, s, last=True)

        @block.vector
        def _(dve):
            v = nc.vector
            v.tensor_reduce(negtop[:], rowmax[:], X, ALU.max).then_inc(top_ready, 1)
            dve.wait_ge(top_ready, 1)
            v.tensor_scalar(negtop[:], negtop[:], -1.0, None, ALU.mult).then_inc(top_ready, 1)

            def row(t):
                return x[:, bass.ds(t, 1), :].rearrange("p a d -> p (a d)")

            def collect(b, j):
                t = b * TB + j
                v.reciprocal(rden[:, j % 2:j % 2 + 1], den[:, j:j + 1]).then_inc(rden_ready, 1)
                wait(dve, rden_ready, t + 1)
                wait(dve, gone, b * STEPS + (j + 1) * QS)
                v.scalar_tensor_tensor(xo[:, j, :], psO[j % 2][:, 0:D], rden[:, j % 2:j % 2 + 1], row(t), ALU.mult, ALU.add).then_inc(summed, 1)
                wait(dve, summed, t + 1)
                v.bn_stats(stats[:, j, :], xo[:, j, :]).then_inc(stat, 1)

            def norm(b, h):
                t0 = b * TB + h * HT
                n = [0]
                wait(dve, stat, t0 + HT)

                def link(*steps):
                    n[0] += len(steps)
                    for ins in steps:
                        ins.then_inc(chain, 1)
                    dve.wait_ge(chain, b * (2 * NORM_LINKS) + (h * NORM_LINKS + n[0]))

                norm_steps(v, link, stats[:, h * HT:(h + 1) * HT, :], mean[:], rstd[:], var[:], tmp[:], magic[:])
                for a in range(HT):
                    v.tensor_scalar(row(t0 + a), xo[:, h * HT + a, :], mean[:, a:a + 1], rstd[:, a:a + 1], ALU.subtract, ALU.mult).then_inc(normed, 1)

            def step(b, s, fresh=False):
                wait(dve, hi_ready, b * STEPS + (s + 1))
                v.tensor_tensor(el[s % EB][:], psT[s % EB][:], eh[s % EB][:].bitcast(F32), ALU.subtract).then_inc(lo_ready, 1)
                j, q = divmod(s, QS)
                if q == LAG and (j > 0 or not fresh):
                    collect(*((b, j - 1) if j > 0 else (b - 1, TB - 1)))
                if q == LAG + 1 and j % HT == 0 and (j > 0 or not fresh):
                    norm(*((b, 0) if j > 0 else (b - 1, 1)))

            for q in range(QS):
                step(0, q, fresh=True)
                cols = slice(q * 4 * D, (q + 1) * 4 * D)
                dve.wait_ge(yh_ready, q + 1)
                v.tensor_tensor(yl[:, 0, cols], y_in[:, q * 4:(q + 1) * 4, :].rearrange("p c d -> p (c d)"),
                                yh[:, 0, cols].bitcast(F32), ALU.subtract).then_inc(y_split, 2)
            for s in range(QS, STEPS):
                step(0, s, fresh=True)
            with dve.Fori(1, B) as b:
                for s in range(STEPS):
                    step(b, s)
            collect(B - 1, TB - 1)
            norm(B - 1, 1)


def program(nc, x_in, router_w, router_b, w1, w2, w_attn, phi, w_slot, b_slot, out):
    x1_dram = nc.dram_tensor("x1_rows", [NT * P, D], F32, kind="Internal").ap()
    ys_dram = nc.dram_tensor("sorted_y", [SLOTS * P, D], F32, kind="Internal").ap()
    l_dram = nc.dram_tensor("logits", [NT, P, NP], F32, kind="Internal").ap()
    y_dram = nc.dram_tensor("slot_y", [B, N, PS, D], F32, kind="Internal").ap()
    with ExitStack() as ctx:
        c = {}
        route = routing_tables(nc, ctx)
        with ExitStack() as held:
            constants(nc, ctx, held, c)
            weights = Weights(nc, held, w1, w2)
            with ExitStack() as first:
                m = Scope(nc, first, "first")
                x1 = m.sb("x", [P, NT, D])
                stats = m.sb("stats", [P, NT, 6])
                dilated_attention(nc, c, x_in, x1, stats, weights)
                normalise_and_route(nc, c, x1, stats, router_w, router_b, x1_dram, route, weights)
            experts(nc, c, weights, route, x1_dram, ys_dram)
        x = Scope(nc, ctx, "last").sb("x", [P, NT, D])
        rowmax = Scope(nc, ctx, "last").sb("rowmax", [P, NT, NBLK])
        with ExitStack() as split:
            m = Scope(nc, split, "phi")
            ph, pl = (m.sb(s, [P, KD, NP], F32R) for s in ("hi", "lo"))
            linear_attention(nc, c, route, x1_dram, ys_dram, w_attn, phi, x, ph, pl)
            dispatch(nc, c, ph, pl, x, rowmax, w_slot, b_slot, l_dram, y_dram)
        combine(nc, c, x, rowmax, l_dram, y_dram, out)


def kernel(L0_attn_x, L0_ffn_router_w, L0_ffn_router_b, L0_ffn_w1, L0_ffn_w2, L1_attn_W, L1_ffn_phi, L1_ffn_W, L1_ffn_b):
    import numpy as np
    import concourse.bacc as bacc
    from concourse.bass_utils import run_bass_kernel_spmd

    nc = bacc.Bacc("TRN2", target_bir_lowering=False, num_devices=1)
    given = {"x": L0_attn_x, "router_w": L0_ffn_router_w, "router_b": L0_ffn_router_b, "w1": L0_ffn_w1, "w2": L0_ffn_w2,
             "w_attn": L1_attn_W, "phi": L1_ffn_phi, "w_slot": L1_ffn_W, "b_slot": L1_ffn_b}
    arrays, args = {}, []
    for name, value in given.items():
        a = np.ascontiguousarray(value)
        arrays[f"in_{name}"] = a
        args.append(nc.dram_tensor(f"in_{name}", a.shape, mybir.dt.from_np(a.dtype), kind="ExternalInput").ap())
    args.append(nc.dram_tensor("out", (B, S, D), F32, kind="ExternalOutput").ap())
    program(nc, *args)
    return run_bass_kernel_spmd(nc, [arrays], core_ids=[0]).results[0]["out"]
```
